# Optimizing a Trainium2 kernel written in Bass

```python
import numpy as np
import jax
import jax.numpy as jnp

def _softmax(x, axis=-1):
    return jax.nn.softmax(x, axis=axis)

def _gelu(x):
    return jax.nn.gelu(x, approximate=True)

def _silu(x):
    return jax.nn.silu(x)

def _sigmoid(x):
    return jax.nn.sigmoid(x)

def _layernorm(x, axis=-1, eps=1e-05):
    m = jnp.mean(x, axis=axis, keepdims=True)
    v = jnp.var(x, axis=axis, keepdims=True)
    return (x - m) / jnp.sqrt(v + eps)

def _scatter_add(tgt, idx, src, axis=0):
    return tgt.at[idx].add(src)

def _segment_sum(src, seg, n):
    return jax.ops.segment_sum(src, seg, n)
kernel_name = 'mk_xattn_seq_d2_seqx_r4_8b6be6'

def setup_inputs(seed: int=0):
    np.random.seed(seed)
    _w = jnp.asarray

    def _rec_inputs():
        import jax
        import jax.numpy as jnp
        _rk = jax.random.key(seed)
        x = 7.22e-05 + 1 * jax.random.normal(jax.random.fold_in(_rk, 1), (2, 512, 512), jnp.float32)
        _lenS = 512 - jax.random.randint(jax.random.fold_in(_rk, 7), (2,), 0, max(1, 512 // 4) + 1, jnp.int32)
        _lenS2 = 1024 - jax.random.randint(jax.random.fold_in(_rk, 8), (2,), 0, max(1, 1024 // 4) + 1, jnp.int32)
        _ctx_1024P = jax.random.normal(jax.random.fold_in(_rk, 11), (2, 16, 256), jnp.float32)
        _ctx_1024c = jax.random.dirichlet(jax.random.fold_in(_rk, 511), 0.3 * jnp.ones((16,), jnp.float32), (2, 1024))
        _ctx_1024t = jnp.einsum('bsk,bkd->bsd', _ctx_1024c, _ctx_1024P)
        _ctx_1024t = _ctx_1024t * jax.lax.rsqrt(jnp.mean(jnp.square(_ctx_1024t)) + 1e-12) * 0.953939
        ctx_1024 = -0.000514642 + 1.00011 * (_ctx_1024t + 0.3 * jax.random.normal(jax.random.fold_in(_rk, 611), (2, 1024, 256), jnp.float32))
        pos_1xS = jnp.broadcast_to(jnp.arange(512, dtype=jnp.int32), (1, 512))
        _validS = jnp.arange(512)[None, :] < _lenS[:, None]
        _validS2 = jnp.arange(1024)[None, :] < _lenS2[:, None]
        _causal = jnp.tril(jnp.ones((512, 512), dtype=bool))
        mask_BxS_ik0 = jnp.where(jnp.broadcast_to(_validS[:, :], (2, 512)), 0, 1).astype(jnp.int32)
        return (x, ctx_1024, pos_1xS, mask_BxS_ik0)
    x, ctx_1024, pos_1xS, mask_BxS_ik0 = _rec_inputs()

    def _L0_xattn_setup():
        import jax, jax.numpy as jnp
        import numpy as np
        H = 512
        NH = 16
        HD = H // NH
        CH = 256
        CC = 256
        CHD = CC // NH
        I = 1376
        B = 2
        L = 512
        LE = 256
        EPS = 1e-06

        def rms_norm(x, w):
            xf = x.astype(jnp.float32)
            var = jnp.mean(xf * xf, axis=-1, keepdims=True)
            return (w * (xf * jax.lax.rsqrt(var + EPS))).astype(x.dtype)

        def expert_mask(tt):
            vm = jnp.zeros(tt.shape, dtype=bool)
            vm = vm.at[:, :-1].set((tt[:, :-1] == 1) & (tt[:, 1:] == 1))
            return vm

        def rotate_half(x):
            d = x.shape[-1] // 2
            return jnp.concatenate([-x[..., d:], x[..., :d]], axis=-1)

        def apply_rotary(q, k, position_ids, seq_len):
            inv = 1.0 / 10000.0 ** (jnp.arange(0, HD, 2, dtype=jnp.float32) / HD)
            t = jnp.arange(seq_len, dtype=jnp.float32)
            freqs = jnp.outer(t, inv)
            emb = jnp.concatenate([freqs, freqs], axis=-1)
            cos = jnp.cos(emb)[position_ids][:, None].astype(q.dtype)
            sin = jnp.sin(emb)[position_ids][:, None].astype(q.dtype)
            return (q * cos + rotate_half(q) * sin, k * cos + rotate_half(k) * sin)

        def sdpa(q, k, v, causal):
            scale = 1.0 / np.sqrt(q.shape[-1])
            scores = jnp.einsum('bhqd,bhkd->bhqk', q * scale, k)
            if causal:
                mask = jnp.tril(jnp.ones((q.shape[-2], k.shape[-2]), dtype=bool))
                scores = jnp.where(mask, scores, jnp.finfo(jnp.float32).min)
            p = jax.nn.softmax(scores.astype(jnp.float32), axis=-1).astype(q.dtype)
            return jnp.einsum('bhqk,bhkd->bhqd', p, v)

        def heads(x, nh, hd):
            b, l, _ = x.shape
            return x.reshape(b, l, nh, hd).transpose(0, 2, 1, 3)
        key = jax.random.key(seed)
        ks = jax.random.split(key, 20)
        s = 0.02
        f32 = jnp.float32
        return {'hidden_states': jax.random.normal(ks[0], (B, L, H), f32), 'encoder_outputs': jax.random.normal(ks[1], (B, LE, CH), f32), 'token_type_ids': jax.random.randint(ks[2], (B, L), 0, 2, jnp.int32), 'position_ids': jnp.arange(L, dtype=jnp.int32)[None, :], 'ln_in_w': jnp.ones((H,), f32), 'ln_post_attn_w': jnp.ones((H,), f32), 'ln_post_cross_w': jnp.ones((H,), f32), 'v_qkv': jax.random.normal(ks[3], (H, 3 * H), f32) * s, 'l_qkv': jax.random.normal(ks[4], (H, 3 * H), f32) * s, 'v_dense': jax.random.normal(ks[5], (H, H), f32) * s, 'l_dense': jax.random.normal(ks[6], (H, H), f32) * s, 'cq_w': jax.random.normal(ks[7], (H, CC), f32) * s, 'ckv_w': jax.random.normal(ks[8], (CH, 2 * CC), f32) * s, 'cdense_w': jax.random.normal(ks[9], (CC, H), f32) * s, 'v_gate': jax.random.normal(ks[10], (H, I), f32) * s, 'v_up': jax.random.normal(ks[11], (H, I), f32) * s, 'v_down': jax.random.normal(ks[12], (I, H), f32) * s, 'l_gate': jax.random.normal(ks[13], (H, I), f32) * s, 'l_up': jax.random.normal(ks[14], (H, I), f32) * s, 'l_down': jax.random.normal(ks[15], (I, H), f32) * s}
    _L0_xattn_all = _L0_xattn_setup()
    _L0_xattn_in = {k: v for k, v in _L0_xattn_all.items() if k in ('ln_in_w', 'ln_post_attn_w', 'ln_post_cross_w', 'v_qkv', 'l_qkv', 'v_dense', 'l_dense', 'cq_w', 'ckv_w', 'cdense_w', 'v_gate', 'v_up', 'v_down', 'l_gate', 'l_up', 'l_down')}
    del _L0_xattn_all

    def _L1_xattn_setup():
        import jax, jax.numpy as jnp
        import numpy as np
        EPS = 1e-06

        def _rmsnorm(x, w):
            var = jnp.mean(jnp.square(x), axis=-1, keepdims=True)
            return x * jax.lax.rsqrt(var + EPS) * w
        key = jax.random.key(seed)
        ks = jax.random.split(key, 6)
        B, N, M = (4, 1024, 512)
        d_model, memory_dim = (512, 256)
        hidden_states = jax.random.normal(ks[0], (B, N, d_model), dtype=jnp.float32)
        memory = jax.random.normal(ks[1], (B, M, memory_dim), dtype=jnp.float32)
        W_mem = jax.random.normal(ks[2], (d_model, memory_dim), dtype=jnp.float32) / np.sqrt(memory_dim)
        W_gate = jax.random.normal(ks[3], (d_model, 2 * d_model), dtype=jnp.float32) / np.sqrt(2 * d_model)
        b_gate = jax.random.normal(ks[4], (d_model,), dtype=jnp.float32) * 0.01
        norm_w = jnp.ones((d_model,), dtype=jnp.float32)
        return {'hidden_states': hidden_states, 'memory': memory, 'W_mem': W_mem, 'W_gate': W_gate, 'b_gate': b_gate, 'norm_w': norm_w}
    _L1_xattn_all = _L1_xattn_setup()
    _L1_xattn_in = {k: v for k, v in _L1_xattn_all.items() if k in ('W_mem', 'W_gate', 'b_gate', 'norm_w')}
    del _L1_xattn_all
    return {'x': x, 'ctx_1024': ctx_1024, 'pos_1xS': pos_1xS, 'mask_BxS_ik0': mask_BxS_ik0, 'L0_xattn_ln_in_w': _L0_xattn_in['ln_in_w'], 'L0_xattn_ln_post_attn_w': _L0_xattn_in['ln_post_attn_w'], 'L0_xattn_ln_post_cross_w': _L0_xattn_in['ln_post_cross_w'], 'L0_xattn_v_qkv': _L0_xattn_in['v_qkv'], 'L0_xattn_l_qkv': _L0_xattn_in['l_qkv'], 'L0_xattn_v_dense': _L0_xattn_in['v_dense'], 'L0_xattn_l_dense': _L0_xattn_in['l_dense'], 'L0_xattn_cq_w': _L0_xattn_in['cq_w'], 'L0_xattn_ckv_w': _L0_xattn_in['ckv_w'], 'L0_xattn_cdense_w': _L0_xattn_in['cdense_w'], 'L0_xattn_v_gate': _L0_xattn_in['v_gate'], 'L0_xattn_v_up': _L0_xattn_in['v_up'], 'L0_xattn_v_down': _L0_xattn_in['v_down'], 'L0_xattn_l_gate': _L0_xattn_in['l_gate'], 'L0_xattn_l_up': _L0_xattn_in['l_up'], 'L0_xattn_l_down': _L0_xattn_in['l_down'], 'L1_xattn_W_mem': _L1_xattn_in['W_mem'], 'L1_xattn_W_gate': _L1_xattn_in['W_gate'], 'L1_xattn_b_gate': _L1_xattn_in['b_gate'], 'L1_xattn_norm_w': _L1_xattn_in['norm_w']}

def reference(x, ctx_1024, pos_1xS, mask_BxS_ik0, L0_xattn_ln_in_w, L0_xattn_ln_post_attn_w, L0_xattn_ln_post_cross_w, L0_xattn_v_qkv, L0_xattn_l_qkv, L0_xattn_v_dense, L0_xattn_l_dense, L0_xattn_cq_w, L0_xattn_ckv_w, L0_xattn_cdense_w, L0_xattn_v_gate, L0_xattn_v_up, L0_xattn_v_down, L0_xattn_l_gate, L0_xattn_l_up, L0_xattn_l_down, L1_xattn_W_mem, L1_xattn_W_gate, L1_xattn_b_gate, L1_xattn_norm_w):
    import jax
    import jax.numpy as jnp

    def _L0_xattn_ref(hidden_states, encoder_outputs, token_type_ids, position_ids, ln_in_w, ln_post_attn_w, ln_post_cross_w, v_qkv, l_qkv, v_dense, l_dense, cq_w, ckv_w, cdense_w, v_gate, v_up, v_down, l_gate, l_up, l_down):
        import jax, jax.numpy as jnp
        import numpy as np
        H = 512
        NH = 16
        HD = H // NH
        CH = 256
        CC = 256
        CHD = CC // NH
        I = 1376
        B = 2
        L = 512
        LE = 256
        EPS = 1e-06

        def rms_norm(x, w):
            xf = x.astype(jnp.float32)
            var = jnp.mean(xf * xf, axis=-1, keepdims=True)
            return (w * (xf * jax.lax.rsqrt(var + EPS))).astype(x.dtype)

        def expert_mask(tt):
            vm = jnp.zeros(tt.shape, dtype=bool)
            vm = vm.at[:, :-1].set((tt[:, :-1] == 1) & (tt[:, 1:] == 1))
            return vm

        def rotate_half(x):
            d = x.shape[-1] // 2
            return jnp.concatenate([-x[..., d:], x[..., :d]], axis=-1)

        def apply_rotary(q, k, position_ids, seq_len):
            inv = 1.0 / 10000.0 ** (jnp.arange(0, HD, 2, dtype=jnp.float32) / HD)
            t = jnp.arange(seq_len, dtype=jnp.float32)
            freqs = jnp.outer(t, inv)
            emb = jnp.concatenate([freqs, freqs], axis=-1)
            cos = jnp.cos(emb)[position_ids][:, None].astype(q.dtype)
            sin = jnp.sin(emb)[position_ids][:, None].astype(q.dtype)
            return (q * cos + rotate_half(q) * sin, k * cos + rotate_half(k) * sin)

        def sdpa(q, k, v, causal):
            scale = 1.0 / np.sqrt(q.shape[-1])
            scores = jnp.einsum('bhqd,bhkd->bhqk', q * scale, k)
            if causal:
                mask = jnp.tril(jnp.ones((q.shape[-2], k.shape[-2]), dtype=bool))
                scores = jnp.where(mask, scores, jnp.finfo(jnp.float32).min)
            p = jax.nn.softmax(scores.astype(jnp.float32), axis=-1).astype(q.dtype)
            return jnp.einsum('bhqk,bhkd->bhqd', p, v)

        def heads(x, nh, hd):
            b, l, _ = x.shape
            return x.reshape(b, l, nh, hd).transpose(0, 2, 1, 3)
        b, l, _ = hidden_states.shape
        vm = expert_mask(token_type_ids)[..., None]
        residual = hidden_states
        x = rms_norm(hidden_states, ln_in_w)
        mixed = jnp.where(vm, x @ v_qkv, x @ l_qkv)
        q, k, v = jnp.split(mixed, 3, axis=-1)
        q, k, v = (heads(q, NH, HD), heads(k, NH, HD), heads(v, NH, HD))
        q, k = apply_rotary(q, k, position_ids, l)
        ctx = sdpa(q, k, v, causal=True)
        ctx = ctx.transpose(0, 2, 1, 3).reshape(b, l, H)
        attn_out = jnp.where(vm, ctx @ v_dense, ctx @ l_dense)
        hidden_states = residual + attn_out
        ci = rms_norm(hidden_states, ln_post_cross_w)
        cq = heads(ci @ cq_w, NH, CHD)
        ckv = encoder_outputs @ ckv_w
        ck, cv = jnp.split(ckv, 2, axis=-1)
        ck, cv = (heads(ck, NH, CHD), heads(cv, NH, CHD))
        cctx = sdpa(cq, ck, cv, causal=False)
        cctx = cctx.transpose(0, 2, 1, 3).reshape(b, l, CC)
        hidden_states = hidden_states + cctx @ cdense_w
        mi = rms_norm(hidden_states, ln_post_attn_w)
        v_out = jax.nn.silu(mi @ v_gate) * (mi @ v_up) @ v_down
        l_out = jax.nn.silu(mi @ l_gate) * (mi @ l_up) @ l_down
        hidden_states = hidden_states + jnp.where(vm, v_out, l_out)
        return hidden_states

    def _L1_xattn_ref(hidden_states, memory, W_mem, W_gate, b_gate, norm_w):
        import jax, jax.numpy as jnp
        import numpy as np
        EPS = 1e-06

        def _rmsnorm(x, w):
            var = jnp.mean(jnp.square(x), axis=-1, keepdims=True)
            return x * jax.lax.rsqrt(var + EPS) * w
        D = hidden_states.shape[-1]
        memory_proj = jnp.einsum('bme,de->bmd', memory, W_mem)
        scores = jnp.einsum('bnd,bmd->bnm', hidden_states, memory_proj) / jnp.sqrt(jnp.float32(D))
        attn = jax.nn.softmax(scores, axis=-1)
        memory_context = jnp.einsum('bnm,bmd->bnd', attn, memory_proj)
        gate_input = jnp.concatenate([hidden_states, memory_context], axis=-1)
        gate = jax.nn.sigmoid(jnp.einsum('bnf,df->bnd', gate_input, W_gate) + b_gate)
        fused = hidden_states + gate * memory_context
        return _rmsnorm(fused, norm_w)
    x = _L0_xattn_ref(x, ctx_1024, mask_BxS_ik0, pos_1xS, L0_xattn_ln_in_w, L0_xattn_ln_post_attn_w, L0_xattn_ln_post_cross_w, L0_xattn_v_qkv, L0_xattn_l_qkv, L0_xattn_v_dense, L0_xattn_l_dense, L0_xattn_cq_w, L0_xattn_ckv_w, L0_xattn_cdense_w, L0_xattn_v_gate, L0_xattn_v_up, L0_xattn_v_down, L0_xattn_l_gate, L0_xattn_l_up, L0_xattn_l_down)
    x = _L1_xattn_ref(x, ctx_1024, L1_xattn_W_mem, L1_xattn_W_gate, L1_xattn_b_gate, L1_xattn_norm_w)
    return x

_drawn_inputs = setup_inputs


def setup_inputs(seed=0):
    import zlib

    import numpy as np

    out = dict(_drawn_inputs(seed))
    spreads = {'L0_xattn_ln_in_w': (1.0, 0.6),
     'L0_xattn_ln_post_attn_w': (1.0, 0.6),
     'L0_xattn_ln_post_cross_w': (1.0, 0.6),
     'L1_xattn_norm_w': (1.0, 0.2)}
    factors = {'L0_xattn_v_qkv': 8.0,
     'L0_xattn_v_dense': 8.0,
     'L0_xattn_cq_w': 8.0,
     'L1_xattn_b_gate': 63.037,
     'L0_xattn_v_gate': 8.0,
     'L0_xattn_v_up': 8.0,
     'L0_xattn_v_down': 8.0}
    for name, (base, spread) in spreads.items():
        noise = np.random.default_rng([zlib.crc32(name.encode()), seed]).standard_normal(out[name].shape)
        drawn = base * np.exp(spread * noise) if base else spread * noise
        out[name] = jnp.asarray(drawn.astype(out[name].dtype))
    for name, factor in factors.items():
        out[name] = (out[name] * factor).astype(out[name].dtype)
    return out
```

```python
import numpy as np
import concourse.bass as bass
from concourse import mybir
from contextlib import ExitStack

F32 = mybir.dt.float32
F32R = mybir.dt.float32r
BF16 = mybir.dt.bfloat16
I32 = mybir.dt.int32
U32 = mybir.dt.uint32
ALU = mybir.AluOpType
ACT = mybir.ActivationFunctionType
AX = mybir.AxisListType.X

P = 128
B, L, H = 2, 512, 512
T = B * L // P
TB = L // P
KH = H // P
NH = 16
HD = H // NH
C = 256
KC = C // P
CHD = C // NH
M = 1024
MT = M // P
F = 1376
EPS = 1e-6
NEG = -1e30
PAIRS = NH // 2
UNITS = B * PAIRS
SLOTS = 4
ONES = 96
FS = [384, 384, 384, 224]

NORMS = ["in", "cross", "mlp"]
TURNS = [(s, t) for s in NORMS for t in range(T)]
turn_no = {k: i for i, k in enumerate(TURNS)}
SMALL = 16 * (3 + B)


def rotary_table():
    inv = (1.0 / np.float32(10000.0) ** (np.arange(0, HD, 2, dtype=np.float32) / np.float32(HD))).astype(np.float32)
    a = np.outer(np.arange(L, dtype=np.float32), inv).astype(np.float32)
    return np.concatenate([np.cos(a), np.sin(a), -np.sin(a)], axis=1).astype(np.float32)


def raw32(ap):
    return ap.bitcast(F32)


def attention_steps(per_unit):
    lead = per_unit + 4
    n = UNITS * per_unit
    steps = []
    for x in range(lead + n + 7):
        todo = []
        if x < n:
            todo.append(("scores", x // per_unit, x % per_unit))
        u, r = divmod(x - 1, per_unit)
        if r == per_unit - 1 and 0 <= u < UNITS:
            todo.append(("max_parts", u, 0))
        u, r = divmod(x - 2, per_unit)
        if r == per_unit - 1 and 0 <= u < UNITS:
            todo.append(("max_rows", u, 0))
        y = x - lead
        if 0 <= y < n:
            todo.append(("probs", y // per_unit, y % per_unit))
        if 0 <= y - 1 < n:
            todo.append(("values", (y - 1) // per_unit, (y - 1) % per_unit))
        u, r = divmod(y - 3, per_unit)
        if y >= 3 and r == per_unit - 1 and u < UNITS:
            todo.append(("turn_back", u, 0))
        u, r = divmod(y - 5, per_unit)
        if y >= 5 and r == per_unit - 1 and u < UNITS and u % PAIRS == PAIRS - 1:
            todo.append(("context", u // PAIRS, 0))
        steps.append(todo)
    return steps


def xattn_kernel(nc, x, ctx_in, pos, tt, ln_in_w, ln_attn_w, ln_cross_w, v_qkv, l_qkv, v_dense, l_dense,
                 cq_w, ckv_w, cdense_w, v_gate, v_up, v_down, l_gate, l_up, l_down,
                 W_mem, W_gate, b_gate, norm_w, out):
    x_d = x.rearrange("b l h -> (b l) h")
    ctx_d = ctx_in.rearrange("b m c -> (b m) c")
    out_d = out.rearrange("b l h -> (b l) h")
    table = nc.inline_tensor(rotary_table(), name="rotary_table")
    table_d = table.ap() if hasattr(table, "ap") else table
    qkv_w, dense_w = [l_qkv, v_qkv], [l_dense, v_dense]
    gate_w, up_w, down_w = [l_gate, v_gate], [l_up, v_up], [l_down, v_down]

    def scratch(name, shape, dt=F32):
        return nc.dram_tensor(name, shape, dt, kind="Internal").ap()

    q_scr = scratch("q_scr", [2, H, B * L])
    k_scr = scratch("k_scr", [2, H, B * L])
    v_scr = scratch("v_scr", [B * L, NH * 64], F32)
    cq_scr = scratch("cq_scr", [2, C, B * L])
    ck_scr = scratch("ck_scr", [2, C, B * M])
    cv_scr = scratch("cv_scr", [B * M, NH * 32], F32)
    ctxT_scr = scratch("ctxT_scr", [2, P, KC, B * M])

    ctx = ExitStack()
    with ctx:
        def sem(name):
            return ctx.enter_context(nc.semaphore(name))

        base = (nc.sbuf_base + 31) // 32 * 32
        place = [base]

        def sb_at(name, shape, dt, offset):
            return nc.alloc_sbuf_tensor_at(name, shape, dt, offset=offset)

        def keep(name, shape, dt):
            words = int(np.prod(shape[1:])) * (2 if dt == BF16 else 4)
            t = sb_at(name, shape, dt, place[0])
            place[0] += (words + 31) // 32 * 32
            return t

        def area(size):
            at = place[0]
            place[0] += size
            return at

        hs = keep("hs", [P, T, H], F32)
        actT_hi = keep("actT_hi", [P, KH, B * L], F32R)
        actT_lo = keep("actT_lo", [P, KH, B * L], F32R)
        ident = keep("ident", [P, P], F32)
        ident_bf = keep("ident_bf", [P, P], BF16)
        hide_s = keep("hide_s", [P, P], BF16)
        hide_t = keep("hide_t", [P, P], BF16)
        w_row = keep("w_row", [P, H], F32)
        rot = keep("rot", [P, TB, 3 * HD // 2], F32)
        pos_i = keep("pos_i", [P, TB], I32)
        tt_now = keep("tt_now", [P, T], I32)
        tt_next = keep("tt_next", [P, T], I32)
        is_v = keep("is_v", [P, T], F32)
        is_l = keep("is_l", [P, T], F32)
        eq_tmp = keep("eq_tmp", [P, T], F32)
        sum_sq = keep("sum_sq", [P, 4, T], F32)
        rstd = keep("rstd", [P, 4, T], F32)
        minus_half = keep("minus_half", [P, 1], F32)
        row_max = keep("row_max", [P, 2, TB, 2], F32)
        max_parts = keep("max_parts", [P, 2, TB, 4], F32R)
        inv_den = keep("inv_den", [P, 2, TB, 2], F32)
        den = keep("den", [P, 2, T], F32)
        square_out = keep("square_out", [P, H], BF16)
        xs = keep("xs", [P, 2, H], F32)
        stage_hi = keep("stage_hi", [P, 2, H], F32R)
        stage_lo = keep("stage_lo", [P, 2, H], F32R)
        KB = 1024
        stage0 = sb_at("stage0", [P, H], F32, place[0] - 8 * KB)
        stage1 = sb_at("stage1", [P, H], F32, place[0] - 4 * KB)
        bias_row = sb_at("bias_row", [P, H], F32, place[0] - 2 * KB)
        area_a = area(48 * KB)
        area_b = area(16 * KB)
        area_c = area(16 * KB)
        area_d = area(36 * KB)
        area_e = area(18 * KB)
        area_f = area(8 * KB)
        assert place[0] <= nc.sbuf_usable_end, (place[0], nc.sbuf_usable_end)

        ctx_tile = sb_at("ctx_tile", [P, 4, C], F32, area_c)
        cv_tile = sb_at("cv_tile", [P, 2, NH, 32], F32, area_c + 4 * KB)
        ctxT_hi = sb_at("ctxT_hi", [P, KC, B * M], F32R, base + 16 * KB)
        ctxT_lo = sb_at("ctxT_lo", [P, KC, B * M], F32R, base + 32 * KB)
        slot_at = [area_d, area_a]
        raw_at = [area_e, area_b]
        qkv_hi = [sb_at(f"qkv_hi{s}", [P, 2, KH, H], F32R, slot_at[s]) for s in range(2)]
        qkv_lo = [sb_at(f"qkv_lo{s}", [P, 2, KH, H], F32R, slot_at[s] + 16 * KB) for s in range(2)]
        qkv_raw = [sb_at(f"qkv_raw{s}", [P, 2, KH, H], F32, raw_at[s]) for s in range(2)]
        ckv_hi = sb_at("ckv_hi", [P, KC, 2 * C], F32R, area_a)
        ckv_lo = sb_at("ckv_lo", [P, KC, 2 * C], F32R, area_a + 4 * KB)
        ckv_raw = sb_at("ckv_raw", [P, KC, 2 * C], F32, area_b)
        mixed = sb_at("mixed", [P, 2, H], F32, area_c)
        by_cos = sb_at("by_cos", [P, 2, H], F32, area_c + 4 * KB)
        by_sin = sb_at("by_sin", [P, 2, H], F32, area_c + 8 * KB)
        v_tile = sb_at("v_tile", [P, 2, NH, 64], F32, area_a + 32 * KB)
        q_st = [sb_at(f"q_st{s}", [P, 2, L], F32R, area_a + s * 12 * KB) for s in range(SLOTS)]
        k_st = [sb_at(f"k_st{s}", [P, 2, M], F32R, area_a + s * 12 * KB + 4 * KB) for s in range(SLOTS)]
        probs = sb_at("probs", [P, 4, 2, L], F32, area_b)
        v_st = [sb_at(f"v_st{s}", [P, 512], F32, area_c + s * 2 * KB) for s in range(SLOTS)]
        heads_out = sb_at("heads_out", [P, TB, H], F32, area_c + 8 * KB)
        cheads_out = sb_at("cheads_out", [P, TB, C], F32, area_c + 8 * KB)
        cq_raw = sb_at("cq_raw", [P, KH, C], F32, area_e)
        cq_hi = sb_at("cq_hi", [P, KH, C], F32R, area_e + 4 * KB)
        cq_lo = sb_at("cq_lo", [P, KH, C], F32R, area_e + 8 * KB)
        cd_raw = sb_at("cd_raw", [P, KC, H], F32, area_e + 12 * KB)
        cd_hi = sb_at("cd_hi", [P, KC, H], F32R, area_f)
        cd_lo = sb_at("cd_lo", [P, KC, H], F32R, area_f + 4 * KB)
        pv_out = xs
        odd_sum = sb_at("odd_sum", [P, 2, TB, 2, CHD + 1], F32, area_c + 12 * KB)
        half_max = sb_at("half_max", [P, 2, 2, TB, 2], F32, area_c + 14 * KB)
        ff_words = KH * 2 * FS[0] + 3 * H
        ff_hi = [sb_at(f"ff_hi{s}", [P, ff_words], F32R, slot_at[s]) for s in range(2)]
        ff_lo = [sb_at(f"ff_lo{s}", [P, ff_words], F32R, slot_at[s] + 18 * KB) for s in range(2)]
        ff_raw = [sb_at(f"ff_raw{s}", [P, ff_words], F32, [area_e, area_a + 36 * KB][s]) for s in range(2)]
        silu_g = sb_at("silu_g", [P, 2, FS[0]], F32, area_c)
        hid = sb_at("hid", [P, 2, FS[0]], F32, area_c + 3 * KB)
        hidT_hi = sb_at("hidT_hi", [P, 2, 3, P], F32R, area_c + 6 * KB)
        hidT_lo = sb_at("hidT_lo", [P, 2, 3, P], F32R, area_c + 9 * KB)
        mem = [area_a]

        def mem_at(name, shape, dt):
            t = sb_at(name, shape, dt, mem[0])
            mem[0] += int(np.prod(shape[1:])) * 4
            return t

        mp_hi = mem_at("mp_hi", [P, MT, H], F32R)
        mp_lo = mem_at("mp_lo", [P, MT, H], F32R)
        mpT_hi = mem_at("mpT_hi", [P, KH, M], F32R)
        mpT_lo = mem_at("mpT_lo", [P, KH, M], F32R)
        wg_raw = sb_at("wg_raw", [P, KH, 2 * H], F32, area_a)
        wm_raw = sb_at("wm_raw", [P, KH, C], F32, area_a + 16 * KB)
        wgT_hi = mem_at("wgT_hi", [P, 2 * KH, H], F32R)
        wgT_lo = mem_at("wgT_lo", [P, 2 * KH, H], F32R)
        wmT_hi = mem_at("wmT_hi", [P, KC, H], F32R)
        wmT_lo = mem_at("wmT_lo", [P, KC, H], F32R)
        mcT_hi = mem_at("mcT_hi", [P, KC, M], F32R)
        mcT_lo = mem_at("mcT_lo", [P, KC, M], F32R)
        attn = mem_at("attn", [P, 2, M], F32)
        attnT_hi = mem_at("attnT_hi", [P, MT, P], F32R)
        attnT_lo = mem_at("attnT_lo", [P, MT, P], F32R)
        mctx = mem_at("mctx", [P, H], F32)
        mctxT_hi = mem_at("mctxT_hi", [P, KH, P], F32R)
        mctxT_lo = mem_at("mctxT_lo", [P, KH, P], F32R)
        assert mem[0] <= area_f + 8 * KB, (mem[0], area_f + 8 * KB)

        def ps(name, shape):
            return ctx.enter_context(nc.psum_tensor(name, shape, F32))

        banks = [ps("work0", [P, H]), ps("work1", [P, H]), ps("pair0", [P, 2, H]), ps("pair1", [P, 2, H]),
                 ps("acc0", [P, H]), ps("acc1", [P, H])]
        W0, W1, PR0, PR1, A0, A1 = range(6)
        bank_filled = [sem(f"bank_filled{i}") for i in range(6)]
        bank_freed = [sem(f"bank_freed{i}") for i in range(6)]
        fills = [0] * 6
        filled_as = {}

        def claim(pe, product, place_):
            n = fills[place_]
            fills[place_] += 1
            assert product not in filled_as, product
            filled_as[product] = (place_, n)
            if n:
                pe.wait_ge(bank_freed[place_], n)
            return banks[place_]

        def fill_done(mm, product):
            mm.then_inc(bank_filled[filled_as[product][0]], 1)

        def wait_filled(eng, product):
            place_, n = filled_as[product]
            eng.wait_ge(bank_filled[place_], n + 1)
            return banks[place_]

        def free(ins, product):
            ins.then_inc(bank_freed[filled_as[product][0]], 1)

        def wait_emptied(eng, product):
            place_, n = filled_as[product]
            eng.wait_ge(bank_freed[place_], n + 1)

        consts_ready = sem("consts_ready")
        rot_ready = sem("rot_ready")
        small_in = sem("small_in")
        masks_ready = sem("masks_ready")
        w_row_in = sem("w_row_in")
        ctx_in_s = [sem(f"ctx_in{i}") for i in range(4)]
        x_in = [sem(f"x_in{t}") for t in range(T)]
        raw_in = [sem(f"raw_in{i}") for i in range(2)]
        weights_ready = [sem(f"weights_ready{i}") for i in range(2)]
        small_w_in = sem("small_w_in")
        small_w_ready = sem("small_w_ready")
        hi_done = sem("hi_done")
        stage_out = [sem(f"stage_out{i}") for i in range(2)]
        v_out = [sem(f"v_out{i}") for i in range(2)]
        ctxT_out = sem("ctxT_out")
        squares_done = sem("squares_done")
        rstd_done = sem("rstd_done")
        xs_done = sem("xs_done")
        by_sin_done = sem("by_sin_done")
        rotated = sem("rotated")
        stack_in = [sem(f"stack_in{i}") for i in range(SLOTS)]
        rows_in = [sem(f"rows_in{i}") for i in range(SLOTS)]
        parts_done = sem("parts_done")
        max_row_ready = sem("max_row_ready")
        values_done = sem("values_done")
        pv_copied = sem("pv_copied")
        heads_done = sem("heads_done")
        zeroed = sem("zeroed")
        silu_done = sem("silu_done")
        hid_done = sem("hid_done")
        pool_chain = sem("pool_chain")
        dve_chain = sem("dve_chain")
        lmem_in = sem("lmem_in")
        mcT_in = sem("mcT_in")
        nmax_done = sem("nmax_done")
        exp_done = sem("exp_done")
        gate_in = sem("gate_in")
        gate_done = sem("gate_done")
        mctx_done = sem("mctx_done")
        fused_done = sem("fused_done")
        row_done = sem("row_done")
        result_out = [sem(f"result_out{i}") for i in range(2)]
        next_zeroed = sem("next_zeroed")

        staged = [("kT", n, m) for n in range(B * M // L) for m in range(KC)]
        staged += [("rotT", c, t) for c in ("k", "q") for t in range(T)]
        staged += [("cqT", b, m) for b in range(B) for m in range(KC)]
        stage_no = {k: i for i, k in enumerate(staged)}
        hi_no = {}
        ff_cuts = [(e, f) for e in range(2) for f in range(len(FS))]
        QKV = ("v", "k", "q")
        uses = [0, 0]
        cut_at = {}
        for c in ["ckv", "v", "k", "q", "dense"] + ff_cuts:
            s = {"ckv": 1, "v": 0, "k": 1, "q": 0, "dense": 0}.get(c, None) if isinstance(c, str) else ff_cuts.index(c) % 2
            cut_at[c] = (s, uses[s])
            uses[s] += 1

        raw_count, loaded = {}, [16 * 6, 16 * 3]
        for e, f in ff_cuts:
            loaded[cut_at[(e, f)][0]] += 16 * (4 if FS[f] % P else 3)
            raw_count[(e, f)] = loaded[cut_at[(e, f)][0]]

        def wait_weights(eng, cut):
            s, n = cut_at[cut]
            eng.wait_ge(weights_ready[s], n + 1)

        self_steps = attention_steps(TB)
        cross_steps = attention_steps(MT)

        def three(pe, acc, stat, mov, first, last):
            s_hi, s_lo = stat
            m_hi, m_lo = mov
            pe.matmul(acc, s_hi, m_hi, start=first, stop=False)
            pe.matmul(acc, s_hi, m_lo, start=False, stop=False)
            return pe.matmul(acc, s_lo, m_hi, start=False, stop=last)

        def both(hi, lo, *key):
            return hi[key], lo[key]

        block = ctx.enter_context(nc.Block())

        @block.tensor
        def _(pe):
            pe.wait_ge(consts_ready, 1)
            for u in range(B * MT):
                pe.wait_ge(ctx_in_s[u % 4], 16 * (u // 4 + 1))
                acc = claim(pe, ("ctxT", u), u % 2)
                for k in range(KC):
                    mm = pe.transpose(acc[:, k * P:(k + 1) * P], ctx_tile[:, u % 4, k * P:(k + 1) * P], ident[:, :])
                fill_done(mm, ("ctxT", u))
            wait_weights(pe, "ckv")
            for n in range(B * M // L):
                for u in range(4 * n + 2, 4 * n + 4):
                    wait_emptied(pe, ("ctxT", u))
                for m in range(KC):
                    acc = claim(pe, ("kT", n, m), (A0, A1)[m])
                    for k in range(KC):
                        mm = three(pe, acc[:, :], both(ckv_hi, ckv_lo, slice(None), k, slice(m * P, (m + 1) * P)),
                                   both(ctxT_hi, ctxT_lo, slice(None), k, slice(n * L, (n + 1) * L)), k == 0, k == KC - 1)
                    fill_done(mm, ("kT", n, m))
            for u in range(B * MT):
                acc = claim(pe, ("cv", u), (PR0, PR1)[u % 2])
                for k in range(KC):
                    mm = three(pe, acc[:, 0, 0:C], both(ctxT_hi, ctxT_lo, slice(None), k, slice(u * P, (u + 1) * P)),
                               both(ckv_hi, ckv_lo, slice(None), k, slice(C, 2 * C)), k == 0, k == KC - 1)
                fill_done(mm, ("cv", u))

            def turn_act(stage, t):
                pe.wait_ge(xs_done, turn_no[(stage, t)] + 1)
                acc = claim(pe, ("actT", stage, t), t % 2)
                for k in range(KH):
                    mm = pe.transpose(acc[:, k * P:(k + 1) * P], xs[:, t % 2, k * P:(k + 1) * P], ident[:, :])
                fill_done(mm, ("actT", stage, t))

            for t in range(T):
                turn_act("in", t)

            def turn_rotated(c, t):
                pe.wait_ge(rotated, {"k": 0, "q": T}[c] + t + 1)
                acc = claim(pe, ("rotT", c, t), t % 2)
                for k in range(KH):
                    mm = pe.transpose(acc[:, k * P:(k + 1) * P], by_cos[:, t % 2, k * P:(k + 1) * P], ident[:, :])
                fill_done(mm, ("rotT", c, t))

            for c in QKV:
                wait_weights(pe, c)
                s = cut_at[c][0]
                for t in range(T):
                    if c == "v":
                        wait_emptied(pe, ("actT", "in", t))
                    for e in range(2):
                        acc = claim(pe, ("qkv", c, t, e), (A0, A1)[e])
                        for k in range(KH):
                            mm = three(pe, acc[:, :], both(actT_hi, actT_lo, slice(None), k, slice(t * P, (t + 1) * P)),
                                       both(qkv_hi[s], qkv_lo[s], slice(None), e, k, slice(None)), k == 0, k == KH - 1)
                        fill_done(mm, ("qkv", c, t, e))
                    if c != "v" and t >= 1:
                        turn_rotated(c, t - 1)
                if c != "v":
                    turn_rotated(c, T - 1)

            work = [0]

            def work_bank():
                work[0] += 1
                return work[0] % 2

            def attend(kind, steps, per_unit, uses_before):
                causal = kind == "self"
                for todo in steps:
                    for what, u, r in todo:
                        slot, use = u % SLOTS, u // SLOTS + uses_before
                        qs, ks = q_st[slot], k_st[slot]
                        if what == "scores":
                            if r == 0:
                                pe.wait_ge(stack_in[slot], 16 * 7 * (use + 1))
                                if u == 0:
                                    pe.wait_ge(zeroed, 1 if causal else 2)
                            for n in (2 * r, 2 * r + 1):
                                if causal:
                                    j, i = divmod(n, TB)
                                    product = (kind, "S", u, j, i)
                                    acc = claim(pe, product, work_bank())
                                    width = max(256, (i + 1) * P)
                                    pe.matmul(acc[:, 0:width], qs[0:ONES, j, i * P:(i + 1) * P], ks[0:ONES, j, 0:width],
                                              start=True, stop=True)
                                    mm = pe.matmul(acc[:, i * P:(i + 1) * P], ident_bf[:, :], hide_s[:, :],
                                                   start=False, stop=True, skip_group_check=True)
                                else:
                                    j, i, h = n // (2 * TB), n // 2 % TB, n % 2
                                    product = (kind, "S", u, j, i, h)
                                    acc = claim(pe, product, work_bank())
                                    mm = pe.matmul(acc[:, :], qs[0:ONES, j, i * P:(i + 1) * P],
                                                   ks[0:ONES, j, h * L:(h + 1) * L], start=True, stop=True)
                                fill_done(mm, product)
                        elif what == "max_rows":
                            pe.wait_ge(parts_done, u + 1 + (0 if causal else UNITS))
                            product = (kind, "max_rows", u)
                            acc = claim(pe, product, work_bank())
                            for i in range(TB):
                                mm = pe.transpose(acc[0:4, i * P:(i + 1) * P], max_parts[:, u % 2, i, :].bitcast(F32), ident[:, :])
                            fill_done(mm, product)
                        elif what == "probs":
                            if r == 0:
                                pe.wait_ge(rows_in[slot], 16 * 2 * (use + 1))
                            product = (kind, "T", u, r)
                            acc = claim(pe, product, (PR0, PR1)[(u * per_unit + r) % 2])
                            for j in range(2):
                                first = min(r * P, L - 256) if causal else 0
                                mm = pe.matmul(acc[:, j, first:L], ks[0:ONES + 2, j, r * P:(r + 1) * P],
                                               qs[0:ONES + 2, j, first:L], start=True, stop=True)
                                if causal:
                                    mm = pe.matmul(acc[:, j, r * P:(r + 1) * P], ident_bf[:, :], hide_t[:, :],
                                                   start=False, stop=True, skip_group_check=True)
                            fill_done(mm, product)
                        elif what == "values":
                            product = (kind, "PV", u)
                            if r == 0:
                                acc = claim(pe, product, (A0, A1)[u % 2])
                            acc = banks[(A0, A1)[u % 2]]
                            wait_emptied(pe, (kind, "T", u, r))
                            n = u * per_unit + r
                            if causal:
                                for j in range(2):
                                    mm = pe.matmul(acc[j * 64:(j + 1) * 64, r * P:L],
                                                   v_st[slot][:, (2 * r + j) * 64:(2 * r + j + 1) * 64],
                                                   probs[:, n % 4, j, r * P:L], start=(r == 0), stop=(r == per_unit - 1))
                            elif r % 2:
                                for j in range(2):
                                    for h in range(2):
                                        mm = pe.matmul(acc[(2 * j + h) * 32:(2 * j + h + 1) * 32, :],
                                                       v_st[slot][:, (2 * (r - 1 + h) + j) * 32:(2 * (r - 1 + h) + j + 1) * 32],
                                                       probs[:, (n - 1 + h) % 4, j, :], start=(r == 1), stop=(r == per_unit - 1))
                            if r == per_unit - 1:
                                fill_done(mm, product)
                            elif causal or r % 2:
                                mm.then_inc(values_done, 1)
                        elif what == "turn_back":
                            pe.wait_ge(pv_copied, u + 1 + (0 if causal else UNITS))
                            product = (kind, "PVT", u)
                            acc = claim(pe, product, work_bank())
                            for i in range(TB):
                                mm = pe.transpose(acc[:, i * P:(i + 1) * P], pv_out[:, u % 2, i * P:(i + 1) * P], ident[:, :])
                            fill_done(mm, product)
                        elif what == "context":
                            src, nk = (heads_out, KH) if causal else (cheads_out, KC)
                            pe.wait_ge(heads_done, (u + 1) * PAIRS + (0 if causal else UNITS))
                            for i in range(TB):
                                product = (kind, "ctxT", u, i)
                                acc = claim(pe, product, work_bank())
                                for k in range(nk):
                                    mm = pe.transpose(acc[:, k * P:(k + 1) * P], src[:, i, k * P:(k + 1) * P], ident[:, :])
                                fill_done(mm, product)

            attend("self", self_steps, TB, 0)

            wait_weights(pe, "dense")
            s = cut_at["dense"][0]
            for n in range(T + 2):
                if n < T:
                    wait_emptied(pe, ("self", "ctxT", n // TB, n % TB))
                    for e in range(2):
                        acc = claim(pe, ("dense", n, e), (A0, A1)[e])
                        for k in range(KH):
                            mm = three(pe, acc[:, :], both(actT_hi, actT_lo, slice(None), k, slice(n * P, (n + 1) * P)),
                                       both(qkv_hi[s], qkv_lo[s], slice(None), e, k, slice(None)), k == 0, k == KH - 1)
                        fill_done(mm, ("dense", n, e))
                if n >= 2:
                    turn_act("cross", n - 2)
            pe.wait_ge(small_w_ready, 1)
            for b in range(B):
                for t in range(b * TB + 2, (b + 1) * TB):
                    wait_emptied(pe, ("actT", "cross", t))
                for m in range(KC):
                    acc = claim(pe, ("cqT", b, m), (PR0, PR1)[m])
                    for k in range(KH):
                        mm = three(pe, acc[:, 0, :], both(cq_hi, cq_lo, slice(None), k, slice(m * P, (m + 1) * P)),
                                   both(actT_hi, actT_lo, slice(None), k, slice(b * L, (b + 1) * L)), k == 0, k == KH - 1)
                    fill_done(mm, ("cqT", b, m))

            attend("cross", cross_steps, MT, UNITS // SLOTS)

            pe.wait_ge(small_w_ready, 2)
            for n in range(T + 2):
                if n < T:
                    wait_emptied(pe, ("cross", "ctxT", n // TB, n % TB))
                    acc = claim(pe, ("cdense", n), (A0, A1)[n % 2])
                    for k in range(KC):
                        mm = three(pe, acc[:, :], both(actT_hi, actT_lo, slice(None), k, slice(n * P, (n + 1) * P)),
                                   both(cd_hi, cd_lo, slice(None), k, slice(None)), k == 0, k == KC - 1)
                    fill_done(mm, ("cdense", n))
                if n >= 2:
                    turn_act("mlp", n - 2)

            items = [(e, f, t) for e, f in ff_cuts for t in range(T)]
            for n in range(len(items) + 2):
                if n < len(items):
                    e, f, t = items[n]
                    fw = FS[f]
                    s = cut_at[(e, f)][0]
                    if t == 0:
                        wait_weights(pe, (e, f))
                    if e == 0 and f == 0:
                        wait_emptied(pe, ("actT", "mlp", t))
                    product = ("gu", e, f, t)
                    acc = claim(pe, product, (PR0, PR1)[n % 2])
                    parts = [(acc[:, 0, 0:fw], 0, fw), (acc[:, 1, 0:fw], fw, fw)] if fw >= 256 else [(acc[:, 0, 0:2 * fw], 0, 2 * fw)]
                    for dst, c0, w in parts:
                        for k in range(KH):
                            cols = slice(k * 2 * fw + c0, k * 2 * fw + c0 + w)
                            mm = three(pe, dst, both(actT_hi, actT_lo, slice(None), k, slice(t * P, (t + 1) * P)),
                                       both(ff_hi[s], ff_lo[s], slice(None), cols), k == 0, k == KH - 1)
                    fill_done(mm, product)
                if 1 <= n <= len(items):
                    e, f, t = items[n - 1]
                    pe.wait_ge(hid_done, n)
                    product = ("hidT", e, f, t)
                    acc = claim(pe, product, n % 2)
                    for k in range((FS[f] + P - 1) // P):
                        w = min(P, FS[f] - k * P)
                        mm = pe.transpose(acc[0:w, k * P:(k + 1) * P], hid[:, (n - 1) % 2, k * P:k * P + w], ident[:, :])
                    fill_done(mm, product)
                if n >= 2:
                    e, f, t = items[n - 2]
                    s = cut_at[(e, f)][0]
                    product = ("down", e, f, t)
                    wait_emptied(pe, ("hidT", e, f, t))
                    acc = claim(pe, product, (A0, A1)[n % 2])
                    nk = (FS[f] + P - 1) // P
                    for k in range(nk):
                        w = min(P, FS[f] - k * P)
                        cols = slice(KH * 2 * FS[f] + k * H, KH * 2 * FS[f] + (k + 1) * H)
                        mm = three(pe, acc[:, :], (hidT_hi[0:w, n % 2, k, :], hidT_lo[0:w, n % 2, k, :]),
                                   (ff_hi[s][0:w, cols], ff_lo[s][0:w, cols]), k == 0, k == nk - 1)
                    fill_done(mm, product)

            pe.wait_ge(lmem_in, 32)
            for g in range(KC + 2 * KH):
                product = ("wT", g)
                acc = claim(pe, product, g % 2)
                src, k = (wm_raw, g) if g < KC else (wg_raw, g - KC)
                for d in range(KH):
                    mm = pe.transpose(acc[:, d * P:(d + 1) * P], src[:, d, k * P:(k + 1) * P], ident[:, :])
                fill_done(mm, product)
            for t in range(T):
                wait_emptied(pe, ("down", 1, len(FS) - 1, t))
                acc = claim(pe, ("hsT", t), t % 2)
                for k in range(KH):
                    mm = pe.transpose(acc[:, k * P:(k + 1) * P], hs[:, t, k * P:(k + 1) * P], ident[:, :])
                fill_done(mm, ("hsT", t))
            for b in range(B):
                pe.wait_ge(mcT_in, 32 * (b + 1))
                for g in range(KC):
                    wait_emptied(pe, ("wT", g))
                for d in range(KH):
                    for n in range(M // L):
                        product = ("mpT", b, d, n)
                        acc = claim(pe, product, (A0, A1)[n % 2])
                        for k in range(KC):
                            mm = three(pe, acc[:, :], both(wmT_hi, wmT_lo, slice(None), k, slice(d * P, (d + 1) * P)),
                                       both(mcT_hi, mcT_lo, slice(None), k, slice(n * L, (n + 1) * L)), k == 0, k == KC - 1)
                        fill_done(mm, product)
                for m in range(MT):
                    product = ("mp", b, m)
                    acc = claim(pe, product, (A0, A1)[m % 2])
                    for k in range(KC):
                        mm = three(pe, acc[:, :], both(mcT_hi, mcT_lo, slice(None), k, slice(m * P, (m + 1) * P)),
                                   both(wmT_hi, wmT_lo, slice(None), k, slice(None)), k == 0, k == KC - 1)
                    fill_done(mm, product)
                wait_emptied(pe, ("mpT", b, KH - 1, 0))
                wait_emptied(pe, ("mpT", b, KH - 1, 1))

                def memory_scores(t):
                    wait_emptied(pe, ("hsT", t))
                    product = ("ms", t)
                    acc = claim(pe, product, (PR0, PR1)[t % 2])
                    for n in range(M // L):
                        for k in range(KH):
                            mm = three(pe, acc[:, n, :], both(actT_hi, actT_lo, slice(None), k, slice(t * P, (t + 1) * P)),
                                       both(mpT_hi, mpT_lo, slice(None), k, slice(n * L, (n + 1) * L)), k == 0, k == KH - 1)
                    fill_done(mm, product)

                memory_scores(b * TB)
                for t in range(b * TB, (b + 1) * TB):
                    if t + 1 < (b + 1) * TB:
                        memory_scores(t + 1)
                    pe.wait_ge(exp_done, t + 1)
                    for h in range(2):
                        product = ("attnT", t, h)
                        acc = claim(pe, product, h)
                        for k in range(4):
                            m = 4 * h + k
                            mm = pe.transpose(acc[:, k * P:(k + 1) * P], attn[:, t % 2, m * P:(m + 1) * P], ident[:, :])
                        fill_done(mm, product)
                    if t == b * TB:
                        wait_emptied(pe, ("mp", b, MT - 2))
                        wait_emptied(pe, ("mp", b, MT - 1))
                    product = ("mctx", t)
                    acc = claim(pe, product, A0)
                    for m in range(MT):
                        if m % 4 == 0:
                            wait_emptied(pe, ("attnT", t, m // 4))
                        mm = three(pe, acc[:, :], both(attnT_hi, attnT_lo, slice(None), m, slice(None)),
                                   both(mp_hi, mp_lo, slice(None), m, slice(None)), m == 0, m == MT - 1)
                    fill_done(mm, product)
                    product = ("gate", t)
                    acc = claim(pe, product, A1)
                    if t == 0:
                        for g in range(KC + 2 * KH - 2, KC + 2 * KH):
                            wait_emptied(pe, ("wT", g))
                    for k in range(KH):
                        three(pe, acc[:, :], both(actT_hi, actT_lo, slice(None), k, slice(t * P, (t + 1) * P)),
                              both(wgT_hi, wgT_lo, slice(None), k, slice(None)), k == 0, False)
                    pe.wait_ge(mctx_done, t + 1)
                    acc2 = claim(pe, ("mctxT", t), t % 2)
                    for k in range(KH):
                        mm = pe.transpose(acc2[:, k * P:(k + 1) * P], mctx[:, k * P:(k + 1) * P], ident[:, :])
                    fill_done(mm, ("mctxT", t))
                    wait_emptied(pe, ("mctxT", t))
                    for k in range(KH):
                        mm = three(pe, acc[:, :], both(mctxT_hi, mctxT_lo, slice(None), k, slice(None)),
                                   both(wgT_hi, wgT_lo, slice(None), KH + k, slice(None)), False, k == KH - 1)
                    fill_done(mm, product)

        @block.scalar
        def _(act):
            def hi_part(product, dst, src_of):
                acc = wait_filled(act, product)
                hi_no[product] = len(hi_no) + 1
                act.activation(dst, src_of(acc), ACT.Copy).then_inc(hi_done, 1)

            def tiles(acc, n=KH):
                return acc[:, 0:n * P].rearrange("p (k t) -> p k t", k=n)

            def staged_hi(product, src_of=lambda a: a[:, :]):
                z = stage_no[product]
                if z >= 2:
                    act.wait_ge(stage_out[z % 2], 32 * (z // 2))
                hi_part(product, stage_hi[:, z % 2, :], src_of)

            def squares(stage, t, product):
                if product is None:
                    act.wait_ge(x_in[t], 16)
                else:
                    wait_emptied(act, product)
                before = NORMS.index(stage) * T + t
                if before:
                    act.wait_ge(squares_done, before)
                act.activation(square_out[:, :], hs[:, t, :], ACT.Square,
                               accum_out=sum_sq[:, NORMS.index(stage), t:t + 1]).then_inc(squares_done, 1)

            def act_hi(product, t, n=KH):
                hi_part(product, actT_hi[:, 0:n, t * P:(t + 1) * P], lambda a: tiles(a, n))

            for u in range(B * MT):
                hi_part(("ctxT", u), ctxT_hi[:, :, u * P:(u + 1) * P], lambda a: tiles(a, KC))
                if u % 2:
                    squares("in", u // 2, None)
            for n in range(B * M // L):
                for m in range(KC):
                    staged_hi(("kT", n, m))
            act.wait_ge(consts_ready, 2)
            for u in range(B * MT):
                acc = wait_filled(act, ("cv", u))
                if u >= 2:
                    act.wait_ge(v_out[u % 2], 16 * (u // 2))
                free(act.activation(cv_tile[:, u % 2, :, 0:CHD], acc[:, 0, 0:C].rearrange("p (h d) -> p h d", h=NH),
                                    ACT.Copy), ("cv", u))
            act.wait_ge(ctxT_out, 32)
            for t in range(T):
                act_hi(("actT", "in", t), t)
            for c in ("k", "q"):
                for t in range(T):
                    staged_hi(("rotT", c, t))

            def attend(kind, steps, per_unit, uses_before):
                causal = kind == "self"
                scale = 1.0 / np.sqrt(HD if causal else CHD)
                for todo in steps:
                    for what, u, r in todo:
                        slot = u % SLOTS
                        if what == "max_rows":
                            acc = wait_filled(act, (kind, "max_rows", u))
                            v = u + (0 if causal else UNITS)
                            if v == 0:
                                act.wait_ge(stage_out[0], 32 * ((stage_no[("rotT", "q", T - 1)] + 1) // 2))
                                act.wait_ge(stage_out[1], 32 * ((stage_no[("rotT", "q", T - 1)] + 1) // 2))
                            if v == UNITS:
                                act.wait_ge(stage_out[0], 32 * (len(staged) // 2))
                                act.wait_ge(stage_out[1], 32 * (len(staged) // 2))
                            if v >= 2:
                                act.wait_ge(rows_in[(v - 2) % SLOTS], 32 * ((v - 2) // SLOTS + 1))
                            ins = act.activation(stage_hi[0:4, v % 2, :], acc[0:4, :], ACT.Copy)
                            free(ins, (kind, "max_rows", u))
                            wait_emptied(act, (kind, "max_rows", u))
                            for part in range(2):
                                act.dma_start(raw32(q_st[slot][ONES + part:ONES + part + 1, :, :]),
                                              raw32(stage_hi[2 * part:2 * part + 2, v % 2, :])).then_inc(rows_in[slot], 16)
                        elif what == "probs":
                            n = u * per_unit + r
                            acc = wait_filled(act, (kind, "T", u, r))
                            if n >= 4:
                                lu, lr = divmod(n - 4, per_unit)
                                lr = lr if causal else lr // 2
                                if lr == 3:
                                    wait_filled(act, (kind, "PV", lu))
                                else:
                                    act.wait_ge(values_done, 3 * (lu + (0 if causal else UNITS)) + lr + 1)
                            first = r * P if causal else 0
                            free(act.activation(probs[:, n % 4, :, first:L], acc[:, :, first:L], ACT.Exp, scale=scale),
                                 (kind, "T", u, r))
                        elif what == "context":
                            for i in range(TB):
                                act_hi((kind, "ctxT", u, i), u * TB + i, KH if causal else KC)

            attend("self", self_steps, TB, 0)
            for n in range(T + 2):
                if n < T:
                    squares("cross", n, ("dense", n, 1))
                if n >= 2:
                    act_hi(("actT", "cross", n - 2), n - 2)
            for v in (UNITS - 2, UNITS - 1):
                act.wait_ge(rows_in[v % SLOTS], 32 * (v // SLOTS + 1))
            for b in range(B):
                for m in range(KC):
                    staged_hi(("cqT", b, m), lambda a: a[:, 0, :])
            attend("cross", cross_steps, MT, UNITS // SLOTS)
            for n in range(T + 2):
                if n < T:
                    squares("mlp", n, ("cdense", n))
                if n >= 2:
                    act_hi(("actT", "mlp", n - 2), n - 2)

            items = [(e, f, t) for e, f in ff_cuts for t in range(T)]
            for n in range(len(items) + 1):
                if n < len(items):
                    e, f, t = items[n]
                    acc = wait_filled(act, ("gu", e, f, t))
                    if n >= 2:
                        act.wait_ge(hid_done, n - 1)
                    act.activation(silu_g[:, n % 2, 0:FS[f]], acc[:, 0, 0:FS[f]], ACT.Silu).then_inc(silu_done, 1)
                if n >= 1:
                    e, f, t = items[n - 1]
                    product = ("hidT", e, f, t)
                    if n >= 3:
                        e0, f0, t0 = items[n - 3]
                        wait_filled(act, ("down", e0, f0, t0))
                    acc = wait_filled(act, product)
                    nk = (FS[f] + P - 1) // P
                    hi_no[product] = len(hi_no) + 1
                    full = FS[f] // P
                    ins = act.activation(hidT_hi[:, (n - 1) % 2, 0:full, :], tiles(acc, full), ACT.Copy)
                    if nk > full:
                        w = FS[f] - full * P
                        ins = act.activation(hidT_hi[0:w, (n - 1) % 2, full, :], acc[0:w, full * P:(full + 1) * P], ACT.Copy)
                    ins.then_inc(hi_done, 1)

            for g in range(KC + 2 * KH):
                dst = wmT_hi[:, g, :] if g < KC else wgT_hi[:, g - KC, :]
                hi_part(("wT", g), dst, lambda a: a[:, :])
            for t in range(T):
                act_hi(("hsT", t), t)
            for b in range(B):
                for d in range(KH):
                    for n in range(M // L):
                        hi_part(("mpT", b, d, n), mpT_hi[:, d, n * L:(n + 1) * L], lambda a: a[:, :])
                for m in range(MT):
                    hi_part(("mp", b, m), mp_hi[:, m, :], lambda a: a[:, :])

                def memory_exp(t):
                    acc = wait_filled(act, ("ms", t))
                    act.wait_ge(nmax_done, t + 1)
                    if t >= 2:
                        wait_filled(act, ("attnT", t - 2, 1))
                    ins = act.activation(attn[:, t % 2, :], acc[:, :, :].rearrange("p a b -> p (a b)"), ACT.Exp,
                                         bias=den[:, 0, t:t + 1], scale=1.0 / np.sqrt(H), accum_out=den[:, 1, t:t + 1])
                    ins.then_inc(exp_done, 1)

                memory_exp(b * TB)
                for t in range(b * TB, (b + 1) * TB):
                    if t + 1 < (b + 1) * TB:
                        memory_exp(t + 1)
                    for h in range(2):
                        hi_part(("attnT", t, h), attnT_hi[:, 4 * h:4 * h + 4, :], lambda a: tiles(a, 4))
                    hi_part(("mctxT", t), mctxT_hi[:, :, :], lambda a: tiles(a, KH))
                    act.wait_ge(gate_in, t + 1)
                    act.activation(stage1[:, :], stage0[:, :], ACT.Tanh, scale=0.5).then_inc(gate_done, 1)
                    act.wait_ge(fused_done, t + 1)
                    act.wait_ge(squares_done, 3 * T + t)
                    act.activation(square_out[:, :], xs[:, t % 2, :], ACT.Square,
                                   accum_out=sum_sq[:, 3, t:t + 1]).then_inc(squares_done, 1)

        @block.vector
        def _(dve):
            chain = [0]

            def link(ins):
                chain[0] += 1
                ins.then_inc(dve_chain, 1)
                dve.wait_ge(dve_chain, chain[0])

            def tiles(acc, n=KH):
                return acc[:, 0:n * P].rearrange("p (k t) -> p k t", k=n)

            def lo_part(product, dst, hi, src_of):
                dve.wait_ge(hi_done, hi_no[product])
                acc = banks[filled_as[product][0]]
                free(dve.tensor_tensor(dst, src_of(acc), hi.bitcast(F32), ALU.subtract), product)

            def staged_lo(product, src_of=lambda a: a[:, :]):
                z = stage_no[product]
                lo_part(product, stage_lo[:, z % 2, :], stage_hi[:, z % 2, :], src_of)

            def act_lo(product, t, n=KH):
                cols = slice(t * P, (t + 1) * P)
                lo_part(product, actT_lo[:, 0:n, cols], actT_hi[:, 0:n, cols], lambda a: tiles(a, n))

            def normed(stage, t):
                no = turn_no[(stage, t)]
                dve.wait_ge(rstd_done, no + 1)
                if no >= 2:
                    wait_filled(dve, ("actT", *TURNS[no - 2]))
                dve.scalar_tensor_tensor(out=xs[:, t % 2, :], in0=hs[:, t, :],
                                         scalar=rstd[:, NORMS.index(stage), t:t + 1], in1=w_row[:, :],
                                         op0=ALU.mult, op1=ALU.mult).then_inc(xs_done, 1)

            dve.wait_ge(small_in, SMALL)
            link(dve.tensor_scalar(eq_tmp[:, :], tt_next[:, :], 1.0, None, ALU.is_equal))
            link(dve.tensor_scalar(is_l[:, :], tt_now[:, :], 1.0, None, ALU.is_equal))
            link(dve.tensor_tensor(is_v[:, :], is_l[:, :], eq_tmp[:, :], ALU.mult))
            link(dve.tensor_scalar(is_l[:, :], is_v[:, :], -1.0, 1.0, ALU.mult, ALU.add))
            masks = [is_l, is_v]

            for u in range(B * MT):
                lo_part(("ctxT", u), ctxT_lo[:, :, u * P:(u + 1) * P], ctxT_hi[:, :, u * P:(u + 1) * P],
                        lambda a: tiles(a, KC))
            for n in range(B * M // L):
                for m in range(KC):
                    staged_lo(("kT", n, m))
            dve.wait_ge(w_row_in, 16)
            for t in range(T):
                normed("in", t)
                if t >= 1:
                    act_lo(("actT", "in", t - 1), t - 1)
            act_lo(("actT", "in", T - 1), T - 1)

            dve.wait_ge(rot_ready, 16 * TB)
            wait_filled(dve, ("cv", B * MT - 1))
            for v in range(2):
                dve.wait_ge(v_out[v], 16 * MT)
            done_mix = 0
            for ci, c in enumerate(QKV):
                for t in range(T):
                    for e in range(2):
                        acc = wait_filled(dve, ("qkv", c, t, e))
                        if c == "v":
                            if e == 0 and t >= 2:
                                dve.wait_ge(v_out[t % 2], 16 * (MT + t // 2))
                            if e == 0 and t < 2:
                                dve.wait_ge(consts_ready, 3)
                            dst = v_tile[:, t % 2, :, 0:HD]
                            src = acc[:, :].rearrange("p (h d) -> p h d", h=NH)
                        else:
                            dst, src = mixed[:, t % 2, :], acc[:, :]
                            if e == 0 and done_mix >= 2:
                                dve.wait_ge(by_sin_done, done_mix - 1)
                        if e == 0:
                            ins = dve.tensor_scalar(dst, src, masks[0][:, t:t + 1], None, ALU.mult)
                            free(ins, ("qkv", c, t, e))
                            wait_emptied(dve, ("qkv", c, t, e))
                        else:
                            ins = dve.scalar_tensor_tensor(out=dst, in0=src, scalar=masks[1][:, t:t + 1], in1=dst,
                                                           op0=ALU.mult, op1=ALU.add)
                            free(ins, ("qkv", c, t, e))
                            wait_emptied(dve, ("qkv", c, t, e))
                    if c == "v":
                        continue
                    done_mix += 1
                    if done_mix >= 3:
                        z = done_mix - 3
                        wait_filled(dve, ("rotT", "kq"[z // T], z % T))
                    heads = mixed[:, t % 2, :].rearrange("p (a d) -> p a d", d=HD // 2)
                    link(dve.tensor_tensor(by_cos[:, t % 2, :].rearrange("p (a d) -> p a d", d=HD // 2), heads,
                                           rot[:, t % TB, 0:HD // 2].unsqueeze(1).to_broadcast([P, 2 * NH, HD // 2]), ALU.mult))
                    dve.wait_ge(by_sin_done, done_mix)
                    dve.tensor_tensor(by_cos[:, t % 2, :], by_cos[:, t % 2, :], by_sin[:, t % 2, :], ALU.add).then_inc(rotated, 1)
                    if t >= 1:
                        staged_lo(("rotT", c, t - 1))
                if c != "v":
                    staged_lo(("rotT", c, T - 1))

            def attend(kind, steps, per_unit):
                causal = kind == "self"
                before = 0 if causal else UNITS
                for todo in steps:
                    for what, u, r in todo:
                        if what == "scores":
                            for n in (2 * r, 2 * r + 1):
                                if causal:
                                    j, i = divmod(n, TB)
                                    product = (kind, "S", u, j, i)
                                    acc = wait_filled(dve, product)
                                    if n == 0 and u + before >= 2:
                                        dve.wait_ge(parts_done, u + before - 1)
                                    free(dve.tensor_reduce(row_max[:, u % 2, i, j:j + 1], acc[:, 0:(i + 1) * P], AX, ALU.max,
                                                           negate=True), product)
                                else:
                                    j, i, h = n // (2 * TB), n // 2 % TB, n % 2
                                    product = (kind, "S", u, j, i, h)
                                    acc = wait_filled(dve, product)
                                    dst = half_max[:, u % 2, h, i, j:j + 1]
                                    free(dve.tensor_reduce(dst, acc[:, :], AX, ALU.max, negate=True), product)
                        elif what == "max_parts":
                            if causal:
                                lasts = [(kind, "S", u, 1, TB - 2), (kind, "S", u, 1, TB - 1)]
                            else:
                                lasts = [(kind, "S", u, 1, TB - 1, 0), (kind, "S", u, 1, TB - 1, 1)]
                            for p_ in lasts:
                                wait_emptied(dve, p_)
                            if not causal:
                                link(dve.tensor_tensor(row_max[:, u % 2, :, :], half_max[:, u % 2, 0, :, :],
                                                       half_max[:, u % 2, 1, :, :], ALU.min))
                            v = u + before
                            if v >= 2:
                                k2 = "self" if v - 2 < UNITS else "cross"
                                wait_filled(dve, (k2, "max_rows", (v - 2) % UNITS))
                            link(dve.tensor_copy(max_parts[:, u % 2, :, 0:2], row_max[:, u % 2, :, :]))
                            dve.tensor_tensor(max_parts[:, u % 2, :, 2:4], row_max[:, u % 2, :, :],
                                              max_parts[:, u % 2, :, 0:2].bitcast(F32), ALU.subtract).then_inc(parts_done, 1)
                        elif what == "values" and r == per_unit - 1:
                            acc = wait_filled(dve, (kind, "PV", u))
                            if u >= 2:
                                wait_filled(dve, (kind, "PVT", u - 2))
                            ins = dve.tensor_copy(pv_out[:, u % 2, :], acc[:, :])
                            ins.then_inc(pv_copied, 1)
                            dve.wait_ge(pv_copied, u + 1 + before)
                            dve.sem_inc(bank_freed[filled_as[(kind, "PV", u)][0]], 1)
                        elif what == "turn_back":
                            acc = wait_filled(dve, (kind, "PVT", u))
                            pair = u % PAIRS
                            if u == PAIRS:
                                for i in range(TB):
                                    wait_filled(dve, (kind, "ctxT", 0, i))
                            if causal:
                                v4 = acc[:, :].rearrange("p (i j d) -> p i j d", i=TB, j=2)
                                link(dve.reciprocal(inv_den[:, u % 2, :, :], v4[:, :, :, HD]))
                                dst = heads_out[:, :, 2 * pair * HD:(2 * pair + 2) * HD].rearrange("p i (j d) -> p i j d", j=2)
                                ins = dve.tensor_tensor(dst, v4[:, :, :, 0:HD],
                                                        inv_den[:, u % 2, :, :].unsqueeze(3).to_broadcast([P, TB, 2, HD]), ALU.mult)
                                ins.then_inc(heads_done, 1)
                                dve.wait_ge(heads_done, u + 1)
                                dve.sem_inc(bank_freed[filled_as[(kind, "PVT", u)][0]], 1)
                            else:
                                v5 = acc[:, :].rearrange("p (i j h d) -> p i j h d", i=TB, j=2, h=2)
                                sums = odd_sum[:, u % 2, :, :, :]
                                link(dve.tensor_copy(sums, v5[:, :, :, 1, 0:CHD + 1]))
                                ins = dve.tensor_tensor(sums, v5[:, :, :, 0, 0:CHD + 1], sums, ALU.add)
                                free(ins, (kind, "PVT", u))
                                wait_emptied(dve, (kind, "PVT", u))
                                link(dve.reciprocal(inv_den[:, u % 2, :, :], sums[:, :, :, CHD]))
                                dst = cheads_out[:, :, 2 * pair * CHD:(2 * pair + 2) * CHD].rearrange("p i (j d) -> p i j d", j=2)
                                dve.tensor_tensor(dst, sums[:, :, :, 0:CHD],
                                                  inv_den[:, u % 2, :, :].unsqueeze(3).to_broadcast([P, TB, 2, CHD]), ALU.mult)\
                                   .then_inc(heads_done, 1)
                        elif what == "context":
                            for i in range(TB):
                                act_lo((kind, "ctxT", u, i), u * TB + i, KH if causal else KC)

            dve.wait_ge(small_in, SMALL)
            wait_filled(dve, ("qkv", "k", T - 1, 1))
            for v in range(2):
                dve.wait_ge(v_out[v], 16 * (MT + T // 2))
            for s in range(SLOTS):
                ins = dve.memset(raw32(k_st[s][ONES:ONES + 2, :, :]), 1.0)
            ins.then_inc(zeroed, 1)
            attend("self", self_steps, TB)
            dve.wait_ge(w_row_in, 32)
            for n in range(T + 2):
                if n < T:
                    for e in range(2):
                        acc = wait_filled(dve, ("dense", n, e))
                        free(dve.scalar_tensor_tensor(out=hs[:, n, :], in0=acc[:, :], scalar=masks[e][:, n:n + 1],
                                                      in1=hs[:, n, :], op0=ALU.mult, op1=ALU.add), ("dense", n, e))
                        wait_emptied(dve, ("dense", n, e))
                if 1 <= n <= T:
                    if n == 1:
                        wait_filled(dve, ("self", "PVT", UNITS - 1))
                    normed("cross", n - 1)
                if n >= 2:
                    act_lo(("actT", "cross", n - 2), n - 2)
            wait_filled(dve, ("self", "PV", UNITS - 1))
            for s in range(SLOTS):
                for r0 in (32, 64):
                    dve.memset(raw32(q_st[s][r0:r0 + 32, :, :]), 0.0)
                    dve.memset(raw32(k_st[s][r0:r0 + 32, :, :]), 0.0)
                ins = dve.memset(raw32(k_st[s][ONES:ONES + 2, :, :]), 1.0)
            ins.then_inc(zeroed, 1)
            for b in range(B):
                for m in range(KC):
                    staged_lo(("cqT", b, m), lambda a: a[:, 0, :])
            attend("cross", cross_steps, MT)
            dve.wait_ge(w_row_in, 48)
            for n in range(T + 2):
                if n < T:
                    acc = wait_filled(dve, ("cdense", n))
                    free(dve.tensor_tensor(hs[:, n, :], acc[:, :], hs[:, n, :], ALU.add), ("cdense", n))
                    wait_emptied(dve, ("cdense", n))
                if 1 <= n <= T:
                    if n == 1:
                        wait_filled(dve, ("cross", "PVT", UNITS - 1))
                    normed("mlp", n - 1)
                if n >= 2:
                    act_lo(("actT", "mlp", n - 2), n - 2)

            items = [(e, f, t) for e, f in ff_cuts for t in range(T)]
            for n in range(len(items) + 2):
                if n < len(items):
                    e, f, t = items[n]
                    fw = FS[f]
                    dve.wait_ge(silu_done, n + 1)
                    acc = banks[filled_as[("gu", e, f, t)][0]]
                    if n >= 2:
                        wait_filled(dve, ("hidT", *items[n - 2]))
                    src = acc[:, 1, 0:fw] if fw >= 256 else acc[:, 0, fw:2 * fw]
                    ins = dve.tensor_tensor(hid[:, n % 2, 0:fw], src, silu_g[:, n % 2, 0:fw], ALU.mult)
                    ins.then_inc(hid_done, 1)
                    dve.wait_ge(hid_done, n + 1)
                    dve.sem_inc(bank_freed[filled_as[("gu", e, f, t)][0]], 1)
                if n >= 1 and n - 1 < len(items):
                    e, f, t = items[n - 1]
                    product = ("hidT", e, f, t)
                    dve.wait_ge(hi_done, hi_no[product])
                    acc = banks[filled_as[product][0]]
                    full = FS[f] // P
                    s = (n - 1) % 2
                    ins = dve.tensor_tensor(hidT_lo[:, s, 0:full, :], tiles(acc, full),
                                            hidT_hi[:, s, 0:full, :].bitcast(F32), ALU.subtract)
                    if FS[f] > full * P:
                        w = FS[f] - full * P
                        ins = dve.tensor_tensor(hidT_lo[0:w, s, full, :], acc[0:w, full * P:(full + 1) * P],
                                                hidT_hi[0:w, s, full, :].bitcast(F32), ALU.subtract)
                    free(ins, product)
                if n >= 2:
                    e, f, t = items[n - 2]
                    product = ("down", e, f, t)
                    acc = wait_filled(dve, product)
                    free(dve.scalar_tensor_tensor(out=hs[:, t, :], in0=acc[:, :], scalar=masks[e][:, t:t + 1],
                                                  in1=hs[:, t, :], op0=ALU.mult, op1=ALU.add), product)

            for g in range(KC + 2 * KH):
                hi, lo = (wmT_hi[:, g, :], wmT_lo[:, g, :]) if g < KC else (wgT_hi[:, g - KC, :], wgT_lo[:, g - KC, :])
                lo_part(("wT", g), lo, hi, lambda a: a[:, :])
            for t in range(T):
                act_lo(("hsT", t), t)
            for b in range(B):
                for d in range(KH):
                    for n in range(M // L):
                        cols = slice(n * L, (n + 1) * L)
                        lo_part(("mpT", b, d, n), mpT_lo[:, d, cols], mpT_hi[:, d, cols], lambda a: a[:, :])
                for m in range(MT):
                    lo_part(("mp", b, m), mp_lo[:, m, :], mp_hi[:, m, :], lambda a: a[:, :])

                def memory_max(t):
                    acc = wait_filled(dve, ("ms", t))
                    link(dve.tensor_reduce(row_max[:, 0, 0, 0:1], acc[:, :, :].rearrange("p a b -> p (a b)"), AX, ALU.max, negate=True))
                    dve.tensor_scalar(den[:, 0, t:t + 1], row_max[:, 0, 0, 0:1], float(1.0 / np.sqrt(H)), None, ALU.mult)\
                       .then_inc(nmax_done, 1)

                def memory_freed(t):
                    dve.wait_ge(exp_done, t + 1)
                    dve.sem_inc(bank_freed[filled_as[("ms", t)][0]], 1)

                memory_max(b * TB)
                for t in range(b * TB, (b + 1) * TB):
                    memory_freed(t)
                    if t + 1 < (b + 1) * TB:
                        memory_max(t + 1)
                    for h in range(2):
                        lo_part(("attnT", t, h), attnT_lo[:, 4 * h:4 * h + 4, :], attnT_hi[:, 4 * h:4 * h + 4, :],
                                lambda a: tiles(a, 4))
                    acc = wait_filled(dve, ("mctx", t))
                    link(dve.reciprocal(inv_den[:, 0, 0, 0:1], den[:, 1, t:t + 1]))
                    ins = dve.tensor_scalar(mctx[:, :], acc[:, :], inv_den[:, 0, 0, 0:1], None, ALU.mult)
                    free(ins, ("mctx", t))
                    wait_emptied(dve, ("mctx", t))
                    dve.sem_inc(mctx_done, 1)
                    lo_part(("mctxT", t), mctxT_lo[:, :, :], mctxT_hi[:, :, :], lambda a: tiles(a, KH))
                    acc = wait_filled(dve, ("gate", t))
                    if t == 0:
                        dve.wait_ge(w_row_in, 80)
                    ins = dve.tensor_tensor(stage0[:, :], acc[:, :], bias_row[:, :], ALU.add)
                    free(ins, ("gate", t))
                    wait_emptied(dve, ("gate", t))
                    dve.sem_inc(gate_in, 1)
                    dve.wait_ge(gate_done, t + 1)
                    link(dve.scalar_tensor_tensor(out=stage0[:, :], in0=stage1[:, :], scalar=1.0,
                                                  in1=mctx[:, :], op0=ALU.add, op1=ALU.mult))
                    if t >= 2:
                        dve.wait_ge(result_out[t % 2], 16 * (t // 2))
                    dve.scalar_tensor_tensor(out=xs[:, t % 2, :], in0=stage0[:, :], scalar=0.5,
                                             in1=hs[:, t, :], op0=ALU.mult, op1=ALU.add).then_inc(fused_done, 1)
                    dve.wait_ge(rstd_done, 3 * T + t + 1)
                    dve.scalar_tensor_tensor(out=xs[:, t % 2, :], in0=xs[:, t % 2, :], scalar=rstd[:, 3, t:t + 1],
                                             in1=w_row[:, :], op0=ALU.mult, op1=ALU.mult).then_inc(row_done, 1)

        @block.gpsimd
        def _(pool):
            chain = [0]

            def link(ins):
                chain[0] += 1
                ins.then_inc(pool_chain, 1)
                pool.wait_ge(pool_chain, chain[0])

            pool.memset(tt_next[:, :], 0).then_inc(next_zeroed, 1)
            link(pool.memset(ident[:, :], 0.0))
            pool.affine_select(out=ident[:, :], in_=ident[:, :], compare_op=ALU.not_equal, fill=1.0, base=0,
                               pattern=[[-1, P]], channel_multiplier=1).then_inc(consts_ready, 1)
            pool.memset(cv_tile[:, :, :, CHD:2 * CHD], 1.0).then_inc(consts_ready, 1)
            link(pool.memset(minus_half[:, :], -0.5))
            pool.wait_ge(small_in, SMALL)
            for i in range(TB):
                pool.indirect_dma_start(rot[:, i, :], None, table_d[:, :],
                                        bass.IndirectOffsetOnAxis(ap=pos_i[:, i:i + 1].bitcast(U32), axis=0))\
                    .then_inc(rot_ready, 16)

            def split(hi, lo, raw, ready):
                link(pool.tensor_copy(hi, raw))
                pool.tensor_tensor(lo, raw, hi.bitcast(F32), ALU.subtract).then_inc(ready, 1)

            def norm_scale(stage, t):
                i = NORMS.index(stage)
                pool.wait_ge(squares_done, i * T + t + 1)
                link(pool.tensor_scalar(sum_sq[:, i, t:t + 1], sum_sq[:, i, t:t + 1], 1.0 / H, EPS, ALU.mult, ALU.add))
                pool.tensor_tensor(rstd[:, i, t:t + 1], sum_sq[:, i, t:t + 1], minus_half[:, :], ALU.pow).then_inc(rstd_done, 1)

            pool.wait_ge(raw_in[1], 16)
            split(ckv_hi[:, :, :], ckv_lo[:, :, :], ckv_raw[:, :, :], weights_ready[1])
            link(pool.memset(ident_bf[:, :], 0.0))
            link(pool.affine_select(out=ident_bf[:, :], in_=ident_bf[:, :], compare_op=ALU.not_equal, fill=1.0, base=0,
                                    pattern=[[-1, P]], channel_multiplier=1))
            link(pool.memset(hide_s[:, :], 0.0))
            link(pool.memset(hide_t[:, :], 0.0))
            link(pool.affine_select(out=hide_s[:, :], in_=hide_s[:, :], compare_op=ALU.is_ge, fill=NEG, base=0,
                                    pattern=[[-1, P]], channel_multiplier=1))
            link(pool.affine_select(out=hide_t[:, :], in_=hide_t[:, :], compare_op=ALU.is_ge, fill=NEG, base=0,
                                    pattern=[[1, P]], channel_multiplier=-1))
            for t in range(T):
                norm_scale("in", t)
                if t == 1:
                    pool.wait_ge(raw_in[0], 32)
                    split(qkv_hi[0][:, :, :, :], qkv_lo[0][:, :, :, :], qkv_raw[0][:, :, :, :], weights_ready[0])
            wait_filled(pool, ("cv", B * MT - 1))
            pool.memset(v_tile[:, :, :, HD:64], 1.0).then_inc(consts_ready, 1)
            pool.wait_ge(raw_in[1], 16 + 32)
            split(qkv_hi[1][:, :, :, :], qkv_lo[1][:, :, :, :], qkv_raw[1][:, :, :, :], weights_ready[1])
            done = 0
            for c in ("k", "q"):
                for t in range(T):
                    wait_emptied(pool, ("qkv", c, t, 1))
                    if t == 0 and c == "k":
                        pool.wait_ge(rot_ready, 16 * TB)
                    if done >= 2:
                        pool.wait_ge(rotated, done - 1)
                    m4 = mixed[:, t % 2, :].rearrange("p (h a d) -> p h a d", h=NH, a=2)
                    b4 = by_sin[:, t % 2, :].rearrange("p (h a d) -> p h a d", h=NH, a=2)
                    hd = HD // 2
                    sin = rot[:, t % TB, hd:2 * hd].unsqueeze(1).to_broadcast([P, NH, hd])
                    nsin = rot[:, t % TB, 2 * hd:3 * hd].unsqueeze(1).to_broadcast([P, NH, hd])
                    pool.tensor_tensor(b4[:, :, 0, :], m4[:, :, 1, :], nsin, ALU.mult)
                    pool.tensor_tensor(b4[:, :, 1, :], m4[:, :, 0, :], sin, ALU.mult).then_inc(by_sin_done, 1)
                    done += 1
                    if c == "k" and t == 0:
                        wait_filled(pool, ("qkv", "v", T - 1, 1))
                        pool.wait_ge(raw_in[0], 64)
                        split(qkv_hi[0][:, :, :, :], qkv_lo[0][:, :, :, :], qkv_raw[0][:, :, :, :], weights_ready[0])
            wait_filled(pool, ("qkv", "q", T - 1, 1))
            pool.wait_ge(raw_in[0], 96)
            split(qkv_hi[0][:, :, :, :], qkv_lo[0][:, :, :, :], qkv_raw[0][:, :, :, :], weights_ready[0])
            pool.wait_ge(small_w_in, 32)
            split(cq_hi[:, :, :], cq_lo[:, :, :], cq_raw[:, :, :], small_w_ready)
            split(cd_hi[:, :, :], cd_lo[:, :, :], cd_raw[:, :, :], small_w_ready)
            for t in range(T):
                norm_scale("cross", t)

            def split_ff(n):
                e, f = ff_cuts[n]
                s, use = cut_at[(e, f)]
                used = [KH * 2 * FS[f], (FS[f] // P) * H, FS[f] % P]
                pool.wait_ge(raw_in[s], raw_count[(e, f)])
                if n == 0:
                    wait_filled(pool, ("dense", T - 1, 1))
                elif n == 1:
                    wait_filled(pool, ("cross", "PV", UNITS - 1))
                elif n >= 2:
                    wait_filled(pool, ("down", *ff_cuts[n - 2], T - 1))
                a, b_, c_ = used
                link(pool.tensor_copy(ff_hi[s][:, 0:a + b_], ff_raw[s][:, 0:a + b_]))
                if c_:
                    link(pool.tensor_copy(ff_hi[s][0:c_, a + b_:a + b_ + H], ff_raw[s][0:c_, a + b_:a + b_ + H]))
                    link(pool.tensor_tensor(ff_lo[s][0:c_, a + b_:a + b_ + H], ff_raw[s][0:c_, a + b_:a + b_ + H],
                                            ff_hi[s][0:c_, a + b_:a + b_ + H].bitcast(F32), ALU.subtract))
                pool.tensor_tensor(ff_lo[s][:, 0:a + b_], ff_raw[s][:, 0:a + b_],
                                   ff_hi[s][:, 0:a + b_].bitcast(F32), ALU.subtract).then_inc(weights_ready[s], 1)

            split_ff(0)
            for t in range(T):
                norm_scale("mlp", t)
            for n in range(1, len(ff_cuts)):
                split_ff(n)
            for t in range(T):
                pool.wait_ge(squares_done, 3 * T + t + 1)
                link(pool.tensor_scalar(sum_sq[:, 3, t:t + 1], sum_sq[:, 3, t:t + 1], 1.0 / H, EPS, ALU.mult, ALU.add))
                pool.tensor_tensor(rstd[:, 3, t:t + 1], sum_sq[:, 3, t:t + 1], minus_half[:, :], ALU.pow).then_inc(rstd_done, 1)

        @block.sync
        def _(sp):
            def rows(w):
                return w.rearrange("(k p) n -> p k n", p=P)

            def row_on_all(v):
                return v.rearrange("(a n) -> a n", a=1).to_broadcast([P, H])

            def load_cut(c):
                s = cut_at[c][0]
                for e in range(2):
                    if c == "dense":
                        src = rows(dense_w[e])
                    else:
                        j = ("q", "k", "v").index(c)
                        src = rows(qkv_w[e])[:, :, j * H:(j + 1) * H]
                    sp.dma_start(qkv_raw[s][:, e, :, :], src).then_inc(raw_in[s], 16)

            for u in range(4):
                sp.dma_start(ctx_tile[:, u, :], ctx_d[u * P:(u + 1) * P, :]).then_inc(ctx_in_s[u], 16)
            sp.dma_start(ckv_raw[:, :, :], rows(ckv_w)).then_inc(raw_in[1], 16)
            with nc.allow_non_contiguous_dma(reason="one small column per token tile"):
                sp.wait_ge(next_zeroed, 1)
                sp.dma_start(pos_i[:, :], pos.rearrange("a (i p) -> p (a i)", p=P)).then_inc(small_in, 16)
                sp.dma_start(tt_now[:, :], tt.rearrange("b (i p) -> p (b i)", p=P)).then_inc(small_in, 16)
                shifted = tt.rearrange("b (i p) -> p b i", p=P)
                sp.dma_start(tt_next[0:P - 1, :].rearrange("p (b i) -> p b i", b=B), shifted[1:P, :, :]).then_inc(small_in, 16)
                for b in range(B):
                    sp.dma_start(tt_next[P - 1:P, b * TB:(b + 1) * TB - 1], shifted[0:1, b, 1:TB]).then_inc(small_in, 16)
            for u in range(4, B * MT):
                wait_filled(sp, ("ctxT", u - 4))
                sp.dma_start(ctx_tile[:, u % 4, :], ctx_d[u * P:(u + 1) * P, :]).then_inc(ctx_in_s[u % 4], 16)
                if u % 2 == 0 and u // 2 - 2 < T:
                    t = u // 2 - 2
                    sp.dma_start(hs[:, t, :], x_d[t * P:(t + 1) * P, :]).then_inc(x_in[t], 16)
            for t in range(6, T):
                sp.dma_start(hs[:, t, :], x_d[t * P:(t + 1) * P, :]).then_inc(x_in[t], 16)
            sp.dma_start(w_row[:, :], row_on_all(ln_in_w)).then_inc(w_row_in, 16)
            load_cut("v")

            def store_staged(product, dst, view):
                z = stage_no[product]
                wait_emptied(sp, product)
                sp.dma_start(dst[0], view(raw32(stage_hi[:, z % 2, :]))).then_inc(stage_out[z % 2], 16)
                sp.dma_start(dst[1], view(raw32(stage_lo[:, z % 2, :]))).then_inc(stage_out[z % 2], 16)

            for n in range(B * M // L):
                for m in range(KC):
                    d = ck_scr[:, m * P:(m + 1) * P, n * L:(n + 1) * L]
                    store_staged(("kT", n, m), (d[0], d[1]), lambda a: a)
            wait_emptied(sp, ("ctxT", B * MT - 1))
            wait_emptied(sp, ("ctxT", B * MT - 2))
            sp.dma_start(ctxT_scr[0], raw32(ctxT_hi[:, :, :])).then_inc(ctxT_out, 16)
            sp.dma_start(ctxT_scr[1], raw32(ctxT_lo[:, :, :])).then_inc(ctxT_out, 16)
            sp.wait_ge(weights_ready[1], 1)
            load_cut("k")
            for u in range(B * MT):
                wait_emptied(sp, ("cv", u))
                sp.dma_start(cv_scr[u * P:(u + 1) * P, :], cv_tile[:, u % 2, :, :].rearrange("p h d -> p (h d)"))\
                    .then_inc(v_out[u % 2], 16)
            sp.wait_ge(weights_ready[0], 1)
            load_cut("q")
            for t in range(T):
                wait_emptied(sp, ("qkv", "v", t, 1))
                sp.dma_start(v_scr[t * P:(t + 1) * P, :], v_tile[:, t % 2, :, :].rearrange("p h d -> p (h d)"))\
                    .then_inc(v_out[t % 2], 16)
            for c, scr in (("k", k_scr), ("q", q_scr)):
                for t in range(T):
                    if c == "q" and t == 0:
                        sp.wait_ge(weights_ready[0], 2)
                        load_cut("dense")
                    d = scr[:, :, t * P:(t + 1) * P].rearrange("a (k p) n -> a p k n", p=P)
                    store_staged(("rotT", c, t), (d[0], d[1]), lambda a: a.rearrange("p (k n) -> p k n", k=KH))

            def load_stack(kind, u, uses_before):
                slot, b, pair = u % SLOTS, u // PAIRS, u % PAIRS
                w, scr_q, scr_k = (HD, q_scr, k_scr) if kind == "self" else (CHD, cq_scr, ck_scr)
                n_k = L if kind == "self" else M
                if u >= SLOTS:
                    wait_filled(sp, (kind, "PV", u - SLOTS))
                for row, part_q, part_k in ((0, 0, 0), (1, 0, 1), (2, 1, 0)):
                    feats = slice(2 * pair * w, (2 * pair + 2) * w)
                    sp.dma_start(raw32(q_st[slot][row * w:(row + 1) * w, :, :]),
                                 scr_q[part_q, feats, b * L:(b + 1) * L].rearrange("(j p) n -> p j n", j=2)).then_inc(stack_in[slot], 16)
                    sp.dma_start(raw32(k_st[slot][row * w:(row + 1) * w, :, 0:n_k]),
                                 scr_k[part_k, feats, b * n_k:(b + 1) * n_k].rearrange("(j p) n -> p j n", j=2)).then_inc(stack_in[slot], 16)
                if kind == "self":
                    src = v_scr[b * L:(b + 1) * L, pair * 128:(pair + 1) * 128].rearrange("(k p) c -> p k c", p=P)
                    dst = v_st[slot][:, :].rearrange("p (k c) -> p k c", k=TB)
                else:
                    src = cv_scr[b * M:(b + 1) * M, pair * 64:(pair + 1) * 64].rearrange("(k p) c -> p k c", p=P)
                    dst = v_st[slot][:, :].rearrange("p (k c) -> p k c", k=MT)
                sp.dma_start(dst, src).then_inc(stack_in[slot], 16)

            n_staged = stage_no[("rotT", "q", T - 1)] + 1
            for i in range(2):
                sp.wait_ge(stage_out[i], 32 * (n_staged // 2))
                sp.wait_ge(v_out[i], 16 * (MT + T // 2))
            sp.wait_ge(zeroed, 1)
            for u in range(UNITS):
                load_stack("self", u, 0)
                if u == 5:
                    sp.wait_ge(weights_ready[0], 3)
                    sp.dma_start(cq_raw[:, :, :], rows(cq_w)).then_inc(small_w_in, 16)
                    sp.dma_start(cd_raw[:, :, :], rows(cdense_w)).then_inc(small_w_in, 16)
                    wait_filled(sp, ("actT", "in", T - 1))
                    sp.dma_start(w_row[:, :], row_on_all(ln_cross_w)).then_inc(w_row_in, 16)
            for b in range(B):
                for m in range(KC):
                    d = cq_scr[:, m * P:(m + 1) * P, b * L:(b + 1) * L]
                    store_staged(("cqT", b, m), (d[0], d[1]), lambda a: a)
            for i in range(2):
                sp.wait_ge(stage_out[i], 32 * (len(staged) // 2))
            sp.wait_ge(zeroed, 2)

            def load_ff(n):
                e, f = ff_cuts[n]
                s = cut_at[(e, f)][0]
                f0, fw = sum(FS[:f]), FS[f]
                a = KH * 2 * fw
                if n >= 2:
                    sp.wait_ge(weights_ready[s], cut_at[(e, f)][1])
                gu = ff_raw[s][:, 0:a].rearrange("p (k g n) -> p k g n", k=KH, g=2)
                sp.dma_start(gu[:, :, 0, :], rows(gate_w[e])[:, :, f0:f0 + fw]).then_inc(raw_in[s], 16)
                sp.dma_start(gu[:, :, 1, :], rows(up_w[e])[:, :, f0:f0 + fw]).then_inc(raw_in[s], 16)
                full = fw // P
                dn = ff_raw[s][:, a:a + full * H].rearrange("p (k n) -> p k n", k=full)
                sp.dma_start(dn, rows(down_w[e][f0:f0 + full * P, :])).then_inc(raw_in[s], 16)
                if fw % P:
                    w = fw % P
                    sp.dma_start(ff_raw[s][0:w, a + full * H:a + (full + 1) * H],
                                 down_w[e][f0 + full * P:f0 + fw, :]).then_inc(raw_in[s], 16)

            for u in range(UNITS):
                load_stack("cross", u, UNITS // SLOTS)
                if u == 5:
                    sp.wait_ge(small_w_ready, 2)
                    wait_filled(sp, ("cqT", B - 1, KC - 1))
                    load_ff(0)
                    wait_filled(sp, ("actT", "cross", T - 1))
                    sp.dma_start(w_row[:, :], row_on_all(ln_attn_w)).then_inc(w_row_in, 16)
            wait_filled(sp, ("cross", "PV", UNITS - 1))
            for n in range(1, len(ff_cuts)):
                load_ff(n)
            wait_filled(sp, ("down", 1, len(FS) - 1, T - 1))
            sp.dma_start(wm_raw[:, :, :], rows(W_mem)).then_inc(lmem_in, 16)
            sp.dma_start(wg_raw[:, :, :], rows(W_gate)).then_inc(lmem_in, 16)
            sp.dma_start(w_row[:, :], row_on_all(norm_w)).then_inc(w_row_in, 16)
            sp.dma_start(bias_row[:, :], row_on_all(b_gate)).then_inc(w_row_in, 16)
            for b in range(B):
                if b:
                    wait_filled(sp, ("mp", b - 1, MT - 1))
                for part, dst in enumerate((mcT_hi, mcT_lo)):
                    sp.dma_start(raw32(dst[:, :, :]), ctxT_scr[part, :, :, b * M:(b + 1) * M]).then_inc(mcT_in, 16)
            for t in range(T):
                sp.wait_ge(row_done, t + 1)
                sp.dma_start(out_d[t * P:(t + 1) * P, :], xs[:, t % 2, :]).then_inc(result_out[t % 2], 16)
            for i in range(2):
                sp.wait_ge(result_out[i], 16 * T // 2)


_INS = ["x", "ctx_1024", "pos_1xS", "mask_BxS_ik0", "L0_xattn_ln_in_w", "L0_xattn_ln_post_attn_w",
        "L0_xattn_ln_post_cross_w", "L0_xattn_v_qkv", "L0_xattn_l_qkv", "L0_xattn_v_dense", "L0_xattn_l_dense",
        "L0_xattn_cq_w", "L0_xattn_ckv_w", "L0_xattn_cdense_w", "L0_xattn_v_gate", "L0_xattn_v_up",
        "L0_xattn_v_down", "L0_xattn_l_gate", "L0_xattn_l_up", "L0_xattn_l_down", "L1_xattn_W_mem",
        "L1_xattn_W_gate", "L1_xattn_b_gate", "L1_xattn_norm_w"]
_OUTS = [((B, L, H), "float32")]


def kernel(**inputs):
    import numpy as _np
    import concourse.bacc as _bacc
    from concourse import mybir as _mybir
    from concourse.bass_utils import run_bass_kernel_spmd as _run

    nc = _bacc.Bacc("TRN2", target_bir_lowering=False, num_devices=1)
    arrays, args = {}, []
    for name in _INS:
        a = _np.ascontiguousarray(inputs[name])
        arrays[f"in_{name}_dram"] = a
        args.append(nc.dram_tensor(f"in_{name}_dram", a.shape, _mybir.dt.from_np(a.dtype), kind="ExternalInput").ap())
    for i, (shape, dtype) in enumerate(_OUTS):
        dt = _mybir.dt.from_np(_np.dtype(dtype))
        args.append(nc.dram_tensor(f"out_{i}_dram", shape, dt, kind="ExternalOutput").ap())
    xattn_kernel(nc, *args)
    r = _run(nc, [arrays], core_ids=[0])
    got = tuple(r.results[0][f"out_{i}_dram"] for i in range(len(_OUTS)))
    return got[0]
```

```python
import numpy as np
import concourse.bass as bass
from concourse import mybir
from contextlib import ExitStack

F32 = mybir.dt.float32
F32R = mybir.dt.float32r
BF16 = mybir.dt.bfloat16
I32 = mybir.dt.int32
U32 = mybir.dt.uint32
ALU = mybir.AluOpType
ACT = mybir.ActivationFunctionType
AX = mybir.AxisListType.X

P = 128
B, L, H = 2, 512, 512
T = B * L // P
TB = L // P
KH = H // P
NH = 16
HD = H // NH
C = 256
KC = C // P
CHD = C // NH
M = 1024
MT = M // P
F = 1376
EPS = 1e-6
NEG = -1e30
PAIRS = NH // 2
UNITS = B * PAIRS
SLOTS = 4
ONES = 96
FS = [384, 384, 384, 224]

NORMS = ["in", "cross", "mlp"]
TURNS = [(s, t) for s in NORMS for t in range(T)]
turn_no = {k: i for i, k in enumerate(TURNS)}
SMALL = 16 * (3 + B)


def rotary_table():
    inv = (1.0 / np.float32(10000.0) ** (np.arange(0, HD, 2, dtype=np.float32) / np.float32(HD))).astype(np.float32)
    a = np.outer(np.arange(L, dtype=np.float32), inv).astype(np.float32)
    return np.concatenate([np.cos(a), np.sin(a), -np.sin(a)], axis=1).astype(np.float32)


def raw32(ap):
    return ap.bitcast(F32)


def attention_steps(per_unit):
    lead = per_unit + 4
    n = UNITS * per_unit
    steps = []
    for x in range(lead + n + 7):
        todo = []
        if x < n:
            todo.append(("scores", x // per_unit, x % per_unit))
        u, r = divmod(x - 1, per_unit)
        if r == per_unit - 1 and 0 <= u < UNITS:
            todo.append(("max_parts", u, 0))
        u, r = divmod(x - 2, per_unit)
        if r == per_unit - 1 and 0 <= u < UNITS:
            todo.append(("max_rows", u, 0))
        y = x - lead
        if 0 <= y < n:
            todo.append(("probs", y // per_unit, y % per_unit))
        if 0 <= y - 1 < n:
            todo.append(("values", (y - 1) // per_unit, (y - 1) % per_unit))
        u, r = divmod(y - 3, per_unit)
        if y >= 3 and r == per_unit - 1 and u < UNITS:
            todo.append(("turn_back", u, 0))
        u, r = divmod(y - 5, per_unit)
        if y >= 5 and r == per_unit - 1 and u < UNITS and u % PAIRS == PAIRS - 1:
            todo.append(("context", u // PAIRS, 0))
        steps.append(todo)
    return steps


def xattn_kernel(nc, x, ctx_in, pos, tt, ln_in_w, ln_attn_w, ln_cross_w, v_qkv, l_qkv, v_dense, l_dense,
                 cq_w, ckv_w, cdense_w, v_gate, v_up, v_down, l_gate, l_up, l_down,
                 W_mem, W_gate, b_gate, norm_w, out):
    x_d = x.rearrange("b l h -> (b l) h")
    ctx_d = ctx_in.rearrange("b m c -> (b m) c")
    out_d = out.rearrange("b l h -> (b l) h")
    table = nc.inline_tensor(rotary_table(), name="rotary_table")
    table_d = table.ap() if hasattr(table, "ap") else table
    qkv_w, dense_w = [l_qkv, v_qkv], [l_dense, v_dense]
    gate_w, up_w, down_w = [l_gate, v_gate], [l_up, v_up], [l_down, v_down]

    def scratch(name, shape, dt=F32):
        return nc.dram_tensor(name, shape, dt, kind="Internal").ap()

    q_scr = scratch("q_scr", [2, H, B * L])
    k_scr = scratch("k_scr", [2, H, B * L])
    v_scr = scratch("v_scr", [B * L, NH * 64], F32)
    cq_scr = scratch("cq_scr", [2, C, B * L])
    ck_scr = scratch("ck_scr", [2, C, B * M])
    cv_scr = scratch("cv_scr", [B * M, NH * 32], F32)

    ctx = ExitStack()
    with ctx:
        def sem(name):
            return ctx.enter_context(nc.semaphore(name))

        base = (nc.sbuf_base + 31) // 32 * 32
        place = [base]

        def sb_at(name, shape, dt, offset):
            return nc.alloc_sbuf_tensor_at(name, shape, dt, offset=offset)

        def keep(name, shape, dt):
            words = int(np.prod(shape[1:])) * (2 if dt == BF16 else 4)
            t = sb_at(name, shape, dt, place[0])
            place[0] += (words + 31) // 32 * 32
            return t

        def area(size):
            at = place[0]
            place[0] += size
            return at

        hs = keep("hs", [P, T, H], F32)
        actT_hi = keep("actT_hi", [P, KH, B * L], F32R)
        actT_lo = keep("actT_lo", [P, KH, B * L], F32R)
        ident = keep("ident", [P, P], F32)
        ident_bf = keep("ident_bf", [P, P], BF16)
        hide_s = keep("hide_s", [P, P], BF16)
        hide_t = keep("hide_t", [P, P], BF16)
        w_row = keep("w_row", [P, H], F32)
        rot = keep("rot", [P, TB, 3 * HD // 2], F32)
        pos_i = keep("pos_i", [P, TB], I32)
        tt_now = keep("tt_now", [P, T], I32)
        tt_next = keep("tt_next", [P, T], I32)
        is_v = keep("is_v", [P, T], F32)
        is_l = keep("is_l", [P, T], F32)
        vision_count = keep("vision_count", [1, T], I32)
        eq_tmp = keep("eq_tmp", [P, T], F32)
        sum_sq = keep("sum_sq", [P, 4, T], F32)
        rstd = keep("rstd", [P, 4, T], F32)
        minus_half = keep("minus_half", [P, 1], F32)
        row_max = keep("row_max", [P, 2, TB, 2], F32)
        max_parts = keep("max_parts", [P, 2, TB, 4], F32R)
        inv_den = keep("inv_den", [P, 2, TB, 2], F32)
        den = keep("den", [P, 2, T], F32)
        square_out = keep("square_out", [P, H], BF16)
        xs = keep("xs", [P, 2, H], F32)
        stage_hi = keep("stage_hi", [P, 2, H], F32R)
        stage_lo = keep("stage_lo", [P, 2, H], F32R)
        KB = 1024
        stage0 = sb_at("stage0", [P, H], F32, place[0] - 8 * KB)
        stage1 = sb_at("stage1", [P, H], F32, place[0] - 4 * KB)
        bias_row = sb_at("bias_row", [P, H], F32, place[0] - 2 * KB)
        area_a = area(48 * KB)
        area_b = area(16 * KB)
        area_c = area(16 * KB)
        area_d = area(36 * KB)
        area_e = area(18 * KB)
        area_f = area(8 * KB)
        assert place[0] <= nc.sbuf_usable_end, (place[0], nc.sbuf_usable_end)

        ctx_tile = sb_at("ctx_tile", [P, B * MT, C], F32, area_e)
        cv_tile = sb_at("cv_tile", [P, 4, NH, 32], F32, area_c + 8 * KB)
        ctxT_hi = sb_at("ctxT_hi", [P, KC, B * M], F32R, base + 16 * KB)
        ctxT_lo = sb_at("ctxT_lo", [P, KC, B * M], F32R, base + 32 * KB)
        slot_at = [area_d, area_a]
        raw_at = [area_e, area_b]
        qkv_hi = [sb_at(f"qkv_hi{s}", [P, 2, KH, H], F32R, slot_at[s]) for s in range(2)]
        qkv_lo = [sb_at(f"qkv_lo{s}", [P, 2, KH, H], F32R, slot_at[s] + 16 * KB) for s in range(2)]
        qkv_raw = [sb_at(f"qkv_raw{s}", [P, 2, KH, H], F32, raw_at[s]) for s in range(2)]
        ckv_hi = sb_at("ckv_hi", [P, KC, 2 * C], F32R, area_f)
        ckv_lo = sb_at("ckv_lo", [P, KC, 2 * C], F32R, area_f + 4 * KB)
        ckv_raw = sb_at("ckv_raw", [P, KC, 2 * C], F32, area_c)
        mixed = sb_at("mixed", [P, 2, H], F32, area_b)
        by_cos = sb_at("by_cos", [P, 2, H], F32, area_b + 4 * KB)
        by_sin = sb_at("by_sin", [P, 2, H], F32, area_b + 8 * KB)
        v_tile = sb_at("v_tile", [P, 2, NH, 64], F32, area_a + 32 * KB)
        q_st = [sb_at(f"q_st{s}", [P, 2, L], F32R, area_a + s * 12 * KB) for s in range(SLOTS)]
        k_st = [sb_at(f"k_st{s}", [P, 2, M], F32R, area_a + s * 12 * KB + 4 * KB) for s in range(SLOTS)]
        probs = sb_at("probs", [P, 4, 2, L], F32, area_b)
        v_st = [sb_at(f"v_st{s}", [P, 512], F32, area_c + s * 2 * KB) for s in range(SLOTS)]
        heads_out = sb_at("heads_out", [P, TB, H], F32, area_c + 8 * KB)
        cheads_out = sb_at("cheads_out", [P, TB, C], F32, area_c + 8 * KB)
        cq_raw = sb_at("cq_raw", [P, KH, C], F32, area_e)
        cq_hi = sb_at("cq_hi", [P, KH, C], F32R, area_e + 4 * KB)
        cq_lo = sb_at("cq_lo", [P, KH, C], F32R, area_e + 8 * KB)
        cd_raw = sb_at("cd_raw", [P, KC, H], F32, area_e + 12 * KB)
        cd_hi = sb_at("cd_hi", [P, KC, H], F32R, area_f)
        cd_lo = sb_at("cd_lo", [P, KC, H], F32R, area_f + 4 * KB)
        pv_out = xs
        odd_sum = sb_at("odd_sum", [P, 2, TB, 2, CHD + 1], F32, area_c + 12 * KB)
        half_max = sb_at("half_max", [P, 2, 2, TB, 2], F32, area_c + 14 * KB)
        ff_words = KH * 2 * FS[0] + 3 * H
        ff_hi = [sb_at(f"ff_hi{s}", [P, ff_words], F32R, slot_at[s]) for s in range(2)]
        ff_lo = [sb_at(f"ff_lo{s}", [P, ff_words], F32R, slot_at[s] + 18 * KB) for s in range(2)]
        ff_raw = [sb_at(f"ff_raw{s}", [P, ff_words], F32, [area_e, area_a + 36 * KB][s]) for s in range(2)]
        silu_g = sb_at("silu_g", [P, 2, FS[0]], F32, area_c)
        hid = sb_at("hid", [P, 2, FS[0]], F32, area_c + 3 * KB)
        hidT_hi = sb_at("hidT_hi", [P, 2, 3, P], F32R, area_c + 6 * KB)
        hidT_lo = sb_at("hidT_lo", [P, 2, 3, P], F32R, area_c + 9 * KB)
        wg_raw = sb_at("wg_raw", [P, KH, 2 * H], F32, area_e)
        wm_raw = sb_at("wm_raw", [P, KH, C], F32, area_f)
        wgT_hi = sb_at("wgT_hi", [P, 2 * KH, H], F32R, area_d)
        wgT_lo = sb_at("wgT_lo", [P, 2 * KH, H], F32R, area_d + 16 * KB)
        qm_hi = sb_at("qm_hi", [P, KC, B * L], F32R, area_d + 8 * KB)
        qm_lo = sb_at("qm_lo", [P, KC, B * L], F32R, area_d + 24 * KB)
        mem = [area_a]

        def mem_at(name, shape, dt, cursor=mem):
            t = sb_at(name, shape, dt, cursor[0])
            cursor[0] += int(np.prod(shape[1:])) * 4
            return t

        mcT_hi = mem_at("mcT_hi", [P, KC, B * M], F32R)
        mcT_lo = mem_at("mcT_lo", [P, KC, B * M], F32R)
        mc_hi = mem_at("mc_hi", [P, MT, C], F32R)
        mc_lo = mem_at("mc_lo", [P, MT, C], F32R)
        mc_raw = mem_at("mc_raw", [P, MT, C], F32)
        wm_hi = mem_at("wm_hi", [P, KH, C], F32R)
        wm_lo = mem_at("wm_lo", [P, KH, C], F32R)
        wmT_hi = mem_at("wmT_hi", [P, KC, H], F32R)
        wmT_lo = mem_at("wmT_lo", [P, KC, H], F32R)
        G_hi = mem_at("G_hi", [P, KC, H], F32R)
        G_lo = mem_at("G_lo", [P, KC, H], F32R)
        assert mem[0] <= area_d, (mem[0], area_d)
        mem2 = [area_e]
        attn = mem_at("attn", [P, 2, M], F32, mem2)
        attnT_hi = mem_at("attnT_hi", [P, MT, P], F32R, mem2)
        attnT_lo = mem_at("attnT_lo", [P, MT, P], F32R, mem2)
        am = mem_at("am", [P, C], F32, mem2)
        amT_hi = mem_at("amT_hi", [P, KC, P], F32R, mem2)
        assert mem2[0] <= area_f, (mem2[0], area_f)
        amT_lo = sb_at("amT_lo", [P, KC, P], F32R, area_f + 4 * KB)

        def ps(name, shape):
            return ctx.enter_context(nc.psum_tensor(name, shape, F32))

        banks = [ps("work0", [P, H]), ps("work1", [P, H]), ps("pair0", [P, 2, H]), ps("pair1", [P, 2, H]),
                 ps("acc0", [P, H]), ps("acc1", [P, H])]
        W0, W1, PR0, PR1, A0, A1 = range(6)
        bank_filled = [sem(f"bank_filled{i}") for i in range(6)]
        bank_freed = [sem(f"bank_freed{i}") for i in range(6)]
        fills = [0] * 6
        filled_as = {}

        def claim(pe, product, place_):
            n = fills[place_]
            fills[place_] += 1
            assert product not in filled_as, product
            filled_as[product] = (place_, n)
            if n:
                pe.wait_ge(bank_freed[place_], n)
            return banks[place_]

        def fill_done(mm, product):
            mm.then_inc(bank_filled[filled_as[product][0]], 1)

        def wait_filled(eng, product):
            place_, n = filled_as[product]
            eng.wait_ge(bank_filled[place_], n + 1)
            return banks[place_]

        def wait_used(eng, *last_two):
            for product in last_two:
                wait_filled(eng, product)

        def free(ins, product):
            ins.then_inc(bank_freed[filled_as[product][0]], 1)

        def wait_emptied(eng, product):
            place_, n = filled_as[product]
            eng.wait_ge(bank_freed[place_], n + 1)

        consts_ready = sem("consts_ready")
        rot_ready = sem("rot_ready")
        small_in = sem("small_in")
        masks_ready = sem("masks_ready")
        vision_counted = sem("vision_counted")
        w_row_in = sem("w_row_in")
        ctx_in_s = [sem(f"ctx_in{i}") for i in range(4)]
        x_in = [sem(f"x_in{t}") for t in range(T)]
        raw_in = [sem(f"raw_in{i}") for i in range(2)]
        weights_ready = [sem(f"weights_ready{i}") for i in range(2)]
        high_copied = [sem(f"high_copied{i}") for i in range(2)]
        v_raw_in = [sem(f"v_raw_in{e}") for e in range(2)]
        ckv_in = sem("ckv_in")
        ckv_ready = sem("ckv_ready")
        small_w_in = sem("small_w_in")
        small_w_ready = sem("small_w_ready")
        hi_done = sem("hi_done")
        stage_out = [sem(f"stage_out{i}") for i in range(2)]
        v_out = [sem(f"v_out{i}") for i in range(2)]
        squares_done = sem("squares_done")
        rstd_done = sem("rstd_done")
        xs_done = sem("xs_done")
        by_sin_done = sem("by_sin_done")
        rotated = sem("rotated")
        stack_in = [sem(f"stack_in{i}") for i in range(SLOTS)]
        rows_in = [sem(f"rows_in{i}") for i in range(SLOTS)]
        parts_done = sem("parts_done")
        max_row_ready = sem("max_row_ready")
        values_done = sem("values_done")
        pv_copied = sem("pv_copied")
        heads_done = sem("heads_done")
        stack_set = sem("stack_set")
        silu_done = sem("silu_done")
        hid_done = sem("hid_done")
        pool_chain = sem("pool_chain")
        dve_chain = sem("dve_chain")
        lmem_in = sem("lmem_in")
        nmax_done = sem("nmax_done")
        exp_done = sem("exp_done")
        gate_in = sem("gate_in")
        gate_done = sem("gate_done")
        wm_hi_done = sem("wm_hi_done")
        wm_ready = sem("wm_ready")
        mc_in = sem("mc_in")
        mc_hi_done = sem("mc_hi_done")
        mc_ready = sem("mc_ready")
        am_done = sem("am_done")
        fused_done = sem("fused_done")
        row_done = sem("row_done")
        result_out = [sem(f"result_out{i}") for i in range(2)]
        next_zeroed = sem("next_zeroed")

        staged = [("rotT", c, t) for c in ("k", "q") for t in range(T)]
        staged += [("kT", n, m) for n in range(B * M // L) for m in range(KC)]
        staged += [("cqT", b, m) for b in range(B) for m in range(KC)]
        stage_no = {k: i for i, k in enumerate(staged)}
        hi_no = {}
        ff_cuts = [(e, f) for e in range(2) for f in range(len(FS))]
        QKV = ("v", "k", "q")
        CQ_STEPS = [(b + 1) * TB + 2 for b in range(B)]
        uses = [0, 0]
        cut_at = {}
        for c in ["v", "k", "q", "dense"] + ff_cuts:
            s = {"v": 0, "k": 1, "q": 0, "dense": 0}.get(c, None) if isinstance(c, str) else ff_cuts.index(c) % 2
            cut_at[c] = (s, uses[s])
            uses[s] += 1

        raw_count, loaded = {}, [16 * 4, 16 * 2]
        for e, f in ff_cuts:
            loaded[cut_at[(e, f)][0]] += 16 * (4 if FS[f] % P else 3)
            raw_count[(e, f)] = loaded[cut_at[(e, f)][0]]

        def weight_pieces(cut):
            s = cut_at[cut][0]
            if isinstance(cut, str):
                return [(qkv_hi[s][:, e, k, :], qkv_lo[s][:, e, k, :], qkv_raw[s][:, e, k, :])
                        for e in range(2) for k in range(KH)]
            fw = FS[cut[1]]
            a = KH * 2 * fw
            ends = [(P, 0, a // 2), (P, a // 2, a), (P, a, a + fw // P * H)]
            if fw % P:
                ends.append((fw % P, a + fw // P * H, a + (fw // P + 1) * H))
            return [(ff_hi[s][0:n, c0:c1], ff_lo[s][0:n, c0:c1], ff_raw[s][0:n, c0:c1]) for n, c0, c1 in ends]

        pieces, copies = [0, 0], [0, 0]
        split_count, copy_before = {}, {}
        for c in cut_at:
            s, n = cut_at[c][0], len(weight_pieces(c))
            pieces[s] += n
            split_count[c] = pieces[s]
            if c not in ("dense", ff_cuts[0]):
                copy_before[c] = copies[s]
                copies[s] += n

        def wait_weights(eng, cut, later=0):
            eng.wait_ge(weights_ready[cut_at[cut][0]], split_count[cut] - later)

        self_steps = attention_steps(TB)
        cross_steps = attention_steps(MT)

        def three(pe, acc, stat, mov, first, last):
            s_hi, s_lo = stat
            m_hi, m_lo = mov
            pe.matmul(acc, s_hi, m_hi, start=first, stop=False)
            pe.matmul(acc, s_hi, m_lo, start=False, stop=False)
            return pe.matmul(acc, s_lo, m_hi, start=False, stop=last)

        def load_counts(eng):
            return [eng.value_load(vision_count[0:1, t:t + 1], min_val=0, max_val=P) for t in range(T)]

        def fill_skipped(pe, product):
            pe.sem_inc(bank_filled[filled_as[product][0]], 1)

        def free_skipped(eng, product):
            eng.sem_inc(bank_freed[filled_as[product][0]], 1)

        def both(hi, lo, *key):
            return hi[key], lo[key]

        block = ctx.enter_context(nc.Block())

        @block.tensor
        def _(pe):
            pe.wait_ge(consts_ready, 1)
            def turn_act(stage, t):
                pe.wait_ge(xs_done, turn_no[(stage, t)] + 1)
                acc = claim(pe, ("actT", stage, t), t % 2)
                for k in range(KH):
                    mm = pe.transpose(acc[:, k * P:(k + 1) * P], xs[:, t % 2, k * P:(k + 1) * P], ident[:, :])
                fill_done(mm, ("actT", stage, t))

            pe.wait_ge(consts_ready, 3)
            pe.wait_ge(masks_ready, 1)
            acc = claim(pe, ("vision_count",), A0)
            fill_done(pe.matmul(acc[0:1, 0:T], minus_half[:, :], is_v[:, :], start=True, stop=True), ("vision_count",))
            wait_emptied(pe, ("vision_count",))
            vision = load_counts(pe)
            for t in range(T):
                turn_act("in", t)

            def turn_rotated(c, t):
                pe.wait_ge(rotated, {"k": 0, "q": T}[c] + t + 1)
                acc = claim(pe, ("rotT", c, t), t % 2)
                for k in range(KH):
                    mm = pe.transpose(acc[:, k * P:(k + 1) * P], by_cos[:, t % 2, k * P:(k + 1) * P], ident[:, :])
                fill_done(mm, ("rotT", c, t))

            def expert_product(product, t, e, s):
                acc = claim(pe, product, (A0, A1)[e])

                def multiply():
                    for k in range(KH):
                        mm = three(pe, acc[:, :], both(actT_hi, actT_lo, slice(None), k, slice(t * P, (t + 1) * P)),
                                   both(qkv_hi[s], qkv_lo[s], slice(None), e, k, slice(None)), k == 0, k == KH - 1)
                    fill_done(mm, product)

                if e == 0:
                    multiply()
                else:
                    with pe.If(vision[t] > 0):
                        multiply()
                    with pe.Else():
                        fill_skipped(pe, product)

            for c in QKV:
                s = cut_at[c][0]
                for t in range(T):
                    if c == "v":
                        wait_emptied(pe, ("actT", "in", t))
                    for e in range(2):
                        if t == 0:
                            wait_weights(pe, c, KH * (1 - e))
                        expert_product(("qkv", c, t, e), t, e, s)
                    if c != "v" and t >= 1:
                        turn_rotated(c, t - 1)
                if c != "v":
                    turn_rotated(c, T - 1)

            for u in range(B * MT):
                pe.wait_ge(ctx_in_s[u // 4], 16)
                acc = claim(pe, ("ctxT", u), u % 2)
                for k in range(KC):
                    mm = pe.transpose(acc[:, k * P:(k + 1) * P], ctx_tile[:, u, k * P:(k + 1) * P], ident[:, :])
                fill_done(mm, ("ctxT", u))
            pe.wait_ge(ckv_ready, 1)
            for n in range(B * M // L):
                for u in range(4 * n + 2, 4 * n + 4):
                    wait_emptied(pe, ("ctxT", u))
                for m in range(KC):
                    acc = claim(pe, ("kT", n, m), (A0, A1)[m])
                    for k in range(KC):
                        mm = three(pe, acc[:, :], both(ckv_hi, ckv_lo, slice(None), k, slice(m * P, (m + 1) * P)),
                                   both(ctxT_hi, ctxT_lo, slice(None), k, slice(n * L, (n + 1) * L)), k == 0, k == KC - 1)
                    fill_done(mm, ("kT", n, m))
            for u in range(B * MT):
                acc = claim(pe, ("cv", u), (PR0, PR1)[u % 2])
                for k in range(KC):
                    mm = three(pe, acc[:, 0, 0:C], both(ctxT_hi, ctxT_lo, slice(None), k, slice(u * P, (u + 1) * P)),
                               both(ckv_hi, ckv_lo, slice(None), k, slice(C, 2 * C)), k == 0, k == KC - 1)
                fill_done(mm, ("cv", u))

            work = [0]

            def work_bank():
                work[0] += 1
                return work[0] % 2

            def attend(kind, steps, per_unit, uses_before):
                causal = kind == "self"
                for todo in steps:
                    for what, u, r in todo:
                        slot, use = u % SLOTS, u // SLOTS + uses_before
                        qs, ks = q_st[slot], k_st[slot]
                        if what == "scores":
                            if r == 0:
                                pe.wait_ge(stack_in[slot], 16 * 7 * (use + 1))
                                if u < SLOTS:
                                    pe.wait_ge(stack_set, (0 if causal else SLOTS) + slot + 1)
                            for n in (2 * r, 2 * r + 1):
                                if causal:
                                    j, i = divmod(n, TB)
                                    product = (kind, "S", u, j, i)
                                    acc = claim(pe, product, work_bank())
                                    width = max(256, (i + 1) * P)
                                    pe.matmul(acc[:, 0:width], qs[0:ONES, j, i * P:(i + 1) * P], ks[0:ONES, j, 0:width],
                                              start=True, stop=True)
                                    mm = pe.matmul(acc[:, i * P:(i + 1) * P], ident_bf[:, :], hide_s[:, :],
                                                   start=False, stop=True, skip_group_check=True)
                                else:
                                    j, i, h = n // (2 * TB), n // 2 % TB, n % 2
                                    product = (kind, "S", u, j, i, h)
                                    acc = claim(pe, product, work_bank())
                                    mm = pe.matmul(acc[:, :], qs[0:ONES, j, i * P:(i + 1) * P],
                                                   ks[0:ONES, j, h * L:(h + 1) * L], start=True, stop=True)
                                fill_done(mm, product)
                        elif what == "max_rows":
                            pe.wait_ge(parts_done, u + 1 + (0 if causal else UNITS))
                            product = (kind, "max_rows", u)
                            acc = claim(pe, product, work_bank())
                            for i in range(TB):
                                mm = pe.transpose(acc[0:4, i * P:(i + 1) * P], max_parts[:, u % 2, i, :].bitcast(F32), ident[:, :])
                            fill_done(mm, product)
                        elif what == "probs":
                            if r == 0:
                                pe.wait_ge(rows_in[slot], 16 * 2 * (use + 1))
                            product = (kind, "T", u, r)
                            acc = claim(pe, product, (PR0, PR1)[(u * per_unit + r) % 2])
                            for j in range(2):
                                first = min(r * P, L - 256) if causal else 0
                                mm = pe.matmul(acc[:, j, first:L], ks[0:ONES + 2, j, r * P:(r + 1) * P],
                                               qs[0:ONES + 2, j, first:L], start=True, stop=True)
                                if causal:
                                    mm = pe.matmul(acc[:, j, r * P:(r + 1) * P], ident_bf[:, :], hide_t[:, :],
                                                   start=False, stop=True, skip_group_check=True)
                            fill_done(mm, product)
                        elif what == "values":
                            product = (kind, "PV", u)
                            if r == 0:
                                acc = claim(pe, product, (A0, A1)[u % 2])
                            acc = banks[(A0, A1)[u % 2]]
                            wait_emptied(pe, (kind, "T", u, r))
                            n = u * per_unit + r
                            if causal:
                                for j in range(2):
                                    mm = pe.matmul(acc[j * 64:(j + 1) * 64, r * P:L],
                                                   v_st[slot][:, (2 * r + j) * 64:(2 * r + j + 1) * 64],
                                                   probs[:, n % 4, j, r * P:L], start=(r == 0), stop=(r == per_unit - 1))
                            elif r % 2:
                                for j in range(2):
                                    for h in range(2):
                                        mm = pe.matmul(acc[(2 * j + h) * 32:(2 * j + h + 1) * 32, :],
                                                       v_st[slot][:, (2 * (r - 1 + h) + j) * 32:(2 * (r - 1 + h) + j + 1) * 32],
                                                       probs[:, (n - 1 + h) % 4, j, :], start=(r == 1), stop=(r == per_unit - 1))
                            if r == per_unit - 1:
                                fill_done(mm, product)
                            elif causal or r % 2:
                                mm.then_inc(values_done, 1)
                        elif what == "turn_back":
                            pe.wait_ge(pv_copied, u + 1 + (0 if causal else UNITS))
                            product = (kind, "PVT", u)
                            acc = claim(pe, product, work_bank())
                            for i in range(TB):
                                mm = pe.transpose(acc[:, i * P:(i + 1) * P], pv_out[:, u % 2, i * P:(i + 1) * P], ident[:, :])
                            fill_done(mm, product)
                        elif what == "context":
                            src, nk = (heads_out, KH) if causal else (cheads_out, KC)
                            pe.wait_ge(heads_done, (u + 1) * PAIRS + (0 if causal else UNITS))
                            for i in range(TB):
                                product = (kind, "ctxT", u, i)
                                acc = claim(pe, product, work_bank())
                                for k in range(nk):
                                    mm = pe.transpose(acc[:, k * P:(k + 1) * P], src[:, i, k * P:(k + 1) * P], ident[:, :])
                                fill_done(mm, product)

            attend("self", self_steps, TB, 0)

            wait_weights(pe, "dense")
            s = cut_at["dense"][0]
            for n in range(T + 3):
                if n < T:
                    wait_emptied(pe, ("self", "ctxT", n // TB, n % TB))
                    for e in range(2):
                        expert_product(("dense", n, e), n, e, s)
                if 2 <= n < T + 2:
                    turn_act("cross", n - 2)
                if n in CQ_STEPS:
                    b = CQ_STEPS.index(n)
                    pe.wait_ge(small_w_ready, 1)
                    for t in range((b + 1) * TB - 2, (b + 1) * TB):
                        wait_emptied(pe, ("actT", "cross", t))
                    for m in range(KC):
                        acc = claim(pe, ("cqT", b, m), (PR0, PR1)[m])
                        for k in range(KH):
                            mm = three(pe, acc[:, 0, :], both(cq_hi, cq_lo, slice(None), k, slice(m * P, (m + 1) * P)),
                                       both(actT_hi, actT_lo, slice(None), k, slice(b * L, (b + 1) * L)), k == 0, k == KH - 1)
                        fill_done(mm, ("cqT", b, m))

            attend("cross", cross_steps, MT, UNITS // SLOTS)

            pe.wait_ge(small_w_ready, 2)
            for n in range(T + 2):
                if n < T:
                    wait_emptied(pe, ("cross", "ctxT", n // TB, n % TB))
                    acc = claim(pe, ("cdense", n), (A0, A1)[n % 2])
                    for k in range(KC):
                        mm = three(pe, acc[:, :], both(actT_hi, actT_lo, slice(None), k, slice(n * P, (n + 1) * P)),
                                   both(cd_hi, cd_lo, slice(None), k, slice(None)), k == 0, k == KC - 1)
                    fill_done(mm, ("cdense", n))
                if n >= 2:
                    turn_act("mlp", n - 2)

            def gate_up(product, acc, e, f, t):
                fw, s = FS[f], cut_at[(e, f)][0]
                parts = [(acc[:, 0, 0:fw], 0, fw), (acc[:, 1, 0:fw], fw, fw)] if fw >= 256 else [(acc[:, 0, 0:2 * fw], 0, 2 * fw)]
                for dst, c0, w in parts:
                    for k in range(KH):
                        cols = slice(k * 2 * fw + c0, k * 2 * fw + c0 + w)
                        mm = three(pe, dst, both(actT_hi, actT_lo, slice(None), k, slice(t * P, (t + 1) * P)),
                                   both(ff_hi[s], ff_lo[s], slice(None), cols), k == 0, k == KH - 1)
                fill_done(mm, product)

            def turn_hid(product, acc, f, slot):
                for k in range((FS[f] + P - 1) // P):
                    w = min(P, FS[f] - k * P)
                    mm = pe.transpose(acc[0:w, k * P:(k + 1) * P], hid[:, slot, k * P:k * P + w], ident[:, :])
                fill_done(mm, product)

            def down(product, acc, e, f, slot):
                s = cut_at[(e, f)][0]
                nk = (FS[f] + P - 1) // P
                for k in range(nk):
                    w = min(P, FS[f] - k * P)
                    cols = slice(KH * 2 * FS[f] + k * H, KH * 2 * FS[f] + (k + 1) * H)
                    mm = three(pe, acc[:, :], (hidT_hi[0:w, slot, k, :], hidT_lo[0:w, slot, k, :]),
                               (ff_hi[s][0:w, cols], ff_lo[s][0:w, cols]), k == 0, k == nk - 1)
                fill_done(mm, product)

            items = [(e, f, t) for e, f in ff_cuts for t in range(T)]
            for n in range(len(items) + 2):
                if n < len(items):
                    e, f, t = items[n]
                    if t == 0:
                        wait_weights(pe, (e, f))
                    if e == 0 and f == 0:
                        wait_emptied(pe, ("actT", "mlp", t))
                    product = ("gu", e, f, t)
                    acc = claim(pe, product, (PR0, PR1)[n % 2])
                    if e == 0:
                        gate_up(product, acc, e, f, t)
                    else:
                        with pe.If(vision[t] > 0):
                            gate_up(product, acc, e, f, t)
                        with pe.Else():
                            fill_skipped(pe, product)
                if 1 <= n <= len(items):
                    e, f, t = items[n - 1]
                    pe.wait_ge(hid_done, n)
                    product = ("hidT", e, f, t)
                    acc = claim(pe, product, n % 2)
                    if e == 0:
                        turn_hid(product, acc, f, (n - 1) % 2)
                    else:
                        with pe.If(vision[t] > 0):
                            turn_hid(product, acc, f, (n - 1) % 2)
                        with pe.Else():
                            fill_skipped(pe, product)
                if n >= 2:
                    e, f, t = items[n - 2]
                    product = ("down", e, f, t)
                    wait_emptied(pe, ("hidT", e, f, t))
                    acc = claim(pe, product, (A0, A1)[n % 2])
                    if e == 0:
                        down(product, acc, e, f, n % 2)
                    else:
                        with pe.If(vision[t] > 0):
                            down(product, acc, e, f, n % 2)
                        with pe.Else():
                            fill_skipped(pe, product)

            pe.wait_ge(lmem_in, 32)
            for g in range(KC + 2 * KH):
                product = ("wT", g)
                acc = claim(pe, product, g % 2)
                src, k = (wm_raw, g) if g < KC else (wg_raw, g - KC)
                for d in range(KH):
                    mm = pe.transpose(acc[:, d * P:(d + 1) * P], src[:, d, k * P:(k + 1) * P], ident[:, :])
                fill_done(mm, product)
            for t in range(T):
                wait_emptied(pe, ("down", 1, len(FS) - 1, t))
                acc = claim(pe, ("hsT", t), t % 2)
                for k in range(KH):
                    mm = pe.transpose(acc[:, k * P:(k + 1) * P], hs[:, t, k * P:(k + 1) * P], ident[:, :])
                fill_done(mm, ("hsT", t))
            pe.wait_ge(wm_ready, 1)
            for g in range(KC + 2 * KH - 2, KC + 2 * KH):
                wait_emptied(pe, ("wT", g))
            for m in range(KC):
                acc = claim(pe, ("G", m), (A0, A1)[m])
                for k in range(KH):
                    mm = three(pe, acc[:, :], both(wm_hi, wm_lo, slice(None), k, slice(m * P, (m + 1) * P)),
                               both(wgT_hi, wgT_lo, slice(None), KH + k, slice(None)), k == 0, k == KH - 1)
                fill_done(mm, ("G", m))
            for b in range(B):
                for t in range((b + 1) * TB - 2, (b + 1) * TB):
                    wait_emptied(pe, ("hsT", t))
                for m in range(KC):
                    acc = claim(pe, ("qm", b, m), (PR0, PR1)[m])
                    for k in range(KH):
                        mm = three(pe, acc[:, 0, :], both(wm_hi, wm_lo, slice(None), k, slice(m * P, (m + 1) * P)),
                                   both(actT_hi, actT_lo, slice(None), k, slice(b * L, (b + 1) * L)), k == 0, k == KH - 1)
                    fill_done(mm, ("qm", b, m))
            def turn_context(b):
                pe.wait_ge(mc_in, 16 * (b + 1))
                for g in range(TB):
                    product = ("mcT", b, g)
                    acc = claim(pe, product, (W0, W1)[g % 2])
                    for k in range(KC):
                        for u in range(2):
                            mm = pe.transpose(acc[:, (2 * k + u) * P:(2 * k + u + 1) * P],
                                              mc_raw[:, 2 * g + u, k * P:(k + 1) * P], ident[:, :])
                    fill_done(mm, product)

            turn_context(0)
            for n in range(T + 2):
                if n < T:
                    b = n // TB
                    if n % TB == 0:
                        for m in range(KC):
                            wait_emptied(pe, ("qm", b, m))
                        for g in range(TB - 2, TB):
                            wait_emptied(pe, ("mcT", b, g))
                    acc = claim(pe, ("ms", n), (PR0, PR1)[n % 2])
                    for h in range(M // L):
                        c0 = b * M + h * L
                        for k in range(KC):
                            mm = three(pe, acc[:, h, :], both(qm_hi, qm_lo, slice(None), k, slice(n * P, (n + 1) * P)),
                                       both(mcT_hi, mcT_lo, slice(None), k, slice(c0, c0 + L)), k == 0, k == KC - 1)
                    fill_done(mm, ("ms", n))
                if n >= 2:
                    pe.wait_ge(am_done, n - 1)
                    acc = claim(pe, ("amT", n - 2), W0)
                    for k in range(KC):
                        mm = pe.transpose(acc[:, k * P:(k + 1) * P], am[:, k * P:(k + 1) * P], ident[:, :])
                    fill_done(mm, ("amT", n - 2))
                if 1 <= n <= T:
                    t = n - 1
                    pe.wait_ge(exp_done, t + 1)
                    for h in range(2):
                        acc = claim(pe, ("attnT", t, h), (W1, W0)[h])
                        for k in range(4):
                            m = 4 * h + k
                            mm = pe.transpose(acc[:, k * P:(k + 1) * P], attn[:, t % 2, m * P:(m + 1) * P], ident[:, :])
                        fill_done(mm, ("attnT", t, h))
                if n >= 2:
                    t = n - 2
                    wait_emptied(pe, ("amT", t))
                    if n == 2:
                        for m in range(KC):
                            wait_emptied(pe, ("G", m))
                    acc = banks[A1]
                    for k in range(KC):
                        mm = three(pe, acc[:, :], both(amT_hi, amT_lo, slice(None), k, slice(None)),
                                   both(G_hi, G_lo, slice(None), k, slice(None)), False, k == KC - 1)
                    fill_done(mm, ("gate", t))
                    acc = claim(pe, ("mctx", t), W1)
                    for k in range(KC):
                        mm = three(pe, acc[:, :], both(amT_hi, amT_lo, slice(None), k, slice(None)),
                                   both(wmT_hi, wmT_lo, slice(None), k, slice(None)), k == 0, k == KC - 1)
                    fill_done(mm, ("mctx", t))
                if 1 <= n <= T:
                    t = n - 1
                    acc = claim(pe, ("gate", t), A1)
                    for k in range(KH):
                        three(pe, acc[:, :], both(actT_hi, actT_lo, slice(None), k, slice(t * P, (t + 1) * P)),
                              both(wgT_hi, wgT_lo, slice(None), k, slice(None)), k == 0, False)
                    pe.wait_ge(mc_ready, t // TB + 1)
                    acc = claim(pe, ("am", t), A0)
                    for m in range(MT):
                        if m % 4 == 0:
                            wait_emptied(pe, ("attnT", t, m // 4))
                        mm = three(pe, acc[:, 0:C], both(attnT_hi, attnT_lo, slice(None), m, slice(None)),
                                   both(mc_hi, mc_lo, slice(None), m, slice(None)), m == 0, m == MT - 1)
                    fill_done(mm, ("am", t))
                if n == TB - 2:
                    turn_context(1)

        @block.scalar
        def _(act):
            def hi_part(product, dst, src_of):
                acc = wait_filled(act, product)
                hi_no[product] = len(hi_no) + 1
                act.activation(dst, src_of(acc), ACT.Copy).then_inc(hi_done, 1)

            def tiles(acc, n=KH):
                return acc[:, 0:n * P].rearrange("p (k t) -> p k t", k=n)

            def staged_hi(product, src_of=lambda a: a[:, :]):
                z = stage_no[product]
                if z >= 2:
                    act.wait_ge(stage_out[z % 2], 32 * (z // 2))
                hi_part(product, stage_hi[:, z % 2, :], src_of)

            def squares(stage, t, product):
                if product is None:
                    act.wait_ge(x_in[t], 16)
                else:
                    wait_emptied(act, product)
                before = NORMS.index(stage) * T + t
                if before:
                    act.wait_ge(squares_done, before)
                act.activation(square_out[:, :], hs[:, t, :], ACT.Square,
                               accum_out=sum_sq[:, NORMS.index(stage), t:t + 1]).then_inc(squares_done, 1)

            def act_hi(product, t, n=KH):
                hi_part(product, actT_hi[:, 0:n, t * P:(t + 1) * P], lambda a: tiles(a, n))

            def copy_high(cut, i=None):
                s = cut_at[cut][0]
                for hi, lo, raw in weight_pieces(cut)[slice(None) if i is None else slice(i, i + 1)]:
                    act.activation(hi, raw, ACT.Copy).then_inc(high_copied[s], 1)

            for e in range(2):
                for t in range(e * TB, (e + 1) * TB):
                    squares("in", t, None)
                act.wait_ge(v_raw_in[e], 16)
                for k in range(KH):
                    copy_high("v", e * KH + k)
            for t in range(T):
                act_hi(("actT", "in", t), t)
            act.wait_ge(raw_in[1], 32)
            copy_high("k")
            for c in ("k", "q"):
                for t in range(T):
                    if c == "k" and t < 4:
                        if t == 0:
                            wait_used(act, ("qkv", "v", T - 1, 0), ("qkv", "v", T - 1, 1))
                            act.wait_ge(raw_in[0], 32)
                        copy_high("q", 2 * t)
                        copy_high("q", 2 * t + 1)
                    staged_hi(("rotT", c, t))
            for u in range(B * MT):
                hi_part(("ctxT", u), ctxT_hi[:, :, u * P:(u + 1) * P], lambda a: tiles(a, KC))
            for n in range(B * M // L):
                for m in range(KC):
                    staged_hi(("kT", n, m))

            def attend(kind, steps, per_unit, uses_before):
                causal = kind == "self"
                scale = 1.0 / np.sqrt(HD if causal else CHD)
                for todo in steps:
                    for what, u, r in todo:
                        slot = u % SLOTS
                        if what == "max_rows":
                            acc = wait_filled(act, (kind, "max_rows", u))
                            v = u + (0 if causal else UNITS)
                            if v == 0:
                                for i in range(2):
                                    act.wait_ge(stage_out[i], 32 * ((stage_no[("kT", B * M // L - 1, KC - 1)] + 1) // 2))
                            if v == UNITS:
                                act.wait_ge(stage_out[0], 32 * (len(staged) // 2))
                                act.wait_ge(stage_out[1], 32 * (len(staged) // 2))
                            if v >= 2:
                                act.wait_ge(rows_in[(v - 2) % SLOTS], 32 * ((v - 2) // SLOTS + 1))
                            ins = act.activation(stage_hi[0:4, v % 2, :], acc[0:4, :], ACT.Copy)
                            free(ins, (kind, "max_rows", u))
                            wait_emptied(act, (kind, "max_rows", u))
                            for part in range(2):
                                act.dma_start(raw32(q_st[slot][ONES + part:ONES + part + 1, :, :]),
                                              raw32(stage_hi[2 * part:2 * part + 2, v % 2, :])).then_inc(rows_in[slot], 16)
                        elif what == "probs":
                            n = u * per_unit + r
                            acc = wait_filled(act, (kind, "T", u, r))
                            if n >= 4:
                                lu, lr = divmod(n - 4, per_unit)
                                lr = lr if causal else lr // 2
                                if lr == 3:
                                    wait_filled(act, (kind, "PV", lu))
                                else:
                                    act.wait_ge(values_done, 3 * (lu + (0 if causal else UNITS)) + lr + 1)
                            first = r * P if causal else 0
                            free(act.activation(probs[:, n % 4, :, first:L], acc[:, :, first:L], ACT.Exp, scale=scale),
                                 (kind, "T", u, r))
                        elif what == "context":
                            for i in range(TB):
                                act_hi((kind, "ctxT", u, i), u * TB + i, KH if causal else KC)

            attend("self", self_steps, TB, 0)
            for n in range(T + 3):
                if n < T:
                    squares("cross", n, ("dense", n, 1))
                if 2 <= n < T + 2:
                    act_hi(("actT", "cross", n - 2), n - 2)
                if n in CQ_STEPS:
                    b = CQ_STEPS.index(n)
                    if b == 0:
                        for v in (UNITS - 2, UNITS - 1):
                            act.wait_ge(rows_in[v % SLOTS], 32 * (v // SLOTS + 1))
                    for m in range(KC):
                        staged_hi(("cqT", b, m), lambda a: a[:, 0, :])
            attend("cross", cross_steps, MT, UNITS // SLOTS)
            for n in range(T + 2):
                if n < T:
                    squares("mlp", n, ("cdense", n))
                if n >= 2:
                    act_hi(("actT", "mlp", n - 2), n - 2)

            vision = load_counts(act)
            items = [(e, f, t) for e, f in ff_cuts for t in range(T)]
            for n in range(len(items) + 1):
                if n < len(items):
                    e, f, t = items[n]
                    acc = wait_filled(act, ("gu", e, f, t))
                    if n >= 2:
                        act.wait_ge(hid_done, n - 1)
                    def silu():
                        act.activation(silu_g[:, n % 2, 0:FS[f]], acc[:, 0, 0:FS[f]], ACT.Silu).then_inc(silu_done, 1)

                    if e == 0:
                        silu()
                    else:
                        with act.If(vision[t] > 0):
                            silu()
                        with act.Else():
                            act.wait_ge(silu_done, n)
                            act.sem_inc(silu_done, 1)
                if n >= 1:
                    e, f, t = items[n - 1]
                    product = ("hidT", e, f, t)
                    if n >= 3:
                        e0, f0, t0 = items[n - 3]
                        wait_filled(act, ("down", e0, f0, t0))
                    acc = wait_filled(act, product)
                    nk = (FS[f] + P - 1) // P
                    hi_no[product] = len(hi_no) + 1
                    full = FS[f] // P

                    def hid_hi():
                        ins = act.activation(hidT_hi[:, (n - 1) % 2, 0:full, :], tiles(acc, full), ACT.Copy)
                        if nk > full:
                            w = FS[f] - full * P
                            ins = act.activation(hidT_hi[0:w, (n - 1) % 2, full, :], acc[0:w, full * P:(full + 1) * P], ACT.Copy)
                        ins.then_inc(hi_done, 1)

                    if e == 0:
                        hid_hi()
                    else:
                        with act.If(vision[t] > 0):
                            hid_hi()
                        with act.Else():
                            act.wait_ge(hi_done, hi_no[product] - 1)
                            act.sem_inc(hi_done, 1)
                if n < len(items):
                    c, t = divmod(n, T)
                    if c + 1 < len(ff_cuts):
                        nxt = ff_cuts[c + 1]
                        if t == 2:
                            act.wait_ge(raw_in[cut_at[nxt][0]], raw_count[nxt])
                            if c == 0:
                                wait_filled(act, ("cross", "PV", UNITS - 1))
                            else:
                                wait_used(act, ("down", *ff_cuts[c - 1], T - 2), ("down", *ff_cuts[c - 1], T - 1))
                        if 2 <= t < 2 + len(weight_pieces(nxt)):
                            copy_high(nxt, t - 2)

            for g in range(KC + 2 * KH):
                dst = wmT_hi[:, g, :] if g < KC else wgT_hi[:, g - KC, :]
                hi_part(("wT", g), dst, lambda a: a[:, :])
            act.activation(wm_hi[:, :, :], wm_raw[:, :, :], ACT.Copy).then_inc(wm_hi_done, 1)
            for t in range(T):
                act_hi(("hsT", t), t)
            for m in range(KC):
                hi_part(("G", m), G_hi[:, m, :], lambda a: a[:, :])
            for m in range(KC):
                wait_filled(act, ("G", m))
            for b in range(B):
                for m in range(KC):
                    hi_part(("qm", b, m), qm_hi[:, m, b * L:(b + 1) * L], lambda a: a[:, 0, :])

            def context_hi(b):
                act.wait_ge(mc_in, 16 * (b + 1))
                if b:
                    wait_filled(act, ("am", b * TB - 1))
                act.activation(mc_hi[:, :, :], mc_raw[:, :, :], ACT.Copy).then_inc(mc_hi_done, 1)

            def turned_context(b):
                for g in range(TB):
                    cols = slice((b * MT + 2 * g) * P, (b * MT + 2 * g + 2) * P)
                    hi_part(("mcT", b, g), mcT_hi[:, :, cols], lambda a: a[:, :].rearrange("p (k t) -> p k t", k=KC))

            turned_context(0)
            context_hi(0)
            for n in range(T + 2):
                if n >= 2:
                    hi_part(("amT", n - 2), amT_hi[:, :, :], lambda a: tiles(a, KC))
                if 1 <= n <= T:
                    for h in range(2):
                        hi_part(("attnT", n - 1, h), attnT_hi[:, 4 * h:4 * h + 4, :], lambda a: tiles(a, 4))
                if n < T:
                    acc = wait_filled(act, ("ms", n))
                    act.wait_ge(nmax_done, n + 1)
                    if n >= 2:
                        wait_filled(act, ("attnT", n - 2, 1))
                    act.activation(attn[:, n % 2, :], acc[:, :, :].rearrange("p a b -> p (a b)"), ACT.Exp,
                                   bias=den[:, 0, n:n + 1], scale=1.0 / np.sqrt(H), accum_out=den[:, 1, n:n + 1])\
                       .then_inc(exp_done, 1)
                if n >= 2:
                    t = n - 2
                    act.wait_ge(gate_in, t + 1)
                    act.activation(stage1[:, :], stage0[:, :], ACT.Tanh, scale=0.5).then_inc(gate_done, 1)
                    act.wait_ge(fused_done, t + 1)
                    act.wait_ge(squares_done, 3 * T + t)
                    act.activation(square_out[:, :], xs[:, t % 2, :], ACT.Square,
                                   accum_out=sum_sq[:, 3, t:t + 1]).then_inc(squares_done, 1)
                if n == TB - 2:
                    turned_context(1)
                if n == TB:
                    context_hi(1)

        @block.vector
        def _(dve):
            chain = [0]

            def link(ins):
                chain[0] += 1
                ins.then_inc(dve_chain, 1)
                dve.wait_ge(dve_chain, chain[0])

            def tiles(acc, n=KH):
                return acc[:, 0:n * P].rearrange("p (k t) -> p k t", k=n)

            def lo_part(product, dst, hi, src_of):
                dve.wait_ge(hi_done, hi_no[product])
                acc = banks[filled_as[product][0]]
                free(dve.tensor_tensor(dst, src_of(acc), hi.bitcast(F32), ALU.subtract), product)

            def staged_lo(product, src_of=lambda a: a[:, :]):
                z = stage_no[product]
                lo_part(product, stage_lo[:, z % 2, :], stage_hi[:, z % 2, :], src_of)

            def act_lo(product, t, n=KH):
                cols = slice(t * P, (t + 1) * P)
                lo_part(product, actT_lo[:, 0:n, cols], actT_hi[:, 0:n, cols], lambda a: tiles(a, n))

            def normed(stage, t):
                no = turn_no[(stage, t)]
                dve.wait_ge(rstd_done, no + 1)
                if no >= 2:
                    wait_filled(dve, ("actT", *TURNS[no - 2]))
                dve.scalar_tensor_tensor(out=xs[:, t % 2, :], in0=hs[:, t, :],
                                         scalar=rstd[:, NORMS.index(stage), t:t + 1], in1=w_row[:, :],
                                         op0=ALU.mult, op1=ALU.mult).then_inc(xs_done, 1)

            dve.wait_ge(small_in, SMALL)
            link(dve.tensor_scalar(eq_tmp[:, :], tt_next[:, :], 1.0, None, ALU.is_equal))
            link(dve.tensor_scalar(is_l[:, :], tt_now[:, :], 1.0, None, ALU.is_equal))
            link(dve.tensor_tensor(is_v[:, :], is_l[:, :], eq_tmp[:, :], ALU.mult))
            dve.tensor_scalar(is_l[:, :], is_v[:, :], -1.0, 1.0, ALU.mult, ALU.add).then_inc(masks_ready, 1)
            dve.wait_ge(masks_ready, 1)
            masks = [is_l, is_v]
            acc = wait_filled(dve, ("vision_count",))
            free(dve.tensor_scalar(vision_count[:, :], acc[0:1, 0:T], -2.0, None, ALU.mult), ("vision_count",))
            wait_emptied(dve, ("vision_count",))
            vision = load_counts(dve)

            dve.wait_ge(w_row_in, 16)
            for t in range(T):
                normed("in", t)
                if t >= 1:
                    act_lo(("actT", "in", t - 1), t - 1)
            act_lo(("actT", "in", T - 1), T - 1)

            def add_expert(product, t, e):
                acc = wait_filled(dve, product)

                def add():
                    free(dve.scalar_tensor_tensor(out=hs[:, t, :], in0=acc[:, :], scalar=masks[e][:, t:t + 1],
                                                  in1=hs[:, t, :], op0=ALU.mult, op1=ALU.add), product)

                if e == 0:
                    add()
                else:
                    with dve.If(vision[t] > 0):
                        add()
                    with dve.Else():
                        free_skipped(dve, product)

            done_mix = 0
            for ci, c in enumerate(QKV):
                for t in range(T):
                    for e in range(2):
                        acc = wait_filled(dve, ("qkv", c, t, e))
                        if c == "v":
                            if e == 0 and t >= 2:
                                dve.wait_ge(v_out[t % 2], 16 * (t // 2))
                            if e == 0 and t < 2:
                                dve.wait_ge(consts_ready, 4)
                            dst = v_tile[:, t % 2, :, 0:HD]
                            src = acc[:, :].rearrange("p (h d) -> p h d", h=NH)
                        else:
                            dst, src = mixed[:, t % 2, :], acc[:, :]
                            if e == 0 and done_mix >= 2:
                                dve.wait_ge(by_sin_done, done_mix - 1)
                        if e == 0:
                            ins = dve.tensor_scalar(dst, src, masks[0][:, t:t + 1], None, ALU.mult)
                            free(ins, ("qkv", c, t, e))
                            wait_emptied(dve, ("qkv", c, t, e))
                        else:
                            with dve.If(vision[t] > 0):
                                ins = dve.scalar_tensor_tensor(out=dst, in0=src, scalar=masks[1][:, t:t + 1], in1=dst,
                                                               op0=ALU.mult, op1=ALU.add)
                                free(ins, ("qkv", c, t, e))
                                wait_emptied(dve, ("qkv", c, t, e))
                            with dve.Else():
                                free_skipped(dve, ("qkv", c, t, e))
                    if c == "v":
                        continue
                    if c == "k" and t == 0:
                        dve.wait_ge(rot_ready, 16 * TB)
                    done_mix += 1
                    if done_mix >= 3:
                        z = done_mix - 3
                        wait_filled(dve, ("rotT", "kq"[z // T], z % T))
                    heads = mixed[:, t % 2, :].rearrange("p (a d) -> p a d", d=HD // 2)
                    link(dve.tensor_tensor(by_cos[:, t % 2, :].rearrange("p (a d) -> p a d", d=HD // 2), heads,
                                           rot[:, t % TB, 0:HD // 2].unsqueeze(1).to_broadcast([P, 2 * NH, HD // 2]), ALU.mult))
                    dve.wait_ge(by_sin_done, done_mix)
                    dve.tensor_tensor(by_cos[:, t % 2, :], by_cos[:, t % 2, :], by_sin[:, t % 2, :], ALU.add).then_inc(rotated, 1)
                    if t >= 1:
                        staged_lo(("rotT", c, t - 1))
                if c != "v":
                    staged_lo(("rotT", c, T - 1))
            for u in range(B * MT):
                lo_part(("ctxT", u), ctxT_lo[:, :, u * P:(u + 1) * P], ctxT_hi[:, :, u * P:(u + 1) * P],
                        lambda a: tiles(a, KC))
            for n in range(B * M // L):
                for m in range(KC):
                    staged_lo(("kT", n, m))
            dve.wait_ge(consts_ready, 2)
            for u in range(B * MT):
                acc = wait_filled(dve, ("cv", u))
                if u >= 4 and u % 2 == 0:
                    dve.wait_ge(v_out[u // 2 % 2], 16 * (T // 2 + u // 4))
                free(dve.tensor_copy(cv_tile[:, u % 4, :, 0:CHD], acc[:, 0, 0:C].rearrange("p (h d) -> p h d", h=NH)),
                     ("cv", u))

            def attend(kind, steps, per_unit):
                causal = kind == "self"
                before = 0 if causal else UNITS
                for todo in steps:
                    for what, u, r in todo:
                        if what == "scores":
                            for n in (2 * r, 2 * r + 1):
                                if causal:
                                    j, i = divmod(n, TB)
                                    product = (kind, "S", u, j, i)
                                    acc = wait_filled(dve, product)
                                    if n == 0 and u + before >= 2:
                                        dve.wait_ge(parts_done, u + before - 1)
                                    free(dve.tensor_reduce(row_max[:, u % 2, i, j:j + 1], acc[:, 0:(i + 1) * P], AX, ALU.max,
                                                           negate=True), product)
                                else:
                                    j, i, h = n // (2 * TB), n // 2 % TB, n % 2
                                    product = (kind, "S", u, j, i, h)
                                    acc = wait_filled(dve, product)
                                    dst = half_max[:, u % 2, h, i, j:j + 1]
                                    free(dve.tensor_reduce(dst, acc[:, :], AX, ALU.max, negate=True), product)
                        elif what == "max_parts":
                            if causal:
                                lasts = [(kind, "S", u, 1, TB - 2), (kind, "S", u, 1, TB - 1)]
                            else:
                                lasts = [(kind, "S", u, 1, TB - 1, 0), (kind, "S", u, 1, TB - 1, 1)]
                            for p_ in lasts:
                                wait_emptied(dve, p_)
                            if not causal:
                                link(dve.tensor_tensor(row_max[:, u % 2, :, :], half_max[:, u % 2, 0, :, :],
                                                       half_max[:, u % 2, 1, :, :], ALU.min))
                            v = u + before
                            if v >= 2:
                                k2 = "self" if v - 2 < UNITS else "cross"
                                wait_filled(dve, (k2, "max_rows", (v - 2) % UNITS))
                            link(dve.tensor_copy(max_parts[:, u % 2, :, 0:2], row_max[:, u % 2, :, :]))
                            dve.tensor_tensor(max_parts[:, u % 2, :, 2:4], row_max[:, u % 2, :, :],
                                              max_parts[:, u % 2, :, 0:2].bitcast(F32), ALU.subtract).then_inc(parts_done, 1)
                        elif what == "values" and r == per_unit - 1:
                            acc = wait_filled(dve, (kind, "PV", u))
                            if u >= 2:
                                wait_filled(dve, (kind, "PVT", u - 2))
                            ins = dve.tensor_copy(pv_out[:, u % 2, :], acc[:, :])
                            ins.then_inc(pv_copied, 1)
                            dve.wait_ge(pv_copied, u + 1 + before)
                            dve.sem_inc(bank_freed[filled_as[(kind, "PV", u)][0]], 1)
                        elif what == "turn_back":
                            acc = wait_filled(dve, (kind, "PVT", u))
                            pair = u % PAIRS
                            if u == PAIRS:
                                for i in range(TB):
                                    wait_filled(dve, (kind, "ctxT", 0, i))
                            if causal:
                                v4 = acc[:, :].rearrange("p (i j d) -> p i j d", i=TB, j=2)
                                link(dve.reciprocal(inv_den[:, u % 2, :, :], v4[:, :, :, HD]))
                                dst = heads_out[:, :, 2 * pair * HD:(2 * pair + 2) * HD].rearrange("p i (j d) -> p i j d", j=2)
                                ins = dve.tensor_tensor(dst, v4[:, :, :, 0:HD],
                                                        inv_den[:, u % 2, :, :].unsqueeze(3).to_broadcast([P, TB, 2, HD]), ALU.mult)
                                ins.then_inc(heads_done, 1)
                                dve.wait_ge(heads_done, u + 1)
                                dve.sem_inc(bank_freed[filled_as[(kind, "PVT", u)][0]], 1)
                            else:
                                v5 = acc[:, :].rearrange("p (i j h d) -> p i j h d", i=TB, j=2, h=2)
                                sums = odd_sum[:, u % 2, :, :, :]
                                link(dve.tensor_copy(sums, v5[:, :, :, 1, 0:CHD + 1]))
                                ins = dve.tensor_tensor(sums, v5[:, :, :, 0, 0:CHD + 1], sums, ALU.add)
                                free(ins, (kind, "PVT", u))
                                wait_emptied(dve, (kind, "PVT", u))
                                link(dve.reciprocal(inv_den[:, u % 2, :, :], sums[:, :, :, CHD]))
                                dst = cheads_out[:, :, 2 * pair * CHD:(2 * pair + 2) * CHD].rearrange("p i (j d) -> p i j d", j=2)
                                dve.tensor_tensor(dst, sums[:, :, :, 0:CHD],
                                                  inv_den[:, u % 2, :, :].unsqueeze(3).to_broadcast([P, TB, 2, CHD]), ALU.mult)\
                                   .then_inc(heads_done, 1)
                        elif what == "context":
                            for i in range(TB):
                                act_lo((kind, "ctxT", u, i), u * TB + i, KH if causal else KC)

            attend("self", self_steps, TB)
            dve.wait_ge(w_row_in, 32)
            for n in range(T + 3):
                if n < T:
                    for e in range(2):
                        add_expert(("dense", n, e), n, e)
                        wait_emptied(dve, ("dense", n, e))
                if 1 <= n <= T:
                    if n == 1:
                        wait_filled(dve, ("self", "PVT", UNITS - 1))
                    normed("cross", n - 1)
                if 2 <= n < T + 2:
                    act_lo(("actT", "cross", n - 2), n - 2)
                if n in CQ_STEPS:
                    for m in range(KC):
                        staged_lo(("cqT", CQ_STEPS.index(n), m), lambda a: a[:, 0, :])
            attend("cross", cross_steps, MT)
            dve.wait_ge(w_row_in, 48)
            for n in range(T + 2):
                if n < T:
                    acc = wait_filled(dve, ("cdense", n))
                    free(dve.tensor_tensor(hs[:, n, :], acc[:, :], hs[:, n, :], ALU.add), ("cdense", n))
                    wait_emptied(dve, ("cdense", n))
                if 1 <= n <= T:
                    if n == 1:
                        wait_filled(dve, ("cross", "PVT", UNITS - 1))
                    normed("mlp", n - 1)
                if n >= 2:
                    act_lo(("actT", "mlp", n - 2), n - 2)

            items = [(e, f, t) for e, f in ff_cuts for t in range(T)]
            for n in range(len(items) + 2):
                if n < len(items):
                    e, f, t = items[n]
                    fw = FS[f]
                    dve.wait_ge(silu_done, n + 1)
                    acc = banks[filled_as[("gu", e, f, t)][0]]
                    if n >= 2:
                        wait_filled(dve, ("hidT", *items[n - 2]))
                    src = acc[:, 1, 0:fw] if fw >= 256 else acc[:, 0, fw:2 * fw]

                    def gated():
                        dve.tensor_tensor(hid[:, n % 2, 0:fw], src, silu_g[:, n % 2, 0:fw], ALU.mult).then_inc(hid_done, 1)
                        dve.wait_ge(hid_done, n + 1)

                    if e == 0:
                        gated()
                    else:
                        with dve.If(vision[t] > 0):
                            gated()
                        with dve.Else():
                            dve.sem_inc(hid_done, 1)
                    dve.sem_inc(bank_freed[filled_as[("gu", e, f, t)][0]], 1)
                if n >= 1 and n - 1 < len(items):
                    e, f, t = items[n - 1]
                    product = ("hidT", e, f, t)
                    dve.wait_ge(hi_done, hi_no[product])
                    acc = banks[filled_as[product][0]]
                    full = FS[f] // P
                    s = (n - 1) % 2

                    def hid_lo():
                        ins = dve.tensor_tensor(hidT_lo[:, s, 0:full, :], tiles(acc, full),
                                                hidT_hi[:, s, 0:full, :].bitcast(F32), ALU.subtract)
                        if FS[f] > full * P:
                            w = FS[f] - full * P
                            ins = dve.tensor_tensor(hidT_lo[0:w, s, full, :], acc[0:w, full * P:(full + 1) * P],
                                                    hidT_hi[0:w, s, full, :].bitcast(F32), ALU.subtract)
                        free(ins, product)

                    if e == 0:
                        hid_lo()
                    else:
                        with dve.If(vision[t] > 0):
                            hid_lo()
                        with dve.Else():
                            free_skipped(dve, product)
                if n >= 2:
                    e, f, t = items[n - 2]
                    product = ("down", e, f, t)
                    add_expert(product, t, e)

            for g in range(KC + 2 * KH):
                hi, lo = (wmT_hi[:, g, :], wmT_lo[:, g, :]) if g < KC else (wgT_hi[:, g - KC, :], wgT_lo[:, g - KC, :])
                lo_part(("wT", g), lo, hi, lambda a: a[:, :])
            dve.wait_ge(wm_hi_done, 1)
            dve.tensor_tensor(wm_lo[:, :, :], wm_raw[:, :, :], wm_hi[:, :, :].bitcast(F32), ALU.subtract).then_inc(wm_ready, 1)
            for t in range(T):
                act_lo(("hsT", t), t)
            for m in range(KC):
                lo_part(("G", m), G_lo[:, m, :], G_hi[:, m, :], lambda a: a[:, :])
            for b in range(B):
                for m in range(KC):
                    cols = slice(b * L, (b + 1) * L)
                    lo_part(("qm", b, m), qm_lo[:, m, cols], qm_hi[:, m, cols], lambda a: a[:, 0, :])

            def context_lo(b):
                dve.wait_ge(mc_hi_done, b + 1)
                dve.tensor_tensor(mc_lo[:, :, :], mc_raw[:, :, :], mc_hi[:, :, :].bitcast(F32), ALU.subtract).then_inc(mc_ready, 1)

            def turned_context(b):
                for g in range(TB):
                    cols = slice((b * MT + 2 * g) * P, (b * MT + 2 * g + 2) * P)
                    lo_part(("mcT", b, g), mcT_lo[:, :, cols], mcT_hi[:, :, cols],
                            lambda a: a[:, :].rearrange("p (k t) -> p k t", k=KC))

            turned_context(0)
            context_lo(0)
            dve.wait_ge(w_row_in, 80)
            for n in range(T + 3):
                if 2 <= n < T + 2:
                    lo_part(("amT", n - 2), amT_lo[:, :, :], amT_hi[:, :, :], lambda a: tiles(a, KC))
                if n < T:
                    acc = wait_filled(dve, ("ms", n))
                    link(dve.tensor_reduce(row_max[:, n % 2, 0, 0:1], acc[:, :, :].rearrange("p a b -> p (a b)"), AX,
                                           ALU.max, negate=True))
                    dve.tensor_scalar(den[:, 0, n:n + 1], row_max[:, n % 2, 0, 0:1], float(1.0 / np.sqrt(H)), None, ALU.mult)\
                       .then_inc(nmax_done, 1)
                if 1 <= n <= T:
                    for h in range(2):
                        lo_part(("attnT", n - 1, h), attnT_lo[:, 4 * h:4 * h + 4, :], attnT_hi[:, 4 * h:4 * h + 4, :],
                                lambda a: tiles(a, 4))
                if n >= 3:
                    t = n - 3
                    dve.wait_ge(rstd_done, 3 * T + t + 1)
                    dve.scalar_tensor_tensor(out=xs[:, t % 2, :], in0=xs[:, t % 2, :], scalar=rstd[:, 3, t:t + 1],
                                             in1=w_row[:, :], op0=ALU.mult, op1=ALU.mult).then_inc(row_done, 1)
                if 2 <= n < T + 2:
                    t = n - 2
                    acc = wait_filled(dve, ("gate", t))
                    if t >= 1:
                        dve.wait_ge(fused_done, t)
                    ins = dve.tensor_tensor(stage0[:, :], acc[:, :], bias_row[:, :], ALU.add)
                    free(ins, ("gate", t))
                    wait_emptied(dve, ("gate", t))
                    dve.sem_inc(gate_in, 1)
                    acc = wait_filled(dve, ("mctx", t))
                    dve.wait_ge(gate_done, t + 1)
                    ins = dve.scalar_tensor_tensor(out=stage0[:, :], in0=stage1[:, :], scalar=1.0,
                                                   in1=acc[:, :], op0=ALU.add, op1=ALU.mult)
                    free(ins, ("mctx", t))
                    wait_emptied(dve, ("mctx", t))
                    if t >= 2:
                        dve.wait_ge(result_out[t % 2], 16 * (t // 2))
                    dve.scalar_tensor_tensor(out=xs[:, t % 2, :], in0=stage0[:, :], scalar=0.5,
                                             in1=hs[:, t, :], op0=ALU.mult, op1=ALU.add).then_inc(fused_done, 1)
                if n < T:
                    dve.wait_ge(exp_done, n + 1)
                    dve.sem_inc(bank_freed[filled_as[("ms", n)][0]], 1)
                if 1 <= n <= T:
                    t = n - 1
                    acc = wait_filled(dve, ("am", t))
                    link(dve.reciprocal(inv_den[:, t % 2, 0, 0:1], den[:, 1, t:t + 1]))
                    if t >= 1:
                        wait_filled(dve, ("amT", t - 1))
                    ins = dve.tensor_scalar(am[:, :], acc[:, 0:C], inv_den[:, t % 2, 0, 0:1], None, ALU.mult)
                    free(ins, ("am", t))
                    wait_emptied(dve, ("am", t))
                    dve.sem_inc(am_done, 1)
                if n == TB - 2:
                    turned_context(1)
                if n == TB:
                    context_lo(1)

        @block.gpsimd
        def _(pool):
            chain = [0]

            def link(ins):
                chain[0] += 1
                ins.then_inc(pool_chain, 1)
                pool.wait_ge(pool_chain, chain[0])

            pool.memset(tt_next[:, :], 0).then_inc(next_zeroed, 1)
            link(pool.memset(ident[:, :], 0.0))
            pool.affine_select(out=ident[:, :], in_=ident[:, :], compare_op=ALU.not_equal, fill=1.0, base=0,
                               pattern=[[-1, P]], channel_multiplier=1).then_inc(consts_ready, 1)
            pool.memset(cv_tile[:, :, :, CHD:2 * CHD], 1.0).then_inc(consts_ready, 1)
            pool.memset(minus_half[:, :], -0.5).then_inc(consts_ready, 1)
            pool.wait_ge(consts_ready, 3)
            def split(hi, lo, raw, ready):
                link(pool.tensor_copy(hi, raw))
                pool.tensor_tensor(lo, raw, hi.bitcast(F32), ALU.subtract).then_inc(ready, 1)

            def take_rest(cut, some=None):
                s = cut_at[cut][0]
                for i, (hi, lo, raw) in enumerate(weight_pieces(cut)):
                    if some is not None and i not in some:
                        continue
                    pool.wait_ge(high_copied[s], copy_before[cut] + i + 1)
                    pool.tensor_tensor(lo, raw, hi.bitcast(F32), ALU.subtract).then_inc(weights_ready[s], 1)

            def norm_scale(stage, t):
                i = NORMS.index(stage)
                pool.wait_ge(squares_done, i * T + t + 1)
                link(pool.tensor_scalar(sum_sq[:, i, t:t + 1], sum_sq[:, i, t:t + 1], 1.0 / H, EPS, ALU.mult, ALU.add))
                pool.tensor_tensor(rstd[:, i, t:t + 1], sum_sq[:, i, t:t + 1], minus_half[:, :], ALU.pow).then_inc(rstd_done, 1)

            link(pool.memset(ident_bf[:, :], 0.0))
            link(pool.affine_select(out=ident_bf[:, :], in_=ident_bf[:, :], compare_op=ALU.not_equal, fill=1.0, base=0,
                                    pattern=[[-1, P]], channel_multiplier=1))
            link(pool.memset(hide_s[:, :], 0.0))
            link(pool.memset(hide_t[:, :], 0.0))
            link(pool.affine_select(out=hide_s[:, :], in_=hide_s[:, :], compare_op=ALU.is_ge, fill=NEG, base=0,
                                    pattern=[[-1, P]], channel_multiplier=1))
            link(pool.affine_select(out=hide_t[:, :], in_=hide_t[:, :], compare_op=ALU.is_ge, fill=NEG, base=0,
                                    pattern=[[1, P]], channel_multiplier=-1))
            for t in range(T):
                norm_scale("in", t)
                if t == 1:
                    take_rest("v")
            pool.memset(v_tile[:, :, :, HD:64], 1.0).then_inc(consts_ready, 1)
            take_rest("k")
            pool.wait_ge(small_in, SMALL)
            for i in range(TB):
                pool.indirect_dma_start(rot[:, i, :], None, table_d[:, :],
                                        bass.IndirectOffsetOnAxis(ap=pos_i[:, i:i + 1].bitcast(U32), axis=0))\
                    .then_inc(rot_ready, 16)
            done = 0
            for c in ("k", "q"):
                for t in range(T):
                    wait_emptied(pool, ("qkv", c, t, 1))
                    if t == 0 and c == "k":
                        pool.wait_ge(rot_ready, 16 * TB)
                    if done >= 2:
                        pool.wait_ge(rotated, done - 1)
                    m4 = mixed[:, t % 2, :].rearrange("p (h a d) -> p h a d", h=NH, a=2)
                    b4 = by_sin[:, t % 2, :].rearrange("p (h a d) -> p h a d", h=NH, a=2)
                    hd = HD // 2
                    sin = rot[:, t % TB, hd:2 * hd].unsqueeze(1).to_broadcast([P, NH, hd])
                    nsin = rot[:, t % TB, 2 * hd:3 * hd].unsqueeze(1).to_broadcast([P, NH, hd])
                    pool.tensor_tensor(b4[:, :, 0, :], m4[:, :, 1, :], nsin, ALU.mult)
                    pool.tensor_tensor(b4[:, :, 1, :], m4[:, :, 0, :], sin, ALU.mult).then_inc(by_sin_done, 1)
                    done += 1
                    if c == "k" and t < 4:
                        take_rest("q", (2 * t, 2 * t + 1))
                    if c == "k" and t == 4:
                        pool.wait_ge(ckv_in, 16)
                        split(ckv_hi[:, :, :], ckv_lo[:, :, :], ckv_raw[:, :, :], ckv_ready)
            for v in range(2):
                pool.wait_ge(v_out[v], 16 * (T // 2))
            pool.wait_ge(by_sin_done, 2 * T)
            for s in range(SLOTS):
                pool.memset(raw32(k_st[s][ONES:ONES + 2, :, :]), 1.0).then_inc(stack_set, 1)
                pool.wait_ge(stack_set, s + 1)
            wait_used(pool, ("qkv", "q", T - 1, 0), ("qkv", "q", T - 1, 1))
            pool.wait_ge(raw_in[0], 64)
            for hi, lo, raw in weight_pieces("dense"):
                split(hi, lo, raw, weights_ready[0])
            pool.wait_ge(small_w_in, 32)
            split(cq_hi[:, :, :], cq_lo[:, :, :], cq_raw[:, :, :], small_w_ready)
            split(cd_hi[:, :, :], cd_lo[:, :, :], cd_raw[:, :, :], small_w_ready)
            pool.wait_ge(small_w_ready, 2)
            for s in range(SLOTS):
                wait_filled(pool, ("self", "PV", UNITS - SLOTS + s))
                for r0 in (32, 64):
                    link(pool.memset(raw32(q_st[s][r0:r0 + 32, :, :]), 0.0))
                    link(pool.memset(raw32(k_st[s][r0:r0 + 32, :, :]), 0.0))
                pool.memset(raw32(k_st[s][ONES:ONES + 2, :, :]), 1.0).then_inc(stack_set, 1)
                pool.wait_ge(stack_set, SLOTS + s + 1)
            for t in range(T):
                norm_scale("cross", t)

            pool.wait_ge(raw_in[0], raw_count[ff_cuts[0]])
            wait_used(pool, ("dense", T - 1, 0), ("dense", T - 1, 1))
            for hi, lo, raw in weight_pieces(ff_cuts[0]):
                split(hi, lo, raw, weights_ready[0])
            for t in range(T):
                norm_scale("mlp", t)
            for n in range(1, len(ff_cuts)):
                take_rest(ff_cuts[n])
            for t in range(T):
                pool.wait_ge(squares_done, 3 * T + t + 1)
                link(pool.tensor_scalar(sum_sq[:, 3, t:t + 1], sum_sq[:, 3, t:t + 1], 1.0 / H, EPS, ALU.mult, ALU.add))
                pool.tensor_tensor(rstd[:, 3, t:t + 1], sum_sq[:, 3, t:t + 1], minus_half[:, :], ALU.pow).then_inc(rstd_done, 1)

        @block.sync
        def _(sp):
            def rows(w):
                return w.rearrange("(k p) n -> p k n", p=P)

            def row_on_all(v):
                return v.rearrange("(a n) -> a n", a=1).to_broadcast([P, H])

            def load_cut(c):
                s = cut_at[c][0]
                for e in range(2):
                    if c == "dense":
                        src = rows(dense_w[e])
                    else:
                        j = ("q", "k", "v").index(c)
                        src = rows(qkv_w[e])[:, :, j * H:(j + 1) * H]
                    sp.dma_start(qkv_raw[s][:, e, :, :], src).then_inc(v_raw_in[e] if c == "v" else raw_in[s], 16)

            sp.dma_start(hs[:, 0, :], x_d[0:P, :]).then_inc(x_in[0], 16)
            sp.dma_start(w_row[:, :], row_on_all(ln_in_w)).then_inc(w_row_in, 16)
            for t in range(1, 4):
                sp.dma_start(hs[:, t, :], x_d[t * P:(t + 1) * P, :]).then_inc(x_in[t], 16)
            with nc.allow_non_contiguous_dma(reason="one small column per token tile"):
                sp.wait_ge(next_zeroed, 1)
                sp.dma_start(pos_i[:, :], pos.rearrange("a (i p) -> p (a i)", p=P)).then_inc(small_in, 16)
                sp.dma_start(tt_now[:, :], tt.rearrange("b (i p) -> p (b i)", p=P)).then_inc(small_in, 16)
                shifted = tt.rearrange("b (i p) -> p b i", p=P)
                sp.dma_start(tt_next[0:P - 1, :].rearrange("p (b i) -> p b i", b=B), shifted[1:P, :, :]).then_inc(small_in, 16)
                for b in range(B):
                    sp.dma_start(tt_next[P - 1:P, b * TB:(b + 1) * TB - 1], shifted[0:1, b, 1:TB]).then_inc(small_in, 16)
            load_cut("v")
            for t in range(4, T):
                sp.dma_start(hs[:, t, :], x_d[t * P:(t + 1) * P, :]).then_inc(x_in[t], 16)
            load_cut("k")
            sp.dma_start(ckv_raw[:, :, :], rows(ckv_w)).then_inc(ckv_in, 16)

            def store_staged(product, dst, view):
                z = stage_no[product]
                wait_emptied(sp, product)
                sp.dma_start(dst[0], view(raw32(stage_hi[:, z % 2, :]))).then_inc(stage_out[z % 2], 16)
                sp.dma_start(dst[1], view(raw32(stage_lo[:, z % 2, :]))).then_inc(stage_out[z % 2], 16)

            def stored(product):
                n = stage_no[product] + 1
                sp.wait_ge(stage_out[0], 32 * ((n + 1) // 2))
                sp.wait_ge(stage_out[1], 32 * (n // 2))

            def load_stack(kind, u, uses_before):
                slot, b, pair = u % SLOTS, u // PAIRS, u % PAIRS
                w, scr_q, scr_k = (HD, q_scr, k_scr) if kind == "self" else (CHD, cq_scr, ck_scr)
                n_k = L if kind == "self" else M
                if u >= SLOTS:
                    wait_filled(sp, (kind, "PV", u - SLOTS))
                for row, part_q, part_k in ((0, 0, 0), (1, 0, 1), (2, 1, 0)):
                    feats = slice(2 * pair * w, (2 * pair + 2) * w)
                    sp.dma_start(raw32(q_st[slot][row * w:(row + 1) * w, :, :]),
                                 scr_q[part_q, feats, b * L:(b + 1) * L].rearrange("(j p) n -> p j n", j=2)).then_inc(stack_in[slot], 16)
                    sp.dma_start(raw32(k_st[slot][row * w:(row + 1) * w, :, 0:n_k]),
                                 scr_k[part_k, feats, b * n_k:(b + 1) * n_k].rearrange("(j p) n -> p j n", j=2)).then_inc(stack_in[slot], 16)
                if kind == "self":
                    src = v_scr[b * L:(b + 1) * L, pair * 128:(pair + 1) * 128].rearrange("(k p) c -> p k c", p=P)
                    dst = v_st[slot][:, :].rearrange("p (k c) -> p k c", k=TB)
                else:
                    src = cv_scr[b * M:(b + 1) * M, pair * 64:(pair + 1) * 64].rearrange("(k p) c -> p k c", p=P)
                    dst = v_st[slot][:, :].rearrange("p (k c) -> p k c", k=MT)
                sp.dma_start(dst, src).then_inc(stack_in[slot], 16)

            wait_weights(sp, "v")
            load_cut("q")
            for t in range(T):
                wait_emptied(sp, ("qkv", "v", t, 1))
                sp.dma_start(v_scr[t * P:(t + 1) * P, :], v_tile[:, t % 2, :, :].rearrange("p h d -> p (h d)"))\
                    .then_inc(v_out[t % 2], 16)
            for c, scr in (("k", k_scr), ("q", q_scr)):
                for t in range(T):
                    if c == "q" and t == 0:
                        wait_weights(sp, "q")
                        for d in range(4):
                            sp.dma_start(ctx_tile[:, 4 * d:4 * d + 4, :],
                                         ctx_d[4 * d * P:4 * (d + 1) * P, :].rearrange("(u p) c -> p u c", p=P)).then_inc(ctx_in_s[d], 16)
                    d = scr[:, :, t * P:(t + 1) * P].rearrange("a (k p) n -> a p k n", p=P)
                    store_staged(("rotT", c, t), (d[0], d[1]), lambda a: a.rearrange("p (k n) -> p k n", k=KH))
                    if c == "q" and t == TB - 1:
                        stored(("rotT", "q", t))
                        for i in range(2):
                            sp.wait_ge(v_out[i], 16 * (T // 2))
                        load_stack("self", 0, 0)
                        load_stack("self", 1, 0)

            for n in range(B * M // L):
                for m in range(KC):
                    d = ck_scr[:, m * P:(m + 1) * P, n * L:(n + 1) * L]
                    store_staged(("kT", n, m), (d[0], d[1]), lambda a: a)
            for u in range(0, B * MT, 2):
                wait_emptied(sp, ("cv", u))
                wait_emptied(sp, ("cv", u + 1))
                sp.dma_start(cv_scr[u * P:(u + 2) * P, :].rearrange("(u p) c -> p u c", p=P),
                             cv_tile[:, u % 4:u % 4 + 2, :, :].rearrange("p u h d -> p u (h d)")).then_inc(v_out[u // 2 % 2], 16)
            load_cut("dense")
            stored(("kT", B * M // L - 1, KC - 1))
            for i in range(2):
                sp.wait_ge(v_out[i], 16 * (T // 2 + MT // 2))
            for u in range(2, UNITS):
                load_stack("self", u, 0)
                if u == 5:
                    wait_weights(sp, "dense")
                    sp.dma_start(cq_raw[:, :, :], rows(cq_w)).then_inc(small_w_in, 16)
                    sp.dma_start(cd_raw[:, :, :], rows(cdense_w)).then_inc(small_w_in, 16)
                    wait_filled(sp, ("actT", "in", T - 1))
                    sp.dma_start(w_row[:, :], row_on_all(ln_cross_w)).then_inc(w_row_in, 16)
            for b in range(B):
                for m in range(KC):
                    d = cq_scr[:, m * P:(m + 1) * P, b * L:(b + 1) * L]
                    store_staged(("cqT", b, m), (d[0], d[1]), lambda a: a)
                stored(("cqT", b, KC - 1))
                if b == 0:
                    for u in range(SLOTS):
                        sp.wait_ge(stack_set, SLOTS + u + 1)
                        load_stack("cross", u, UNITS // SLOTS)

            def load_ff(n):
                e, f = ff_cuts[n]
                s = cut_at[(e, f)][0]
                f0, fw = sum(FS[:f]), FS[f]
                a = KH * 2 * fw
                if n >= 2:
                    wait_weights(sp, ff_cuts[n - 2])
                gu = ff_raw[s][:, 0:a].rearrange("p (k g n) -> p k g n", k=KH, g=2)
                sp.dma_start(gu[:, :, 0, :], rows(gate_w[e])[:, :, f0:f0 + fw]).then_inc(raw_in[s], 16)
                sp.dma_start(gu[:, :, 1, :], rows(up_w[e])[:, :, f0:f0 + fw]).then_inc(raw_in[s], 16)
                full = fw // P
                dn = ff_raw[s][:, a:a + full * H].rearrange("p (k n) -> p k n", k=full)
                sp.dma_start(dn, rows(down_w[e][f0:f0 + full * P, :])).then_inc(raw_in[s], 16)
                if fw % P:
                    w = fw % P
                    sp.dma_start(ff_raw[s][0:w, a + full * H:a + (full + 1) * H],
                                 down_w[e][f0 + full * P:f0 + fw, :]).then_inc(raw_in[s], 16)

            for u in range(SLOTS, UNITS):
                load_stack("cross", u, UNITS // SLOTS)
                if u == 5:
                    sp.wait_ge(small_w_ready, 2)
                    wait_filled(sp, ("cqT", B - 1, KC - 1))
                    load_ff(0)
                    wait_filled(sp, ("actT", "cross", T - 1))
                    sp.dma_start(w_row[:, :], row_on_all(ln_attn_w)).then_inc(w_row_in, 16)
            wait_filled(sp, ("cross", "PV", UNITS - 1))
            for n in range(1, len(ff_cuts)):
                load_ff(n)
            wait_weights(sp, ff_cuts[-2])
            sp.dma_start(wg_raw[:, :, :], rows(W_gate)).then_inc(lmem_in, 16)
            sp.dma_start(wm_raw[:, :, :], rows(W_mem)).then_inc(lmem_in, 16)
            wait_filled(sp, ("actT", "mlp", T - 1))
            sp.dma_start(w_row[:, :], row_on_all(norm_w)).then_inc(w_row_in, 16)
            sp.dma_start(bias_row[:, :], row_on_all(b_gate)).then_inc(w_row_in, 16)
            wait_used(sp, ("down", 1, len(FS) - 1, T - 2), ("down", 1, len(FS) - 1, T - 1))
            for b in range(B):
                if b:
                    sp.wait_ge(mc_ready, b)
                    wait_filled(sp, ("mcT", b - 1, TB - 1))
                sp.dma_start(mc_raw[:, :, :], ctx_d[b * M:(b + 1) * M, :].rearrange("(m p) c -> p m c", p=P)).then_inc(mc_in, 16)
            for t in range(T):
                sp.wait_ge(row_done, t + 1)
                sp.dma_start(out_d[t * P:(t + 1) * P, :], xs[:, t % 2, :]).then_inc(result_out[t % 2], 16)
            for i in range(2):
                sp.wait_ge(result_out[i], 16 * T // 2)


_INS = ["x", "ctx_1024", "pos_1xS", "mask_BxS_ik0", "L0_xattn_ln_in_w", "L0_xattn_ln_post_attn_w",
        "L0_xattn_ln_post_cross_w", "L0_xattn_v_qkv", "L0_xattn_l_qkv", "L0_xattn_v_dense", "L0_xattn_l_dense",
        "L0_xattn_cq_w", "L0_xattn_ckv_w", "L0_xattn_cdense_w", "L0_xattn_v_gate", "L0_xattn_v_up",
        "L0_xattn_v_down", "L0_xattn_l_gate", "L0_xattn_l_up", "L0_xattn_l_down", "L1_xattn_W_mem",
        "L1_xattn_W_gate", "L1_xattn_b_gate", "L1_xattn_norm_w"]
_OUTS = [((B, L, H), "float32")]


def kernel(**inputs):
    import numpy as _np
    import concourse.bacc as _bacc
    from concourse import mybir as _mybir
    from concourse.bass_utils import run_bass_kernel_spmd as _run

    nc = _bacc.Bacc("TRN2", target_bir_lowering=False, num_devices=1)
    arrays, args = {}, []
    for name in _INS:
        a = _np.ascontiguousarray(inputs[name])
        arrays[f"in_{name}_dram"] = a
        args.append(nc.dram_tensor(f"in_{name}_dram", a.shape, _mybir.dt.from_np(a.dtype), kind="ExternalInput").ap())
    for i, (shape, dtype) in enumerate(_OUTS):
        dt = _mybir.dt.from_np(_np.dtype(dtype))
        args.append(nc.dram_tensor(f"out_{i}_dram", shape, dt, kind="ExternalOutput").ap())
    xattn_kernel(nc, *args)
    r = _run(nc, [arrays], core_ids=[0])
    got = tuple(r.results[0][f"out_{i}_dram"] for i in range(len(_OUTS)))
    return got[0]
```

```python
import numpy as np
import concourse.bass as bass
from concourse import mybir
from contextlib import ExitStack

F32 = mybir.dt.float32
F32R = mybir.dt.float32r
BF16 = mybir.dt.bfloat16
I32 = mybir.dt.int32
U32 = mybir.dt.uint32
ALU = mybir.AluOpType
ACT = mybir.ActivationFunctionType
AX = mybir.AxisListType.X

P = 128
B, L, H = 2, 512, 512
T = B * L // P
TB = L // P
KH = H // P
NH = 16
HD = H // NH
C = 256
KC = C // P
CHD = C // NH
M = 1024
MT = M // P
F = 1376
EPS = 1e-6
NEG = -1e30
PAIRS = NH // 2
UNITS = B * PAIRS
SLOTS = {"self": 6, "cross": 4}
ONES = 96
FS = [384, 384, 384, 224]

NORMS = ["in", "cross", "mlp"]
TURNS = [(s, t) for s in NORMS for t in range(T)]
turn_no = {k: i for i, k in enumerate(TURNS)}
SMALL = 16 * (3 + B)


def rotary_table():
    inv = (1.0 / np.float32(10000.0) ** (np.arange(0, HD, 2, dtype=np.float32) / np.float32(HD))).astype(np.float32)
    a = np.outer(np.arange(L, dtype=np.float32), inv).astype(np.float32)
    return np.concatenate([np.cos(a), np.sin(a), -np.sin(a)], axis=1).astype(np.float32)


def raw32(ap):
    return ap.bitcast(F32)


def attention_steps(per_unit):
    rows_lag, values_lag = 2, 1
    lead = per_unit + 5
    n = UNITS * per_unit
    steps = []
    for x in range(lead + n + values_lag + 6):
        todo = []

        def at_end(what, since):
            u, r = divmod(since, per_unit)
            if since >= 0 and r == per_unit - 1 and u < UNITS:
                todo.append((what, u, 0))

        y = x - lead
        v = y - values_lag
        if x < n:
            todo.append(("scores", x // per_unit, x % per_unit))
        at_end("max_parts", x - 1)
        if 0 <= y < n:
            todo.append(("probs", y // per_unit, y % per_unit))
        if 0 <= v < n:
            todo.append(("values", v // per_unit, v % per_unit))
        at_end("max_rows", x - rows_lag)
        at_end("turn_back", v - 2)
        u, r = divmod(v - 4, per_unit)
        if v >= 4 and r == per_unit - 1 and u < UNITS and u % PAIRS == PAIRS - 1:
            todo.append(("context", u // PAIRS, 0))
        steps.append(todo)
    return steps


def xattn_kernel(nc, x, ctx_in, pos, tt, ln_in_w, ln_attn_w, ln_cross_w, v_qkv, l_qkv, v_dense, l_dense,
                 cq_w, ckv_w, cdense_w, v_gate, v_up, v_down, l_gate, l_up, l_down,
                 W_mem, W_gate, b_gate, norm_w, out):
    x_d = x.rearrange("b l h -> (b l) h")
    ctx_d = ctx_in.rearrange("b m c -> (b m) c")
    out_d = out.rearrange("b l h -> (b l) h")
    table = nc.inline_tensor(rotary_table(), name="rotary_table")
    table_d = table.ap() if hasattr(table, "ap") else table
    qkv_w, dense_w = [l_qkv, v_qkv], [l_dense, v_dense]
    gate_w, up_w, down_w = [l_gate, v_gate], [l_up, v_up], [l_down, v_down]

    def scratch(name, shape, dt=F32):
        return nc.dram_tensor(name, shape, dt, kind="Internal").ap()

    q_scr = scratch("q_scr", [2, H, B * L])
    k_scr = scratch("k_scr", [2, H, B * L])
    v_scr = scratch("v_scr", [B * L, NH * 64], F32)
    cq_scr = scratch("cq_scr", [2, C, B * L])
    ck_scr = scratch("ck_scr", [2, C, B * M])
    cv_scr = scratch("cv_scr", [B * M, NH * 32], F32)

    ctx = ExitStack()
    with ctx:
        def sem(name):
            return ctx.enter_context(nc.semaphore(name))

        base = (nc.sbuf_base + 31) // 32 * 32
        place = [base]

        def sb_at(name, shape, dt, offset):
            return nc.alloc_sbuf_tensor_at(name, shape, dt, offset=offset)

        def keep(name, shape, dt):
            words = int(np.prod(shape[1:])) * (2 if dt == BF16 else 4)
            t = sb_at(name, shape, dt, place[0])
            place[0] += (words + 31) // 32 * 32
            return t

        def area(size):
            at = place[0]
            place[0] += size
            return at

        hs = keep("hs", [P, T, H], F32)
        actT_hi = keep("actT_hi", [P, KH, B * L], F32R)
        actT_lo = keep("actT_lo", [P, KH, B * L], F32R)
        ident = keep("ident", [P, P], F32)
        ident_bf = keep("ident_bf", [P, P], BF16)
        hide_s = keep("hide_s", [P, P], BF16)
        hide_t = keep("hide_t", [P, P], BF16)
        w_row = keep("w_row", [P, H], F32)
        rot = keep("rot", [P, TB, 3 * HD // 2], F32)
        pos_i = keep("pos_i", [P, TB], I32)
        tt_now = keep("tt_now", [P, T], I32)
        tt_next = keep("tt_next", [P, T], I32)
        is_v = keep("is_v", [P, T], F32)
        is_l = keep("is_l", [P, T], F32)
        vision_count = keep("vision_count", [1, T + 1], I32)
        eq_tmp = keep("eq_tmp", [P, T], F32)
        sum_sq = keep("sum_sq", [P, 4, T], F32)
        rstd = keep("rstd", [P, 4, T], F32)
        minus_half = keep("minus_half", [P, 1], F32)
        row_max = keep("row_max", [P, 2, TB, 2], F32)
        max_parts = keep("max_parts", [P, 2, TB, 4], F32R)
        inv_den = keep("inv_den", [P, 2, TB, 2], F32)
        den = keep("den", [P, 2, T], F32)
        square_out = keep("square_out", [P, H], BF16)
        xs = keep("xs", [P, 2, H], F32)
        stage_hi = keep("stage_hi", [P, 2, H], F32R)
        stage_lo = keep("stage_lo", [P, 2, H], F32R)
        KB = 1024
        stage0 = sb_at("stage0", [P, H], F32, place[0] - 8 * KB)
        stage1 = sb_at("stage1", [P, H], F32, place[0] - 4 * KB)
        bias_row = sb_at("bias_row", [P, H], F32, place[0] - 2 * KB)
        area_a = area(48 * KB)
        area_b = area(16 * KB)
        area_c = area(16 * KB)
        area_d = area(36 * KB)
        area_e = area(18 * KB)
        area_f = area(8 * KB)
        assert place[0] <= nc.sbuf_usable_end, (place[0], nc.sbuf_usable_end)

        ctx_tile = sb_at("ctx_tile", [P, B * MT, C], F32, area_e)
        cv_tile = sb_at("cv_tile", [P, 4, NH, 32], F32, area_c + 8 * KB)
        ctxT_hi = sb_at("ctxT_hi", [P, KC, B * M], F32R, base + 16 * KB)
        ctxT_lo = sb_at("ctxT_lo", [P, KC, B * M], F32R, base + 32 * KB)
        slot_at = [area_d, area_a]
        raw_at = [area_e, area_b]
        qkv_hi = [sb_at(f"qkv_hi{s}", [P, 2, KH, H], F32R, slot_at[s]) for s in range(2)]
        qkv_lo = [sb_at(f"qkv_lo{s}", [P, 2, KH, H], F32R, slot_at[s] + 16 * KB) for s in range(2)]
        qkv_raw = [sb_at(f"qkv_raw{s}", [P, 2, KH, H], F32, raw_at[s]) for s in range(2)]
        ckv_hi = sb_at("ckv_hi", [P, KC, 2 * C], F32R, area_f)
        ckv_lo = sb_at("ckv_lo", [P, KC, 2 * C], F32R, area_f + 4 * KB)
        ckv_raw = sb_at("ckv_raw", [P, KC, 2 * C], F32, area_c)
        mixed = sb_at("mixed", [P, 2, H], F32, area_b)
        by_cos = sb_at("by_cos", [P, 2, H], F32, area_b + 4 * KB)
        by_sin = sb_at("by_sin", [P, 2, H], F32, area_b + 8 * KB)
        v_tile = sb_at("v_tile", [P, 2, NH, 64], F32, area_a + 32 * KB)
        q_stacks, k_stacks, v_stacks = {}, {}, {}
        v_at = [area_c, area_c + 2 * KB, area_c + 4 * KB, area_c + 6 * KB, area_f, area_f + 2 * KB]
        for kind, n_k in (("self", L), ("cross", M)):
            size = (2 * L + 2 * n_k) * 4
            q_stacks[kind] = [sb_at(f"q_{kind}{s}", [P, 2, L], F32R, area_a + s * size) for s in range(SLOTS[kind])]
            k_stacks[kind] = [sb_at(f"k_{kind}{s}", [P, 2, n_k], F32R, area_a + s * size + 2 * L * 4) for s in range(SLOTS[kind])]
            v_stacks[kind] = [sb_at(f"v_{kind}{s}", [P, 512], F32, v_at[s]) for s in range(SLOTS[kind])]
        probs = sb_at("probs", [P, 4, 2, L], F32, area_b)
        heads_out = sb_at("heads_out", [P, TB, H], F32, area_c + 8 * KB)
        cheads_out = sb_at("cheads_out", [P, TB, C], F32, area_c + 8 * KB)
        cq_raw = sb_at("cq_raw", [P, KH, C], F32, area_e)
        cq_hi = sb_at("cq_hi", [P, KH, C], F32R, area_e + 4 * KB)
        cq_lo = sb_at("cq_lo", [P, KH, C], F32R, area_e + 8 * KB)
        cd_raw = sb_at("cd_raw", [P, KC, H], F32, area_e + 12 * KB)
        cd_hi = sb_at("cd_hi", [P, KC, H], F32R, area_f)
        cd_lo = sb_at("cd_lo", [P, KC, H], F32R, area_f + 4 * KB)
        pv_out = xs
        odd_sum = sb_at("odd_sum", [P, 2, TB, 2, CHD + 1], F32, area_c + 12 * KB)
        half_max = sb_at("half_max", [P, 2, 2, TB, 2], F32, area_c + 14 * KB)
        ff_words = KH * 2 * FS[0] + 3 * H
        ff_hi = [sb_at(f"ff_hi{s}", [P, ff_words], F32R, slot_at[s]) for s in range(2)]
        ff_lo = [sb_at(f"ff_lo{s}", [P, ff_words], F32R, slot_at[s] + 18 * KB) for s in range(2)]
        ff_raw = [sb_at(f"ff_raw{s}", [P, ff_words], F32, [area_e, area_a + 36 * KB][s]) for s in range(2)]
        silu_g = sb_at("silu_g", [P, 2, FS[0]], F32, area_c)
        hid = sb_at("hid", [P, 2, FS[0]], F32, area_c + 3 * KB)
        hidT_hi = sb_at("hidT_hi", [P, 2, 3, P], F32R, area_c + 6 * KB)
        hidT_lo = sb_at("hidT_lo", [P, 2, 3, P], F32R, area_c + 9 * KB)
        wg_raw = sb_at("wg_raw", [P, KH, 2 * H], F32, area_e)
        wm_raw = sb_at("wm_raw", [P, KH, C], F32, area_f)
        wgT_hi = sb_at("wgT_hi", [P, 2 * KH, H], F32R, area_d)
        wgT_lo = sb_at("wgT_lo", [P, 2 * KH, H], F32R, area_d + 16 * KB)
        qm_hi = sb_at("qm_hi", [P, KC, B * L], F32R, area_d + 8 * KB)
        qm_lo = sb_at("qm_lo", [P, KC, B * L], F32R, area_d + 24 * KB)
        mem = [area_a]

        def mem_at(name, shape, dt, cursor=mem):
            t = sb_at(name, shape, dt, cursor[0])
            cursor[0] += int(np.prod(shape[1:])) * 4
            return t

        mcT_hi = mem_at("mcT_hi", [P, KC, B * M], F32R)
        mcT_lo = mem_at("mcT_lo", [P, KC, B * M], F32R)
        mc_hi = mem_at("mc_hi", [P, MT, C], F32R)
        mc_lo = mem_at("mc_lo", [P, MT, C], F32R)
        mc_raw = mem_at("mc_raw", [P, MT, C], F32)
        wm_hi = mem_at("wm_hi", [P, KH, C], F32R)
        wm_lo = mem_at("wm_lo", [P, KH, C], F32R)
        wmT_hi = mem_at("wmT_hi", [P, KC, H], F32R)
        wmT_lo = mem_at("wmT_lo", [P, KC, H], F32R)
        G_hi = mem_at("G_hi", [P, KC, H], F32R)
        G_lo = mem_at("G_lo", [P, KC, H], F32R)
        assert mem[0] <= area_d, (mem[0], area_d)
        mem2 = [area_e]
        attn = mem_at("attn", [P, 2, M], F32, mem2)
        attnT_hi = mem_at("attnT_hi", [P, MT, P], F32R, mem2)
        attnT_lo = mem_at("attnT_lo", [P, MT, P], F32R, mem2)
        am = mem_at("am", [P, C], F32, mem2)
        amT_hi = mem_at("amT_hi", [P, KC, P], F32R, mem2)
        assert mem2[0] <= area_f, (mem2[0], area_f)
        amT_lo = sb_at("amT_lo", [P, KC, P], F32R, area_f + 4 * KB)

        def ps(name, shape):
            return ctx.enter_context(nc.psum_tensor(name, shape, F32))

        banks = [ps("work0", [P, H]), ps("work1", [P, H]), ps("pair0", [P, 2, H]), ps("pair1", [P, 2, H]),
                 ps("acc0", [P, H]), ps("acc1", [P, H])]
        W0, W1, PR0, PR1, A0, A1, H0, H1, H2, H3 = range(10)
        banks += [pair[:, i, :] for pair in banks[PR0:PR1 + 1] for i in range(2)]
        shared = {PR0: (H0, H1), PR1: (H2, H3), H0: (PR0,), H1: (PR0,), H2: (PR1,), H3: (PR1,)}
        bank_filled = [sem(f"bank_filled{i}") for i in range(10)]
        bank_freed = [sem(f"bank_freed{i}") for i in range(10)]
        fills = [0] * 10
        other_seen = {}
        filled_as = {}

        def claim(pe, product, place_):
            n = fills[place_]
            fills[place_] += 1
            assert product not in filled_as, product
            filled_as[product] = (place_, n)
            if n:
                pe.wait_ge(bank_freed[place_], n)
            for other in shared.get(place_, ()):
                if fills[other] > other_seen.get((place_, other), 0):
                    other_seen[(place_, other)] = fills[other]
                    pe.wait_ge(bank_freed[other], fills[other])
            return banks[place_]

        def fill_done(mm, product):
            mm.then_inc(bank_filled[filled_as[product][0]], 1)

        def wait_filled(eng, product):
            place_, n = filled_as[product]
            eng.wait_ge(bank_filled[place_], n + 1)
            return banks[place_]

        def wait_used(eng, *last_two):
            for product in last_two:
                wait_filled(eng, product)

        def free(ins, product):
            ins.then_inc(bank_freed[filled_as[product][0]], 1)

        def wait_emptied(eng, product):
            place_, n = filled_as[product]
            eng.wait_ge(bank_freed[place_], n + 1)

        consts_ready = sem("consts_ready")
        rot_ready = sem("rot_ready")
        small_in = sem("small_in")
        masks_ready = sem("masks_ready")
        vision_counted = sem("vision_counted")
        w_row_in = sem("w_row_in")
        ctx_in_s = [sem(f"ctx_in{i}") for i in range(4)]
        x_in = [sem(f"x_in{t}") for t in range(T)]
        raw_in = [sem(f"raw_in{i}") for i in range(2)]
        weights_ready = [sem(f"weights_ready{i}") for i in range(2)]
        high_copied = [sem(f"high_copied{i}") for i in range(2)]
        v_raw_in = [sem(f"v_raw_in{i}") for i in range(2 * KH)]
        ckv_in = sem("ckv_in")
        ckv_ready = sem("ckv_ready")
        small_w_in = sem("small_w_in")
        small_w_ready = sem("small_w_ready")
        hi_done = sem("hi_done")
        stage_out = [sem(f"stage_out{i}") for i in range(2)]
        v_out = [sem(f"v_out{i}") for i in range(2)]
        squares_done = sem("squares_done")
        rstd_done = sem("rstd_done")
        xs_done = sem("xs_done")
        by_sin_done = sem("by_sin_done")
        rotated = sem("rotated")
        stack_in = [sem(f"stack_in{i}") for i in range(SLOTS["self"])]
        rows_in = [sem(f"rows_in{i}") for i in range(SLOTS["self"])]
        parts_done = sem("parts_done")
        max_row_ready = sem("max_row_ready")
        values_done = sem("values_done")
        heads_done = sem("heads_done")
        stack_set = sem("stack_set")
        silu_done = sem("silu_done")
        hid_done = sem("hid_done")
        pool_chain = sem("pool_chain")
        dve_chain = sem("dve_chain")
        lmem_in = sem("lmem_in")
        nmax_done = sem("nmax_done")
        exp_done = sem("exp_done")
        gate_in = sem("gate_in")
        gate_done = sem("gate_done")
        wm_hi_done = sem("wm_hi_done")
        wm_ready = sem("wm_ready")
        mc_in = sem("mc_in")
        mc_hi_done = sem("mc_hi_done")
        mc_ready = sem("mc_ready")
        am_done = sem("am_done")
        fused_done = sem("fused_done")
        row_done = sem("row_done")
        result_out = [sem(f"result_out{i}") for i in range(2)]
        next_zeroed = sem("next_zeroed")

        staged = [("rotT", c, t) for c in ("k", "q") for t in range(T)]
        staged += [("kT", n, m) for n in range(B * M // L) for m in range(KC)]
        staged += [("cqT", b, m) for b in range(B) for m in range(KC)]
        stage_no = {k: i for i, k in enumerate(staged)}
        hi_no = {}
        ff_cuts = [(e, f) for e in range(2) for f in range(len(FS))]
        slot_of, slot_uses = {}, [0] * SLOTS["self"]
        for kind in ("self", "cross"):
            for u in range(UNITS):
                s = u % SLOTS[kind]
                slot_of[(kind, u)] = (s, slot_uses[s])
                slot_uses[s] += 1
        ZERO_ORDER = [(3, 11), (0, 13), (1, 14), (2, 15)]
        zeroed_at = {s: SLOTS["self"] + i + 1 for i, (s, _) in enumerate(ZERO_ORDER)}
        EXPERT_PLACES = [(A0, A1), (PR0, PR1)]
        FF_TILES = [list(range(T)), [b * TB + i for i in reversed(range(TB)) for b in range(B)]]
        FF_ITEMS = [(e, f, t) for e, f in ff_cuts for t in FF_TILES[e]]
        FF_GROUPS = [range(0, len(FS) * T)]
        for c in range(len(FS), 2 * len(FS)):
            FF_GROUPS += [range(c * T, c * T + B), range(c * T + B, (c + 1) * T)]
        ff_fills = {}
        BY_VECTOR = ff_cuts[len(FS) + 1:]
        QKV = ("v", "k", "q")
        ROTATED = [(c, t) for c in ("k", "q") for t in range(T)]
        CQ_STEPS = [(b + 1) * TB + 2 for b in range(B)]
        uses = [0, 0]
        cut_at = {}
        for c in ["v", "k", "q", "dense"] + ff_cuts:
            s = {"v": 0, "k": 1, "q": 0, "dense": 0}.get(c, None) if isinstance(c, str) else ff_cuts.index(c) % 2
            cut_at[c] = (s, uses[s])
            uses[s] += 1

        raw_count, loaded = {}, [16 * (2 + 2 * KH), 16 * 2]
        for e, f in ff_cuts:
            loaded[cut_at[(e, f)][0]] += 16 * (4 if FS[f] % P else 3)
            raw_count[(e, f)] = loaded[cut_at[(e, f)][0]]

        def weight_pieces(cut):
            s = cut_at[cut][0]
            if isinstance(cut, str):
                return [(qkv_hi[s][:, e, k, :], qkv_lo[s][:, e, k, :], qkv_raw[s][:, e, k, :])
                        for e in range(2) for k in range(KH)]
            fw = FS[cut[1]]
            a = KH * 2 * fw
            ends = [(P, 0, a // 2), (P, a // 2, a), (P, a, a + fw // P * H)]
            if fw % P:
                ends.append((fw % P, a + fw // P * H, a + (fw // P + 1) * H))
            return [(ff_hi[s][0:n, c0:c1], ff_lo[s][0:n, c0:c1], ff_raw[s][0:n, c0:c1]) for n, c0, c1 in ends]

        pieces, copies = [0, 0], [0, 0]
        split_count, copy_before = {}, {}
        for c in cut_at:
            s, n = cut_at[c][0], len(weight_pieces(c))
            pieces[s] += n
            split_count[c] = pieces[s]
            if c not in ("dense", ff_cuts[0]):
                copy_before[c] = copies[s]
                copies[s] += n

        def split_pieces(group, n):
            c, i = divmod(n, T)
            if c + 1 == len(ff_cuts) or len(group) == T - B:
                return []
            number = len(weight_pieces(ff_cuts[c + 1]))
            if len(group) == B:
                now = {0: [0], 1: [1], 2: list(range(2, number))}.get(n - group.start, [])
            else:
                now = [i - 2] if 2 <= i < 2 + number and n < group.stop else []
            return [(ff_cuts[c + 1], i) for i in now]

        def wait_weights(eng, cut, later=0):
            eng.wait_ge(weights_ready[cut_at[cut][0]], split_count[cut] - later)

        self_steps = attention_steps(TB)
        cross_steps = attention_steps(MT)

        def three(pe, acc, stat, mov, first, last):
            s_hi, s_lo = stat
            m_hi, m_lo = mov
            pe.matmul(acc, s_hi, m_hi, start=first, stop=False)
            pe.matmul(acc, s_hi, m_lo, start=False, stop=False)
            return pe.matmul(acc, s_lo, m_hi, start=False, stop=last)

        def load_counts(eng):
            return [eng.value_load(vision_count[0:1, t:t + 1], min_val=0, max_val=B * L) for t in range(T + 1)]

        def fill_skipped(pe, product):
            pe.sem_inc(bank_filled[filled_as[product][0]], 1)

        def free_skipped(eng, product):
            eng.sem_inc(bank_freed[filled_as[product][0]], 1)

        def both(hi, lo, *key):
            return hi[key], lo[key]

        block = ctx.enter_context(nc.Block())

        @block.tensor
        def _(pe):
            pe.wait_ge(consts_ready, 1)
            def turn_act(stage, t):
                pe.wait_ge(xs_done, turn_no[(stage, t)] + 1)
                acc = claim(pe, ("actT", stage, t), t % 2)
                for k in range(KH):
                    mm = pe.transpose(acc[:, k * P:(k + 1) * P], xs[:, t % 2, k * P:(k + 1) * P], ident[:, :])
                fill_done(mm, ("actT", stage, t))

            pe.wait_ge(consts_ready, 3)
            pe.wait_ge(masks_ready, 1)
            acc = claim(pe, ("vision_count",), A1)
            fill_done(pe.matmul(acc[0:1, 0:T], minus_half[:, :], is_v[:, :], start=True, stop=True), ("vision_count",))
            turn_act("in", 0)
            turn_act("in", 1)
            pe.wait_ge(vision_counted, 1)
            vision = load_counts(pe)
            turn_act("in", 2)

            def turn_rotated(c, t):
                pe.wait_ge(rotated, {"k": 0, "q": T}[c] + t + 1)
                acc = claim(pe, ("rotT", c, t), t % 2)
                for k in range(KH):
                    mm = pe.transpose(acc[:, k * P:(k + 1) * P], by_cos[:, t % 2, k * P:(k + 1) * P], ident[:, :])
                fill_done(mm, ("rotT", c, t))

            def expert_product(product, t, e, s):
                acc = claim(pe, product, EXPERT_PLACES[e][t % 2])
                if e:
                    acc = acc[:, 0, :]

                def multiply():
                    for k in range(KH):
                        mm = three(pe, acc[:, :], both(actT_hi, actT_lo, slice(None), k, slice(t * P, (t + 1) * P)),
                                   both(qkv_hi[s], qkv_lo[s], slice(None), e, k, slice(None)), k == 0, k == KH - 1)
                    fill_done(mm, product)

                if e == 0:
                    multiply()
                else:
                    with pe.If(vision[t] > 0):
                        wait_weights(pe, product[1] if product[0] == "qkv" else "dense")
                        multiply()
                    with pe.Else():
                        fill_skipped(pe, product)

            for c in QKV:
                s = cut_at[c][0]
                for t in range(T):
                    if c == "v":
                        wait_emptied(pe, ("actT", "in", t))
                    if t == 0:
                        wait_weights(pe, c, KH)
                    for e in range(2):
                        expert_product(("qkv", c, t, e), t, e, s)
                    if c == "v" and 1 <= t < T - 2:
                        turn_act("in", t + 2)
                    if c != "v" and ROTATED.index((c, t)) >= 2:
                        turn_rotated(*ROTATED[ROTATED.index((c, t)) - 2])
            for c, t in ROTATED[-2:]:
                turn_rotated(c, t)

            for u in range(B * MT):
                pe.wait_ge(ctx_in_s[u // 4], 16)
                acc = claim(pe, ("ctxT", u), u % 2)
                for k in range(KC):
                    mm = pe.transpose(acc[:, k * P:(k + 1) * P], ctx_tile[:, u, k * P:(k + 1) * P], ident[:, :])
                fill_done(mm, ("ctxT", u))
            pe.wait_ge(ckv_ready, 1)
            for n in range(B * M // L):
                for u in range(4 * n + 2, 4 * n + 4):
                    wait_emptied(pe, ("ctxT", u))
                for m in range(KC):
                    acc = claim(pe, ("kT", n, m), (A0, A1)[m])
                    for k in range(KC):
                        mm = three(pe, acc[:, :], both(ckv_hi, ckv_lo, slice(None), k, slice(m * P, (m + 1) * P)),
                                   both(ctxT_hi, ctxT_lo, slice(None), k, slice(n * L, (n + 1) * L)), k == 0, k == KC - 1)
                    fill_done(mm, ("kT", n, m))
            for u in range(B * MT):
                acc = claim(pe, ("cv", u), (PR0, PR1)[u % 2])
                for k in range(KC):
                    mm = three(pe, acc[:, 0, 0:C], both(ctxT_hi, ctxT_lo, slice(None), k, slice(u * P, (u + 1) * P)),
                               both(ckv_hi, ckv_lo, slice(None), k, slice(C, 2 * C)), k == 0, k == KC - 1)
                fill_done(mm, ("cv", u))

            work = [0]

            def work_bank():
                work[0] += 1
                return (W0, W1, A1, H0)[work[0] % 4]

            def attend(kind, steps, per_unit):
                causal = kind == "self"
                for todo in steps:
                    for what, u, r in todo:
                        slot, use = slot_of[(kind, u)]
                        qs, ks, vs = q_stacks[kind][slot], k_stacks[kind][slot], v_stacks[kind][slot]
                        if what == "scores":
                            if r == 0:
                                pe.wait_ge(stack_in[slot], 16 * 7 * (use + 1))
                                if u < SLOTS[kind]:
                                    pe.wait_ge(stack_set, slot + 1 if causal else zeroed_at[slot])
                            for n in (2 * r, 2 * r + 1):
                                if causal:
                                    j, i = divmod(n, TB)
                                    product = (kind, "S", u, j, i)
                                    acc = claim(pe, product, work_bank())
                                    width = max(256, (i + 1) * P)
                                    pe.matmul(acc[:, 0:width], qs[0:ONES, j, i * P:(i + 1) * P], ks[0:ONES, j, 0:width],
                                              start=True, stop=True)
                                    mm = pe.matmul(acc[:, i * P:(i + 1) * P], ident_bf[:, :], hide_s[:, :],
                                                   start=False, stop=True, skip_group_check=True)
                                else:
                                    j, i, h = n // (2 * TB), n // 2 % TB, n % 2
                                    product = (kind, "S", u, j, i, h)
                                    acc = claim(pe, product, work_bank())
                                    mm = pe.matmul(acc[:, :], qs[0:ONES, j, i * P:(i + 1) * P],
                                                   ks[0:ONES, j, h * L:(h + 1) * L], start=True, stop=True)
                                fill_done(mm, product)
                        elif what == "max_rows":
                            pe.wait_ge(parts_done, u + 1 + (0 if causal else UNITS))
                            product = (kind, "max_rows", u)
                            acc = claim(pe, product, work_bank())
                            for i in range(TB):
                                mm = pe.transpose(acc[0:4, i * P:(i + 1) * P], max_parts[:, u % 2, i, :].bitcast(F32), ident[:, :])
                            fill_done(mm, product)
                        elif what == "probs":
                            if r == 0:
                                pe.wait_ge(rows_in[slot], 16 * 2 * (use + 1))
                            for j in range(2):
                                product = (kind, "T", u, r, j)
                                acc = claim(pe, product, (H1, H2, H3)[(2 * (u * per_unit + r) + j) % 3])
                                first = min(r * P, L - 256) if causal else 0
                                mm = pe.matmul(acc[:, first:L], ks[0:ONES + 2, j, r * P:(r + 1) * P],
                                               qs[0:ONES + 2, j, first:L], start=True, stop=True)
                                if causal:
                                    mm = pe.matmul(acc[:, r * P:(r + 1) * P], ident_bf[:, :], hide_t[:, :],
                                                   start=False, stop=True, skip_group_check=True)
                                fill_done(mm, product)
                        elif what == "values":
                            product = (kind, "PV", u)
                            if r == 0:
                                claim(pe, product, A0)
                            acc = banks[A0]
                            for j in range(2):
                                wait_emptied(pe, (kind, "T", u, r, j))
                            n = u * per_unit + r
                            if causal:
                                for j in range(2):
                                    mm = pe.matmul(acc[j * 64:(j + 1) * 64, r * P:L],
                                                   vs[:, (2 * r + j) * 64:(2 * r + j + 1) * 64],
                                                   probs[:, n % 4, j, r * P:L], start=(r == 0), stop=(r == per_unit - 1))
                            elif r % 2:
                                for j in range(2):
                                    for h in range(2):
                                        mm = pe.matmul(acc[(2 * j + h) * 32:(2 * j + h + 1) * 32, :],
                                                       vs[:, (2 * (r - 1 + h) + j) * 32:(2 * (r - 1 + h) + j + 1) * 32],
                                                       probs[:, (n - 1 + h) % 4, j, :], start=(r == 1), stop=(r == per_unit - 1))
                            if r == per_unit - 1:
                                fill_done(mm, product)
                            elif causal or r % 2:
                                mm.then_inc(values_done, 1)
                        elif what == "turn_back":
                            wait_emptied(pe, (kind, "PV", u))
                            product = (kind, "PVT", u)
                            acc = claim(pe, product, work_bank())
                            for i in range(TB):
                                mm = pe.transpose(acc[:, i * P:(i + 1) * P], pv_out[:, u % 2, i * P:(i + 1) * P], ident[:, :])
                            fill_done(mm, product)
                        elif what == "context":
                            src, nk = (heads_out, KH) if causal else (cheads_out, KC)
                            pe.wait_ge(heads_done, (u + 1) * PAIRS + (0 if causal else UNITS))
                            for i in range(TB):
                                product = (kind, "ctxT", u, i)
                                acc = claim(pe, product, work_bank())
                                for k in range(nk):
                                    mm = pe.transpose(acc[:, k * P:(k + 1) * P], src[:, i, k * P:(k + 1) * P], ident[:, :])
                                fill_done(mm, product)

            attend("self", self_steps, TB)

            wait_weights(pe, "dense")
            s = cut_at["dense"][0]
            for n in range(T + 3):
                if n < T:
                    wait_emptied(pe, ("self", "ctxT", n // TB, n % TB))
                    for e in range(2):
                        expert_product(("dense", n, e), n, e, s)
                if 2 <= n < T + 2:
                    turn_act("cross", n - 2)
                if n in CQ_STEPS:
                    b = CQ_STEPS.index(n)
                    pe.wait_ge(small_w_ready, 1)
                    for t in range((b + 1) * TB - 2, (b + 1) * TB):
                        wait_emptied(pe, ("actT", "cross", t))
                    for m in range(KC):
                        acc = claim(pe, ("cqT", b, m), (PR0, PR1)[m])
                        for k in range(KH):
                            mm = three(pe, acc[:, 0, :], both(cq_hi, cq_lo, slice(None), k, slice(m * P, (m + 1) * P)),
                                       both(actT_hi, actT_lo, slice(None), k, slice(b * L, (b + 1) * L)), k == 0, k == KH - 1)
                        fill_done(mm, ("cqT", b, m))

            attend("cross", cross_steps, MT)

            pe.wait_ge(small_w_ready, 2)
            for n in range(T + 3):
                if n < T:
                    wait_emptied(pe, ("cross", "ctxT", n // TB, n % TB))
                    acc = claim(pe, ("cdense", n), (A0, A1)[n % 2])
                    for k in range(KC):
                        mm = three(pe, acc[:, :], both(actT_hi, actT_lo, slice(None), k, slice(n * P, (n + 1) * P)),
                                   both(cd_hi, cd_lo, slice(None), k, slice(None)), k == 0, k == KC - 1)
                    fill_done(mm, ("cdense", n))
                if n >= 3:
                    turn_act("mlp", n - 3)

            def gate_up(product, acc, e, f, t):
                fw, s = FS[f], cut_at[(e, f)][0]
                parts = [(acc[:, 0, 0:fw], 0, fw), (acc[:, 1, 0:fw], fw, fw)] if fw >= 256 else [(acc[:, 0, 0:2 * fw], 0, 2 * fw)]
                for dst, c0, w in parts:
                    for k in range(KH):
                        cols = slice(k * 2 * fw + c0, k * 2 * fw + c0 + w)
                        mm = three(pe, dst, both(actT_hi, actT_lo, slice(None), k, slice(t * P, (t + 1) * P)),
                                   both(ff_hi[s], ff_lo[s], slice(None), cols), k == 0, k == KH - 1)
                fill_done(mm, product)

            def turn_hid(product, acc, f, slot):
                for k in range((FS[f] + P - 1) // P):
                    w = min(P, FS[f] - k * P)
                    mm = pe.transpose(acc[0:w, k * P:(k + 1) * P], hid[:, slot, k * P:k * P + w], ident[:, :])
                fill_done(mm, product)

            def down(product, acc, e, f, slot):
                s = cut_at[(e, f)][0]
                nk = (FS[f] + P - 1) // P
                for k in range(nk):
                    w = min(P, FS[f] - k * P)
                    cols = slice(KH * 2 * FS[f] + k * H, KH * 2 * FS[f] + (k + 1) * H)
                    mm = three(pe, acc[:, :], (hidT_hi[0:w, slot, k, :], hidT_lo[0:w, slot, k, :]),
                               (ff_hi[s][0:w, cols], ff_lo[s][0:w, cols]), k == 0, k == nk - 1)
                fill_done(mm, product)

            items = FF_ITEMS

            def feed_forward(group):
                for n in range(group.start, group.stop + 2):
                    if n < group.stop:
                        e, f, t = items[n]
                        if n % T == 0:
                            wait_weights(pe, (e, f))
                        if e == 0 and f == 0:
                            wait_emptied(pe, ("actT", "mlp", t))
                        product = ("gu", e, f, t)
                        acc = claim(pe, product, (PR0, PR1)[n % 2])
                        if e == 0:
                            gate_up(product, acc, e, f, t)
                        else:
                            with pe.If(vision[t] > 0):
                                gate_up(product, acc, e, f, t)
                            with pe.Else():
                                fill_skipped(pe, product)
                    if group.start < n <= group.stop:
                        e, f, t = items[n - 1]
                        pe.wait_ge(hid_done, n)
                        product = ("hidT", e, f, t)
                        acc = claim(pe, product, n % 2)
                        if e == 0:
                            turn_hid(product, acc, f, (n - 1) % 2)
                        else:
                            with pe.If(vision[t] > 0):
                                turn_hid(product, acc, f, (n - 1) % 2)
                            with pe.Else():
                                fill_skipped(pe, product)
                    if n >= group.start + 2:
                        e, f, t = items[n - 2]
                        product = ("down", e, f, t)
                        wait_emptied(pe, ("hidT", e, f, t))
                        acc = claim(pe, product, (A0, A1)[n % 2])
                        if e == 0:
                            down(product, acc, e, f, n % 2)
                        else:
                            with pe.If(vision[t] > 0):
                                down(product, acc, e, f, n % 2)
                            with pe.Else():
                                fill_skipped(pe, product)

            for group in FF_GROUPS:
                before = list(fills)
                if len(group) == T - B:
                    with pe.If(vision[T] > 0):
                        feed_forward(group)
                    with pe.Else():
                        for p_ in range(H0):
                            pe.wait_ge(bank_filled[p_], before[p_])
                            pe.sem_inc(bank_filled[p_], fills[p_] - before[p_])
                else:
                    feed_forward(group)
                ff_fills[group] = (before, list(fills))

            pe.wait_ge(lmem_in, 32)
            for g in range(KC + 2 * KH):
                product = ("wT", g)
                acc = claim(pe, product, g % 2)
                src, k = (wm_raw, g) if g < KC else (wg_raw, g - KC)
                for d in range(KH):
                    mm = pe.transpose(acc[:, d * P:(d + 1) * P], src[:, d, k * P:(k + 1) * P], ident[:, :])
                fill_done(mm, product)
            for t in range(T):
                wait_emptied(pe, ("down", 1, len(FS) - 1, t))
                acc = claim(pe, ("hsT", t), t % 2)
                for k in range(KH):
                    mm = pe.transpose(acc[:, k * P:(k + 1) * P], hs[:, t, k * P:(k + 1) * P], ident[:, :])
                fill_done(mm, ("hsT", t))
            pe.wait_ge(wm_ready, 1)
            for g in range(KC + 2 * KH - 2, KC + 2 * KH):
                wait_emptied(pe, ("wT", g))
            for m in range(KC):
                acc = claim(pe, ("G", m), (A0, A1)[m])
                for k in range(KH):
                    mm = three(pe, acc[:, :], both(wm_hi, wm_lo, slice(None), k, slice(m * P, (m + 1) * P)),
                               both(wgT_hi, wgT_lo, slice(None), KH + k, slice(None)), k == 0, k == KH - 1)
                fill_done(mm, ("G", m))
            for b in range(B):
                for t in range((b + 1) * TB - 2, (b + 1) * TB):
                    wait_emptied(pe, ("hsT", t))
                for m in range(KC):
                    acc = claim(pe, ("qm", b, m), (PR0, PR1)[m])
                    for k in range(KH):
                        mm = three(pe, acc[:, 0, :], both(wm_hi, wm_lo, slice(None), k, slice(m * P, (m + 1) * P)),
                                   both(actT_hi, actT_lo, slice(None), k, slice(b * L, (b + 1) * L)), k == 0, k == KH - 1)
                    fill_done(mm, ("qm", b, m))
            def turn_context(b):
                pe.wait_ge(mc_in, 16 * (b + 1))
                for g in range(TB):
                    product = ("mcT", b, g)
                    acc = claim(pe, product, (W0, W1)[g % 2])
                    for k in range(KC):
                        for u in range(2):
                            mm = pe.transpose(acc[:, (2 * k + u) * P:(2 * k + u + 1) * P],
                                              mc_raw[:, 2 * g + u, k * P:(k + 1) * P], ident[:, :])
                    fill_done(mm, product)

            turn_context(0)
            for n in range(T + 2):
                if n < T:
                    b = n // TB
                    if n % TB == 0:
                        for m in range(KC):
                            wait_emptied(pe, ("qm", b, m))
                        for g in range(TB - 2, TB):
                            wait_emptied(pe, ("mcT", b, g))
                    acc = claim(pe, ("ms", n), (PR0, PR1)[n % 2])
                    for h in range(M // L):
                        c0 = b * M + h * L
                        for k in range(KC):
                            mm = three(pe, acc[:, h, :], both(qm_hi, qm_lo, slice(None), k, slice(n * P, (n + 1) * P)),
                                       both(mcT_hi, mcT_lo, slice(None), k, slice(c0, c0 + L)), k == 0, k == KC - 1)
                    fill_done(mm, ("ms", n))
                if n >= 2:
                    pe.wait_ge(am_done, n - 1)
                    acc = claim(pe, ("amT", n - 2), W0)
                    for k in range(KC):
                        mm = pe.transpose(acc[:, k * P:(k + 1) * P], am[:, k * P:(k + 1) * P], ident[:, :])
                    fill_done(mm, ("amT", n - 2))
                if 1 <= n <= T:
                    t = n - 1
                    pe.wait_ge(exp_done, t + 1)
                    for h in range(2):
                        acc = claim(pe, ("attnT", t, h), (W1, W0)[h])
                        for k in range(4):
                            m = 4 * h + k
                            mm = pe.transpose(acc[:, k * P:(k + 1) * P], attn[:, t % 2, m * P:(m + 1) * P], ident[:, :])
                        fill_done(mm, ("attnT", t, h))
                if n >= 2:
                    t = n - 2
                    wait_emptied(pe, ("amT", t))
                    if n == 2:
                        for m in range(KC):
                            wait_emptied(pe, ("G", m))
                    acc = banks[A1]
                    for k in range(KC):
                        mm = three(pe, acc[:, :], both(amT_hi, amT_lo, slice(None), k, slice(None)),
                                   both(G_hi, G_lo, slice(None), k, slice(None)), False, k == KC - 1)
                    fill_done(mm, ("gate", t))
                    acc = claim(pe, ("mctx", t), W1)
                    for k in range(KC):
                        mm = three(pe, acc[:, :], both(amT_hi, amT_lo, slice(None), k, slice(None)),
                                   both(wmT_hi, wmT_lo, slice(None), k, slice(None)), k == 0, k == KC - 1)
                    fill_done(mm, ("mctx", t))
                if 1 <= n <= T:
                    t = n - 1
                    acc = claim(pe, ("gate", t), A1)
                    for k in range(KH):
                        three(pe, acc[:, :], both(actT_hi, actT_lo, slice(None), k, slice(t * P, (t + 1) * P)),
                              both(wgT_hi, wgT_lo, slice(None), k, slice(None)), k == 0, False)
                    pe.wait_ge(mc_ready, t // TB + 1)
                    acc = claim(pe, ("am", t), A0)
                    for m in range(MT):
                        if m % 4 == 0:
                            wait_emptied(pe, ("attnT", t, m // 4))
                        mm = three(pe, acc[:, 0:C], both(attnT_hi, attnT_lo, slice(None), m, slice(None)),
                                   both(mc_hi, mc_lo, slice(None), m, slice(None)), m == 0, m == MT - 1)
                    fill_done(mm, ("am", t))
                if n == TB - 2:
                    turn_context(1)

        @block.scalar
        def _(act):
            def hi_part(product, dst, src_of):
                acc = wait_filled(act, product)
                hi_no[product] = len(hi_no) + 1
                act.activation(dst, src_of(acc), ACT.Copy).then_inc(hi_done, 1)

            def tiles(acc, n=KH):
                return acc[:, 0:n * P].rearrange("p (k t) -> p k t", k=n)

            def staged_hi(product, src_of=lambda a: a[:, :]):
                z = stage_no[product]
                if z >= 2:
                    act.wait_ge(stage_out[z % 2], 32 * (z // 2))
                hi_part(product, stage_hi[:, z % 2, :], src_of)

            def squares(stage, t, product):
                if product is None:
                    act.wait_ge(x_in[t], 16)
                else:
                    wait_emptied(act, product)
                before = NORMS.index(stage) * T + t
                if before:
                    act.wait_ge(squares_done, before)
                act.activation(square_out[:, :], hs[:, t, :], ACT.Square,
                               accum_out=sum_sq[:, NORMS.index(stage), t:t + 1]).then_inc(squares_done, 1)

            def act_hi(product, t, n=KH):
                hi_part(product, actT_hi[:, 0:n, t * P:(t + 1) * P], lambda a: tiles(a, n))

            def copy_high(cut, i=None):
                s = cut_at[cut][0]
                for hi, lo, raw in weight_pieces(cut)[slice(None) if i is None else slice(i, i + 1)]:
                    act.activation(hi, raw, ACT.Copy).then_inc(high_copied[s], 1)

            with nc.allow_non_contiguous_dma(reason="one small column per token tile"):
                act.wait_ge(next_zeroed, 1)
                act.dma_start(pos_i[:, :], pos.rearrange("a (i p) -> p (a i)", p=P)).then_inc(small_in, 16)
                act.dma_start(tt_now[:, :], tt.rearrange("b (i p) -> p (b i)", p=P)).then_inc(small_in, 16)
                shifted = tt.rearrange("b (i p) -> p b i", p=P)
                act.dma_start(tt_next[0:P - 1, :].rearrange("p (b i) -> p b i", b=B), shifted[1:P, :, :]).then_inc(small_in, 16)
                for b in range(B):
                    act.dma_start(tt_next[P - 1:P, b * TB:(b + 1) * TB - 1], shifted[0:1, b, 1:TB]).then_inc(small_in, 16)

            def copy_v(e):
                for k in range(KH):
                    act.wait_ge(v_raw_in[e * KH + k], 16)
                    copy_high("v", e * KH + k)

            squares("in", 0, None)
            squares("in", 1, None)
            copy_v(0)
            for t in range(3):
                act_hi(("actT", "in", t), t)
                if t < 2:
                    squares("in", t + 2, None)
            copy_v(1)
            for t in range(3, T):
                if t + 1 < T:
                    squares("in", t + 1, None)
                act_hi(("actT", "in", t), t)
                if t >= TB:
                    if t == TB:
                        act.wait_ge(raw_in[1], 32)
                    copy_high("k", 2 * (t - TB))
                    copy_high("k", 2 * (t - TB) + 1)
            act.wait_ge(vision_counted, 1)
            vision = load_counts(act)
            for c in ("k", "q"):
                for t in range(T):
                    if c == "k" and t < 4:
                        if t == 0:
                            wait_used(act, ("qkv", "v", T - 1, 0), ("qkv", "v", T - 1, 1))
                            act.wait_ge(raw_in[0], 32)
                        copy_high("q", 2 * t)
                        copy_high("q", 2 * t + 1)
                    staged_hi(("rotT", c, t))
            for u in range(B * MT):
                hi_part(("ctxT", u), ctxT_hi[:, :, u * P:(u + 1) * P], lambda a: tiles(a, KC))
            for n in range(B * M // L):
                for m in range(KC):
                    staged_hi(("kT", n, m))

            def attend(kind, steps, per_unit):
                causal = kind == "self"
                scale = 1.0 / np.sqrt(HD if causal else CHD)
                for todo in steps:
                    for what, u, r in todo:
                        if what == "max_rows":
                            acc = wait_filled(act, (kind, "max_rows", u))
                            v = u + (0 if causal else UNITS)
                            if v == 0:
                                for i in range(2):
                                    act.wait_ge(stage_out[i], 32 * ((stage_no[("kT", B * M // L - 1, KC - 1)] + 1) // 2))
                            if v == UNITS:
                                act.wait_ge(stage_out[0], 32 * (len(staged) // 2))
                                act.wait_ge(stage_out[1], 32 * (len(staged) // 2))
                            if v >= 2:
                                slot, use = slot_of[("self" if v - 2 < UNITS else "cross", (v - 2) % UNITS)]
                                act.wait_ge(rows_in[slot], 32 * (use + 1))
                            free(act.activation(stage_hi[0:4, v % 2, :], acc[0:4, :], ACT.Copy), (kind, "max_rows", u))
                        elif what == "probs":
                            n = u * per_unit + r
                            if n >= 4:
                                lu, lr = divmod(n - 4, per_unit)
                                lr = lr if causal else lr // 2
                                if lr == 3:
                                    wait_filled(act, (kind, "PV", lu))
                                else:
                                    act.wait_ge(values_done, 3 * (lu + (0 if causal else UNITS)) + lr + 1)
                            first = r * P if causal else 0
                            for j in range(2):
                                acc = wait_filled(act, (kind, "T", u, r, j))
                                free(act.activation(probs[:, n % 4, j, first:L], acc[:, first:L], ACT.Exp, scale=scale),
                                     (kind, "T", u, r, j))
                        elif what == "values" and r == per_unit - 1:
                            acc = wait_filled(act, (kind, "PV", u))
                            if u >= 2:
                                wait_filled(act, (kind, "PVT", u - 2))
                            free(act.activation(pv_out[:, u % 2, :], acc[:, :], ACT.Copy), (kind, "PV", u))
                        elif what == "context":
                            for i in range(TB):
                                act_hi((kind, "ctxT", u, i), u * TB + i, KH if causal else KC)

            attend("self", self_steps, TB)
            for n in range(T + 3):
                if 2 <= n < T + 2:
                    act_hi(("actT", "cross", n - 2), n - 2)
                if n < T:
                    squares("cross", n, ("dense", n, 1))
                if n in CQ_STEPS:
                    b = CQ_STEPS.index(n)
                    if b == 0:
                        for v in (UNITS - 2, UNITS - 1):
                            slot, use = slot_of[("self", v)]
                            act.wait_ge(rows_in[slot], 32 * (use + 1))
                    for m in range(KC):
                        staged_hi(("cqT", b, m), lambda a: a[:, 0, :])
            attend("cross", cross_steps, MT)
            for n in range(T + 3):
                if n >= 3:
                    act_hi(("actT", "mlp", n - 3), n - 3)
                if n < T:
                    squares("mlp", n, ("cdense", n))

            items = FF_ITEMS

            def feed_forward(group):
                for n in range(group.start, group.stop + 1):
                    if n < group.stop:
                        e, f, t = items[n]
                        acc = wait_filled(act, ("gu", e, f, t))
                        if n >= 2:
                            act.wait_ge(hid_done, n - 1)
                        def silu():
                            act.activation(silu_g[:, n % 2, 0:FS[f]], acc[:, 0, 0:FS[f]], ACT.Silu).then_inc(silu_done, 1)

                        if e == 0:
                            silu()
                        else:
                            with act.If(vision[t] > 0):
                                silu()
                            with act.Else():
                                act.wait_ge(silu_done, n)
                                act.sem_inc(silu_done, 1)
                    if n > group.start:
                        e, f, t = items[n - 1]
                        product = ("hidT", e, f, t)
                        if n >= 3:
                            e0, f0, t0 = items[n - 3]
                            wait_filled(act, ("down", e0, f0, t0))
                        acc = wait_filled(act, product)
                        nk = (FS[f] + P - 1) // P
                        hi_no[product] = len(hi_no) + 1
                        full = FS[f] // P

                        def hid_hi():
                            ins = act.activation(hidT_hi[:, (n - 1) % 2, 0:full, :], tiles(acc, full), ACT.Copy)
                            if nk > full:
                                w = FS[f] - full * P
                                ins = act.activation(hidT_hi[0:w, (n - 1) % 2, full, :], acc[0:w, full * P:(full + 1) * P], ACT.Copy)
                            ins.then_inc(hi_done, 1)

                        if e == 0:
                            hid_hi()
                        else:
                            with act.If(vision[t] > 0):
                                hid_hi()
                            with act.Else():
                                act.wait_ge(hi_done, hi_no[product] - 1)
                                act.sem_inc(hi_done, 1)
                    for nxt, i in split_pieces(group, n):
                        if i == 0:
                            c = ff_cuts.index(nxt) - 1
                            act.wait_ge(raw_in[cut_at[nxt][0]], raw_count[nxt])
                            if c == 0:
                                wait_filled(act, ("cross", "PV", UNITS - 1))
                            else:
                                wait_used(act, *[("down", *item) for item in FF_ITEMS[c * T - 2:c * T]])
                        copy_high(nxt, i)

            for group in FF_GROUPS:
                if len(group) == T - B:
                    no = len(hi_no)
                    with act.If(vision[T] > 0):
                        feed_forward(group)
                    with act.Else():
                        act.wait_ge(silu_done, group.start)
                        act.sem_inc(silu_done, len(group))
                        act.wait_ge(hi_done, no)
                        act.sem_inc(hi_done, len(group))
                else:
                    feed_forward(group)

            for g in range(KC + 2 * KH):
                dst = wmT_hi[:, g, :] if g < KC else wgT_hi[:, g - KC, :]
                hi_part(("wT", g), dst, lambda a: a[:, :])
            act.activation(wm_hi[:, :, :], wm_raw[:, :, :], ACT.Copy).then_inc(wm_hi_done, 1)
            for t in range(T):
                act_hi(("hsT", t), t)
            for m in range(KC):
                hi_part(("G", m), G_hi[:, m, :], lambda a: a[:, :])
            for m in range(KC):
                wait_filled(act, ("G", m))
            for b in range(B):
                for m in range(KC):
                    hi_part(("qm", b, m), qm_hi[:, m, b * L:(b + 1) * L], lambda a: a[:, 0, :])

            def context_hi(b):
                act.wait_ge(mc_in, 16 * (b + 1))
                if b:
                    wait_filled(act, ("am", b * TB - 1))
                act.activation(mc_hi[:, :, :], mc_raw[:, :, :], ACT.Copy).then_inc(mc_hi_done, 1)

            def turned_context(b):
                for g in range(TB):
                    cols = slice((b * MT + 2 * g) * P, (b * MT + 2 * g + 2) * P)
                    hi_part(("mcT", b, g), mcT_hi[:, :, cols], lambda a: a[:, :].rearrange("p (k t) -> p k t", k=KC))

            turned_context(0)
            context_hi(0)
            for n in range(T + 2):
                if n >= 2:
                    hi_part(("amT", n - 2), amT_hi[:, :, :], lambda a: tiles(a, KC))
                if 1 <= n <= T:
                    for h in range(2):
                        hi_part(("attnT", n - 1, h), attnT_hi[:, 4 * h:4 * h + 4, :], lambda a: tiles(a, 4))
                if n < T:
                    acc = wait_filled(act, ("ms", n))
                    act.wait_ge(nmax_done, n + 1)
                    if n >= 2:
                        wait_filled(act, ("attnT", n - 2, 1))
                    act.activation(attn[:, n % 2, :], acc[:, :, :].rearrange("p a b -> p (a b)"), ACT.Exp,
                                   bias=den[:, 0, n:n + 1], scale=1.0 / np.sqrt(H), accum_out=den[:, 1, n:n + 1])\
                       .then_inc(exp_done, 1)
                if n >= 2:
                    t = n - 2
                    act.wait_ge(gate_in, t + 1)
                    act.activation(stage1[:, :], stage0[:, :], ACT.Tanh, scale=0.5).then_inc(gate_done, 1)
                    act.wait_ge(fused_done, t + 1)
                    act.wait_ge(squares_done, 3 * T + t)
                    act.activation(square_out[:, :], xs[:, t % 2, :], ACT.Square,
                                   accum_out=sum_sq[:, 3, t:t + 1]).then_inc(squares_done, 1)
                if n == TB - 2:
                    turned_context(1)
                if n == TB:
                    context_hi(1)

        @block.vector
        def _(dve):
            chain = [0]

            def link(ins):
                chain[0] += 1
                ins.then_inc(dve_chain, 1)
                dve.wait_ge(dve_chain, chain[0])

            def tiles(acc, n=KH):
                return acc[:, 0:n * P].rearrange("p (k t) -> p k t", k=n)

            def lo_part(product, dst, hi, src_of):
                dve.wait_ge(hi_done, hi_no[product])
                acc = banks[filled_as[product][0]]
                free(dve.tensor_tensor(dst, src_of(acc), hi.bitcast(F32), ALU.subtract), product)

            def staged_lo(product, src_of=lambda a: a[:, :]):
                z = stage_no[product]
                lo_part(product, stage_lo[:, z % 2, :], stage_hi[:, z % 2, :], src_of)

            def act_lo(product, t, n=KH):
                cols = slice(t * P, (t + 1) * P)
                lo_part(product, actT_lo[:, 0:n, cols], actT_hi[:, 0:n, cols], lambda a: tiles(a, n))

            def normed(stage, t):
                no = turn_no[(stage, t)]
                dve.wait_ge(rstd_done, no + 1)
                if no >= 2:
                    wait_filled(dve, ("actT", *TURNS[no - 2]))
                dve.scalar_tensor_tensor(out=xs[:, t % 2, :], in0=hs[:, t, :],
                                         scalar=rstd[:, NORMS.index(stage), t:t + 1], in1=w_row[:, :],
                                         op0=ALU.mult, op1=ALU.mult).then_inc(xs_done, 1)

            dve.wait_ge(small_in, SMALL)
            link(dve.tensor_scalar(eq_tmp[:, :], tt_next[:, :], 1.0, None, ALU.is_equal))
            link(dve.tensor_scalar(is_l[:, :], tt_now[:, :], 1.0, None, ALU.is_equal))
            link(dve.tensor_tensor(is_v[:, :], is_l[:, :], eq_tmp[:, :], ALU.mult))
            dve.tensor_scalar(is_l[:, :], is_v[:, :], -1.0, 1.0, ALU.mult, ALU.add).then_inc(masks_ready, 1)
            dve.wait_ge(masks_ready, 1)
            masks = [is_l, is_v]
            acc = wait_filled(dve, ("vision_count",))
            free(dve.tensor_scalar(eq_tmp[0:1, :], acc[0:1, 0:T], -2.0, None, ALU.mult), ("vision_count",))
            wait_emptied(dve, ("vision_count",))
            link(dve.tensor_copy(vision_count[:, 0:T], eq_tmp[0:1, :]))
            link(dve.tensor_reduce(row_max[0:1, 0, 0, 0:B], eq_tmp[0:1, :].rearrange("p (b i) -> p b i", b=B)[:, :, 0:TB - 1],
                                   AX, ALU.add))
            dve.tensor_tensor(vision_count[:, T:T + 1], row_max[0:1, 0, 0, 0:1], row_max[0:1, 0, 0, 1:2], ALU.add)\
               .then_inc(vision_counted, 1)
            dve.wait_ge(vision_counted, 1)
            dve.wait_ge(w_row_in, 16)
            for t in range(3):
                normed("in", t)
                if t >= 1:
                    act_lo(("actT", "in", t - 1), t - 1)
            act_lo(("actT", "in", 2), 2)
            vision = load_counts(dve)

            def add_expert(product, t, e):
                acc = wait_filled(dve, product)
                if e and product[0] == "dense":
                    acc = acc[:, 0, :]

                def add():
                    free(dve.scalar_tensor_tensor(out=hs[:, t, :], in0=acc[:, :], scalar=masks[e][:, t:t + 1],
                                                  in1=hs[:, t, :], op0=ALU.mult, op1=ALU.add), product)

                if e == 0:
                    add()
                else:
                    with dve.If(vision[t] > 0):
                        add()
                    with dve.Else():
                        free_skipped(dve, product)

            done_mix = 0
            for ci, c in enumerate(QKV):
                for t in range(T):
                    if c == "k" and t == 0:
                        wait_weights(dve, "k")
                    for e in range(2):
                        acc = wait_filled(dve, ("qkv", c, t, e))
                        if e:
                            acc = acc[:, 0, :]
                        if c == "v":
                            if e == 0 and t >= 2:
                                dve.wait_ge(v_out[t % 2], 16 * (t // 2))
                            if e == 0 and t < 2:
                                dve.wait_ge(consts_ready, 4)
                            dst = v_tile[:, t % 2, :, 0:HD]
                            src = acc[:, :].rearrange("p (h d) -> p h d", h=NH)
                        else:
                            dst, src = mixed[:, t % 2, :], acc[:, :]
                            if e == 0 and done_mix >= 2:
                                dve.wait_ge(by_sin_done, done_mix - 1)
                        if e == 0:
                            ins = dve.tensor_scalar(dst, src, masks[0][:, t:t + 1], None, ALU.mult)
                            free(ins, ("qkv", c, t, e))
                            wait_emptied(dve, ("qkv", c, t, e))
                        else:
                            with dve.If(vision[t] > 0):
                                ins = dve.scalar_tensor_tensor(out=dst, in0=src, scalar=masks[1][:, t:t + 1], in1=dst,
                                                               op0=ALU.mult, op1=ALU.add)
                                free(ins, ("qkv", c, t, e))
                                wait_emptied(dve, ("qkv", c, t, e))
                            with dve.Else():
                                free_skipped(dve, ("qkv", c, t, e))
                    if c == "v":
                        if t + 3 < T:
                            normed("in", t + 3)
                        if 1 <= t < T - 2:
                            act_lo(("actT", "in", t + 2), t + 2)
                        continue
                    if c == "k" and t == 0:
                        dve.wait_ge(rot_ready, 16 * TB)
                    done_mix += 1
                    if done_mix >= 3:
                        z = done_mix - 3
                        wait_filled(dve, ("rotT", "kq"[z // T], z % T))
                    heads = mixed[:, t % 2, :].rearrange("p (a d) -> p a d", d=HD // 2)
                    link(dve.tensor_tensor(by_cos[:, t % 2, :].rearrange("p (a d) -> p a d", d=HD // 2), heads,
                                           rot[:, t % TB, 0:HD // 2].unsqueeze(1).to_broadcast([P, 2 * NH, HD // 2]), ALU.mult))
                    dve.wait_ge(by_sin_done, done_mix)
                    dve.tensor_tensor(by_cos[:, t % 2, :], by_cos[:, t % 2, :], by_sin[:, t % 2, :], ALU.add).then_inc(rotated, 1)
                    if done_mix >= 3:
                        staged_lo(("rotT", *ROTATED[done_mix - 3]))
            for c, t in ROTATED[-2:]:
                staged_lo(("rotT", c, t))
            for u in range(B * MT):
                lo_part(("ctxT", u), ctxT_lo[:, :, u * P:(u + 1) * P], ctxT_hi[:, :, u * P:(u + 1) * P],
                        lambda a: tiles(a, KC))
            for n in range(B * M // L):
                for m in range(KC):
                    staged_lo(("kT", n, m))
            dve.wait_ge(consts_ready, 2)
            for u in range(B * MT):
                acc = wait_filled(dve, ("cv", u))
                if u >= 4 and u % 2 == 0:
                    dve.wait_ge(v_out[u // 2 % 2], 16 * (T // 2 + u // 4))
                free(dve.tensor_copy(cv_tile[:, u % 4, :, 0:CHD], acc[:, 0, 0:C].rearrange("p (h d) -> p h d", h=NH)),
                     ("cv", u))

            def attend(kind, steps, per_unit):
                causal = kind == "self"
                before = 0 if causal else UNITS
                for todo in steps:
                    for what, u, r in todo:
                        if what == "scores":
                            for n in (2 * r, 2 * r + 1):
                                if causal:
                                    j, i = divmod(n, TB)
                                    product = (kind, "S", u, j, i)
                                    acc = wait_filled(dve, product)
                                    if n == 0 and u + before >= 2:
                                        dve.wait_ge(parts_done, u + before - 1)
                                    free(dve.tensor_reduce(row_max[:, u % 2, i, j:j + 1], acc[:, 0:(i + 1) * P], AX, ALU.max,
                                                           negate=True), product)
                                else:
                                    j, i, h = n // (2 * TB), n // 2 % TB, n % 2
                                    product = (kind, "S", u, j, i, h)
                                    acc = wait_filled(dve, product)
                                    dst = half_max[:, u % 2, h, i, j:j + 1]
                                    free(dve.tensor_reduce(dst, acc[:, :], AX, ALU.max, negate=True), product)
                        elif what == "max_parts":
                            if causal:
                                lasts = [(kind, "S", u, 1, TB - 2), (kind, "S", u, 1, TB - 1)]
                            else:
                                lasts = [(kind, "S", u, 1, TB - 1, 0), (kind, "S", u, 1, TB - 1, 1)]
                            for p_ in lasts:
                                wait_emptied(dve, p_)
                            if not causal:
                                link(dve.tensor_tensor(row_max[:, u % 2, :, :], half_max[:, u % 2, 0, :, :],
                                                       half_max[:, u % 2, 1, :, :], ALU.min))
                            v = u + before
                            if v >= 2:
                                k2 = "self" if v - 2 < UNITS else "cross"
                                wait_filled(dve, (k2, "max_rows", (v - 2) % UNITS))
                            link(dve.tensor_copy(max_parts[:, u % 2, :, 0:2], row_max[:, u % 2, :, :]))
                            dve.tensor_tensor(max_parts[:, u % 2, :, 2:4], row_max[:, u % 2, :, :],
                                              max_parts[:, u % 2, :, 0:2].bitcast(F32), ALU.subtract).then_inc(parts_done, 1)
                        elif what == "turn_back":
                            acc = wait_filled(dve, (kind, "PVT", u))
                            pair = u % PAIRS
                            if u == PAIRS:
                                for i in range(TB):
                                    wait_filled(dve, (kind, "ctxT", 0, i))
                            if causal:
                                v4 = acc[:, :].rearrange("p (i j d) -> p i j d", i=TB, j=2)
                                link(dve.reciprocal(inv_den[:, u % 2, :, :], v4[:, :, :, HD]))
                                dst = heads_out[:, :, 2 * pair * HD:(2 * pair + 2) * HD].rearrange("p i (j d) -> p i j d", j=2)
                                ins = dve.tensor_tensor(dst, v4[:, :, :, 0:HD],
                                                        inv_den[:, u % 2, :, :].unsqueeze(3).to_broadcast([P, TB, 2, HD]), ALU.mult)
                                ins.then_inc(heads_done, 1)
                                dve.wait_ge(heads_done, u + 1)
                                dve.sem_inc(bank_freed[filled_as[(kind, "PVT", u)][0]], 1)
                            else:
                                v5 = acc[:, :].rearrange("p (i j h d) -> p i j h d", i=TB, j=2, h=2)
                                sums = odd_sum[:, u % 2, :, :, :]
                                link(dve.tensor_copy(sums, v5[:, :, :, 1, 0:CHD + 1]))
                                ins = dve.tensor_tensor(sums, v5[:, :, :, 0, 0:CHD + 1], sums, ALU.add)
                                free(ins, (kind, "PVT", u))
                                wait_emptied(dve, (kind, "PVT", u))
                                link(dve.reciprocal(inv_den[:, u % 2, :, :], sums[:, :, :, CHD]))
                                dst = cheads_out[:, :, 2 * pair * CHD:(2 * pair + 2) * CHD].rearrange("p i (j d) -> p i j d", j=2)
                                dve.tensor_tensor(dst, sums[:, :, :, 0:CHD],
                                                  inv_den[:, u % 2, :, :].unsqueeze(3).to_broadcast([P, TB, 2, CHD]), ALU.mult)\
                                   .then_inc(heads_done, 1)
                        elif what == "context":
                            for i in range(TB):
                                act_lo((kind, "ctxT", u, i), u * TB + i, KH if causal else KC)

            attend("self", self_steps, TB)
            dve.wait_ge(w_row_in, 32)
            for n in range(T + 3):
                if n < T:
                    for e in range(2):
                        add_expert(("dense", n, e), n, e)
                        wait_emptied(dve, ("dense", n, e))
                if 1 <= n <= T:
                    if n == 1:
                        wait_filled(dve, ("self", "PVT", UNITS - 1))
                    normed("cross", n - 1)
                if 2 <= n < T + 2:
                    act_lo(("actT", "cross", n - 2), n - 2)
                if n in CQ_STEPS:
                    for m in range(KC):
                        staged_lo(("cqT", CQ_STEPS.index(n), m), lambda a: a[:, 0, :])
            attend("cross", cross_steps, MT)
            dve.wait_ge(w_row_in, 48)
            for n in range(T + 3):
                if n < T:
                    acc = wait_filled(dve, ("cdense", n))
                    free(dve.tensor_tensor(hs[:, n, :], acc[:, :], hs[:, n, :], ALU.add), ("cdense", n))
                    wait_emptied(dve, ("cdense", n))
                if 1 <= n <= T:
                    if n == 1:
                        wait_filled(dve, ("cross", "PVT", UNITS - 1))
                    normed("mlp", n - 1)
                if n >= 3:
                    act_lo(("actT", "mlp", n - 3), n - 3)

            items = FF_ITEMS

            def feed_forward(group):
                for n in range(group.start, group.stop + 2):
                    if n < group.stop:
                        e, f, t = items[n]
                        fw = FS[f]
                        dve.wait_ge(silu_done, n + 1)
                        acc = banks[filled_as[("gu", e, f, t)][0]]
                        if n >= 2:
                            wait_filled(dve, ("hidT", *items[n - 2]))
                        src = acc[:, 1, 0:fw] if fw >= 256 else acc[:, 0, fw:2 * fw]

                        def gated():
                            dve.tensor_tensor(hid[:, n % 2, 0:fw], src, silu_g[:, n % 2, 0:fw], ALU.mult).then_inc(hid_done, 1)
                            dve.wait_ge(hid_done, n + 1)

                        if e == 0:
                            gated()
                        else:
                            with dve.If(vision[t] > 0):
                                gated()
                            with dve.Else():
                                dve.sem_inc(hid_done, 1)
                        dve.sem_inc(bank_freed[filled_as[("gu", e, f, t)][0]], 1)
                    if group.start < n <= group.stop:
                        e, f, t = items[n - 1]
                        product = ("hidT", e, f, t)
                        dve.wait_ge(hi_done, hi_no[product])
                        acc = banks[filled_as[product][0]]
                        full = FS[f] // P
                        s = (n - 1) % 2

                        def hid_lo():
                            ins = dve.tensor_tensor(hidT_lo[:, s, 0:full, :], tiles(acc, full),
                                                    hidT_hi[:, s, 0:full, :].bitcast(F32), ALU.subtract)
                            if FS[f] > full * P:
                                w = FS[f] - full * P
                                ins = dve.tensor_tensor(hidT_lo[0:w, s, full, :], acc[0:w, full * P:(full + 1) * P],
                                                        hidT_hi[0:w, s, full, :].bitcast(F32), ALU.subtract)
                            free(ins, product)

                        if e == 0:
                            hid_lo()
                        else:
                            with dve.If(vision[t] > 0):
                                hid_lo()
                            with dve.Else():
                                free_skipped(dve, product)
                    if n >= group.start + 2:
                        e, f, t = items[n - 2]
                        product = ("down", e, f, t)
                        add_expert(product, t, e)
                    for nxt, i in split_pieces(group, n):
                        if nxt in BY_VECTOR:
                            s = cut_at[nxt][0]
                            hi, lo, raw = weight_pieces(nxt)[i]
                            dve.wait_ge(high_copied[s], copy_before[nxt] + i + 1)
                            dve.tensor_tensor(lo, raw, hi.bitcast(F32), ALU.subtract).then_inc(weights_ready[s], 1)

            for group in FF_GROUPS:
                if len(group) == T - B:
                    before, after = ff_fills[group]
                    with dve.If(vision[T] > 0):
                        feed_forward(group)
                    with dve.Else():
                        dve.wait_ge(hid_done, group.start)
                        dve.sem_inc(hid_done, len(group))
                        for p_ in range(H0):
                            dve.wait_ge(bank_freed[p_], before[p_])
                            dve.sem_inc(bank_freed[p_], after[p_] - before[p_])
                else:
                    feed_forward(group)

            for g in range(KC + 2 * KH):
                hi, lo = (wmT_hi[:, g, :], wmT_lo[:, g, :]) if g < KC else (wgT_hi[:, g - KC, :], wgT_lo[:, g - KC, :])
                lo_part(("wT", g), lo, hi, lambda a: a[:, :])
            dve.wait_ge(wm_hi_done, 1)
            dve.tensor_tensor(wm_lo[:, :, :], wm_raw[:, :, :], wm_hi[:, :, :].bitcast(F32), ALU.subtract).then_inc(wm_ready, 1)
            for t in range(T):
                act_lo(("hsT", t), t)
            for m in range(KC):
                lo_part(("G", m), G_lo[:, m, :], G_hi[:, m, :], lambda a: a[:, :])
            for b in range(B):
                for m in range(KC):
                    cols = slice(b * L, (b + 1) * L)
                    lo_part(("qm", b, m), qm_lo[:, m, cols], qm_hi[:, m, cols], lambda a: a[:, 0, :])

            def context_lo(b):
                dve.wait_ge(mc_hi_done, b + 1)
                dve.tensor_tensor(mc_lo[:, :, :], mc_raw[:, :, :], mc_hi[:, :, :].bitcast(F32), ALU.subtract).then_inc(mc_ready, 1)

            def turned_context(b):
                for g in range(TB):
                    cols = slice((b * MT + 2 * g) * P, (b * MT + 2 * g + 2) * P)
                    lo_part(("mcT", b, g), mcT_lo[:, :, cols], mcT_hi[:, :, cols],
                            lambda a: a[:, :].rearrange("p (k t) -> p k t", k=KC))

            turned_context(0)
            context_lo(0)
            dve.wait_ge(w_row_in, 80)
            for n in range(T + 3):
                if 2 <= n < T + 2:
                    lo_part(("amT", n - 2), amT_lo[:, :, :], amT_hi[:, :, :], lambda a: tiles(a, KC))
                if n < T:
                    acc = wait_filled(dve, ("ms", n))
                    link(dve.tensor_reduce(row_max[:, n % 2, 0, 0:1], acc[:, :, :].rearrange("p a b -> p (a b)"), AX,
                                           ALU.max, negate=True))
                    dve.tensor_scalar(den[:, 0, n:n + 1], row_max[:, n % 2, 0, 0:1], float(1.0 / np.sqrt(H)), None, ALU.mult)\
                       .then_inc(nmax_done, 1)
                if 1 <= n <= T:
                    for h in range(2):
                        lo_part(("attnT", n - 1, h), attnT_lo[:, 4 * h:4 * h + 4, :], attnT_hi[:, 4 * h:4 * h + 4, :],
                                lambda a: tiles(a, 4))
                if n >= 3:
                    t = n - 3
                    dve.wait_ge(rstd_done, 3 * T + t + 1)
                    dve.scalar_tensor_tensor(out=xs[:, t % 2, :], in0=xs[:, t % 2, :], scalar=rstd[:, 3, t:t + 1],
                                             in1=w_row[:, :], op0=ALU.mult, op1=ALU.mult).then_inc(row_done, 1)
                if 2 <= n < T + 2:
                    t = n - 2
                    acc = wait_filled(dve, ("gate", t))
                    if t >= 1:
                        dve.wait_ge(fused_done, t)
                    ins = dve.tensor_tensor(stage0[:, :], acc[:, :], bias_row[:, :], ALU.add)
                    free(ins, ("gate", t))
                    wait_emptied(dve, ("gate", t))
                    dve.sem_inc(gate_in, 1)
                    acc = wait_filled(dve, ("mctx", t))
                    dve.wait_ge(gate_done, t + 1)
                    ins = dve.scalar_tensor_tensor(out=stage0[:, :], in0=stage1[:, :], scalar=1.0,
                                                   in1=acc[:, :], op0=ALU.add, op1=ALU.mult)
                    free(ins, ("mctx", t))
                    wait_emptied(dve, ("mctx", t))
                    if t >= 2:
                        dve.wait_ge(result_out[t % 2], 16 * (t // 2))
                    dve.scalar_tensor_tensor(out=xs[:, t % 2, :], in0=stage0[:, :], scalar=0.5,
                                             in1=hs[:, t, :], op0=ALU.mult, op1=ALU.add).then_inc(fused_done, 1)
                if n < T:
                    dve.wait_ge(exp_done, n + 1)
                    dve.sem_inc(bank_freed[filled_as[("ms", n)][0]], 1)
                if 1 <= n <= T:
                    t = n - 1
                    acc = wait_filled(dve, ("am", t))
                    link(dve.reciprocal(inv_den[:, t % 2, 0, 0:1], den[:, 1, t:t + 1]))
                    if t >= 1:
                        wait_filled(dve, ("amT", t - 1))
                    ins = dve.tensor_scalar(am[:, :], acc[:, 0:C], inv_den[:, t % 2, 0, 0:1], None, ALU.mult)
                    free(ins, ("am", t))
                    wait_emptied(dve, ("am", t))
                    dve.sem_inc(am_done, 1)
                if n == TB - 2:
                    turned_context(1)
                if n == TB:
                    context_lo(1)

        @block.gpsimd
        def _(pool):
            chain = [0]

            def link(ins):
                chain[0] += 1
                ins.then_inc(pool_chain, 1)
                pool.wait_ge(pool_chain, chain[0])

            pool.memset(tt_next[:, :], 0).then_inc(next_zeroed, 1)
            link(pool.memset(ident[:, :], 0.0))
            pool.affine_select(out=ident[:, :], in_=ident[:, :], compare_op=ALU.not_equal, fill=1.0, base=0,
                               pattern=[[-1, P]], channel_multiplier=1).then_inc(consts_ready, 1)
            pool.memset(cv_tile[:, :, :, CHD:2 * CHD], 1.0).then_inc(consts_ready, 1)
            pool.memset(minus_half[:, :], -0.5).then_inc(consts_ready, 1)
            pool.wait_ge(consts_ready, 3)
            def split(hi, lo, raw, ready):
                link(pool.tensor_copy(hi, raw))
                pool.tensor_tensor(lo, raw, hi.bitcast(F32), ALU.subtract).then_inc(ready, 1)

            def take_rest(cut, some=None):
                s = cut_at[cut][0]
                for i, (hi, lo, raw) in enumerate(weight_pieces(cut)):
                    if some is not None and i not in some:
                        continue
                    pool.wait_ge(high_copied[s], copy_before[cut] + i + 1)
                    pool.tensor_tensor(lo, raw, hi.bitcast(F32), ALU.subtract).then_inc(weights_ready[s], 1)

            def norm_scale(stage, t):
                i = NORMS.index(stage)
                pool.wait_ge(squares_done, i * T + t + 1)
                link(pool.tensor_scalar(sum_sq[:, i, t:t + 1], sum_sq[:, i, t:t + 1], 1.0 / H, EPS, ALU.mult, ALU.add))
                pool.tensor_tensor(rstd[:, i, t:t + 1], sum_sq[:, i, t:t + 1], minus_half[:, :], ALU.pow).then_inc(rstd_done, 1)

            link(pool.memset(ident_bf[:, :], 0.0))
            link(pool.affine_select(out=ident_bf[:, :], in_=ident_bf[:, :], compare_op=ALU.not_equal, fill=1.0, base=0,
                                    pattern=[[-1, P]], channel_multiplier=1))
            link(pool.memset(hide_s[:, :], 0.0))
            link(pool.memset(hide_t[:, :], 0.0))
            link(pool.affine_select(out=hide_s[:, :], in_=hide_s[:, :], compare_op=ALU.is_ge, fill=NEG, base=0,
                                    pattern=[[-1, P]], channel_multiplier=1))
            link(pool.affine_select(out=hide_t[:, :], in_=hide_t[:, :], compare_op=ALU.is_ge, fill=NEG, base=0,
                                    pattern=[[1, P]], channel_multiplier=-1))
            pool.memset(v_tile[:, :, :, HD:64], 1.0).then_inc(consts_ready, 1)
            for t in range(T):
                norm_scale("in", t)
                if t in (1, 3):
                    take_rest("v", range(0, KH) if t == 1 else range(KH, 2 * KH))
                if t == 3:
                    pool.wait_ge(small_in, SMALL)
                    for i in range(TB):
                        pool.indirect_dma_start(rot[:, i, :], None, table_d[:, :],
                                                bass.IndirectOffsetOnAxis(ap=pos_i[:, i:i + 1].bitcast(U32), axis=0))\
                            .then_inc(rot_ready, 16)
            take_rest("k")
            done = 0
            for c in ("k", "q"):
                for t in range(T):
                    wait_emptied(pool, ("qkv", c, t, 1))
                    if t == 0 and c == "k":
                        pool.wait_ge(rot_ready, 16 * TB)
                        wait_weights(pool, "k")
                    if done >= 2:
                        pool.wait_ge(rotated, done - 1)
                    m4 = mixed[:, t % 2, :].rearrange("p (h a d) -> p h a d", h=NH, a=2)
                    b4 = by_sin[:, t % 2, :].rearrange("p (h a d) -> p h a d", h=NH, a=2)
                    hd = HD // 2
                    sin = rot[:, t % TB, hd:2 * hd].unsqueeze(1).to_broadcast([P, NH, hd])
                    nsin = rot[:, t % TB, 2 * hd:3 * hd].unsqueeze(1).to_broadcast([P, NH, hd])
                    pool.tensor_tensor(b4[:, :, 0, :], m4[:, :, 1, :], nsin, ALU.mult)
                    pool.tensor_tensor(b4[:, :, 1, :], m4[:, :, 0, :], sin, ALU.mult).then_inc(by_sin_done, 1)
                    done += 1
                    if c == "k" and t < 4:
                        take_rest("q", (2 * t, 2 * t + 1))
                    if c == "k" and t == 4:
                        pool.wait_ge(ckv_in, 16)
                        split(ckv_hi[:, :, :], ckv_lo[:, :, :], ckv_raw[:, :, :], ckv_ready)
            for v in range(2):
                pool.wait_ge(v_out[v], 16 * (T // 2))
            pool.wait_ge(by_sin_done, 2 * T)
            for s in range(SLOTS["self"]):
                pool.memset(raw32(k_stacks["self"][s][ONES:ONES + 2, :, :]), 1.0).then_inc(stack_set, 1)
                pool.wait_ge(stack_set, s + 1)
            wait_used(pool, ("qkv", "q", T - 1, 0), ("qkv", "q", T - 1, 1))
            pool.wait_ge(raw_in[0], 16 * (2 + 2 * KH))
            for hi, lo, raw in weight_pieces("dense"):
                split(hi, lo, raw, weights_ready[0])
            pool.wait_ge(small_w_in, 16)
            split(cq_hi[:, :, :], cq_lo[:, :, :], cq_raw[:, :, :], small_w_ready)
            pool.wait_ge(small_w_ready, 1)
            for s, after in ZERO_ORDER:
                wait_filled(pool, ("self", "PV", after))
                for r0 in (32, 64):
                    link(pool.memset(raw32(q_stacks["cross"][s][r0:r0 + 32, :, :]), 0.0))
                    link(pool.memset(raw32(k_stacks["cross"][s][r0:r0 + 32, :, :]), 0.0))
                pool.memset(raw32(k_stacks["cross"][s][ONES:ONES + 2, :, :]), 1.0).then_inc(stack_set, 1)
                pool.wait_ge(stack_set, zeroed_at[s])
            for t in range(T):
                norm_scale("cross", t)
            pool.wait_ge(small_w_in, 32)
            split(cd_hi[:, :, :], cd_lo[:, :, :], cd_raw[:, :, :], small_w_ready)

            pool.wait_ge(raw_in[0], raw_count[ff_cuts[0]])
            wait_used(pool, ("dense", T - 1, 0), ("dense", T - 1, 1))
            for hi, lo, raw in weight_pieces(ff_cuts[0]):
                split(hi, lo, raw, weights_ready[0])
            for t in range(T):
                norm_scale("mlp", t)
            for n in range(1, len(ff_cuts)):
                if ff_cuts[n] not in BY_VECTOR:
                    take_rest(ff_cuts[n])
            for t in range(T):
                pool.wait_ge(squares_done, 3 * T + t + 1)
                link(pool.tensor_scalar(sum_sq[:, 3, t:t + 1], sum_sq[:, 3, t:t + 1], 1.0 / H, EPS, ALU.mult, ALU.add))
                pool.tensor_tensor(rstd[:, 3, t:t + 1], sum_sq[:, 3, t:t + 1], minus_half[:, :], ALU.pow).then_inc(rstd_done, 1)

        @block.sync
        def _(sp):
            def rows(w):
                return w.rearrange("(k p) n -> p k n", p=P)

            def row_on_all(v):
                return v.rearrange("(a n) -> a n", a=1).to_broadcast([P, H])

            def load_cut(c):
                s = cut_at[c][0]
                for e in range(2):
                    if c == "dense":
                        src = rows(dense_w[e])
                    else:
                        j = ("q", "k", "v").index(c)
                        src = rows(qkv_w[e])[:, :, j * H:(j + 1) * H]
                    sp.dma_start(qkv_raw[s][:, e, :, :], src).then_inc(raw_in[s], 16)

            def load_x(t):
                sp.dma_start(hs[:, t, :], x_d[t * P:(t + 1) * P, :]).then_inc(x_in[t], 16)

            def load_v(e):
                for k in range(KH):
                    sp.dma_start(qkv_raw[0][:, e, k, :], qkv_w[e][k * P:(k + 1) * P, 2 * H:3 * H]).then_inc(v_raw_in[e * KH + k], 16)

            load_x(0)
            load_x(1)
            sp.dma_start(w_row[:, :], row_on_all(ln_in_w)).then_inc(w_row_in, 16)
            load_v(0)
            for t in range(2, TB):
                load_x(t)
            load_v(1)
            for t in range(TB, T):
                load_x(t)
            load_cut("k")
            sp.dma_start(ckv_raw[:, :, :], rows(ckv_w)).then_inc(ckv_in, 16)

            def store_staged(product, dst, view):
                z = stage_no[product]
                wait_emptied(sp, product)
                sp.dma_start(dst[0], view(raw32(stage_hi[:, z % 2, :]))).then_inc(stage_out[z % 2], 16)
                sp.dma_start(dst[1], view(raw32(stage_lo[:, z % 2, :]))).then_inc(stage_out[z % 2], 16)

            def stored(product):
                n = stage_no[product] + 1
                sp.wait_ge(stage_out[0], 32 * ((n + 1) // 2))
                sp.wait_ge(stage_out[1], 32 * (n // 2))

            def load_stack(kind, u):
                b, pair, slot = u // PAIRS, u % PAIRS, slot_of[(kind, u)][0]
                qs, ks, vs = q_stacks[kind][slot], k_stacks[kind][slot], v_stacks[kind][slot]
                w, scr_q, scr_k = (HD, q_scr, k_scr) if kind == "self" else (CHD, cq_scr, ck_scr)
                n_k = L if kind == "self" else M
                if u >= SLOTS[kind]:
                    wait_filled(sp, (kind, "PV", u - SLOTS[kind]))
                for row, part_q, part_k in ((0, 0, 0), (1, 0, 1), (2, 1, 0)):
                    feats = slice(2 * pair * w, (2 * pair + 2) * w)
                    sp.dma_start(raw32(qs[row * w:(row + 1) * w, :, :]),
                                 scr_q[part_q, feats, b * L:(b + 1) * L].rearrange("(j p) n -> p j n", j=2)).then_inc(stack_in[slot], 16)
                    sp.dma_start(raw32(ks[row * w:(row + 1) * w, :, 0:n_k]),
                                 scr_k[part_k, feats, b * n_k:(b + 1) * n_k].rearrange("(j p) n -> p j n", j=2)).then_inc(stack_in[slot], 16)
                if kind == "self":
                    src = v_scr[b * L:(b + 1) * L, pair * 128:(pair + 1) * 128].rearrange("(k p) c -> p k c", p=P)
                    dst = vs[:, :].rearrange("p (k c) -> p k c", k=TB)
                else:
                    src = cv_scr[b * M:(b + 1) * M, pair * 64:(pair + 1) * 64].rearrange("(k p) c -> p k c", p=P)
                    dst = vs[:, :].rearrange("p (k c) -> p k c", k=MT)
                sp.dma_start(dst, src).then_inc(stack_in[slot], 16)

            wait_weights(sp, "v")
            load_cut("q")
            for t in range(T):
                wait_emptied(sp, ("qkv", "v", t, 1))
                sp.dma_start(v_scr[t * P:(t + 1) * P, :], v_tile[:, t % 2, :, :].rearrange("p h d -> p (h d)"))\
                    .then_inc(v_out[t % 2], 16)
            for c, scr in (("k", k_scr), ("q", q_scr)):
                for t in range(T):
                    if c == "q" and t == 0:
                        wait_weights(sp, "q")
                        for d in range(4):
                            sp.dma_start(ctx_tile[:, 4 * d:4 * d + 4, :],
                                         ctx_d[4 * d * P:4 * (d + 1) * P, :].rearrange("(u p) c -> p u c", p=P)).then_inc(ctx_in_s[d], 16)
                    d = scr[:, :, t * P:(t + 1) * P].rearrange("a (k p) n -> a p k n", p=P)
                    store_staged(("rotT", c, t), (d[0], d[1]), lambda a: a.rearrange("p (k n) -> p k n", k=KH))
            stored(("rotT", "q", T - 1))
            for i in range(2):
                sp.wait_ge(v_out[i], 16 * (T // 2))
            load_stack("self", 0)

            for n in range(B * M // L):
                for m in range(KC):
                    d = ck_scr[:, m * P:(m + 1) * P, n * L:(n + 1) * L]
                    store_staged(("kT", n, m), (d[0], d[1]), lambda a: a)
                if n < 3:
                    load_stack("self", 1 + n)
            for u in range(0, B * MT, 2):
                wait_emptied(sp, ("cv", u))
                wait_emptied(sp, ("cv", u + 1))
                sp.dma_start(cv_scr[u * P:(u + 2) * P, :].rearrange("(u p) c -> p u c", p=P),
                             cv_tile[:, u % 4:u % 4 + 2, :, :].rearrange("p u h d -> p u (h d)")).then_inc(v_out[u // 2 % 2], 16)
            def store_rows(kind, u):
                wait_emptied(sp, (kind, "max_rows", u))
                v = u + (0 if kind == "self" else UNITS)
                for part in range(2):
                    slot = slot_of[(kind, u)][0]
                    sp.dma_start(raw32(q_stacks[kind][slot][ONES + part:ONES + part + 1, :, :]),
                                 raw32(stage_hi[2 * part:2 * part + 2, v % 2, :])).then_inc(rows_in[slot], 16)

            stored(("kT", B * M // L - 1, KC - 1))
            for i in range(2):
                sp.wait_ge(v_out[i], 16 * (T // 2 + MT // 2))
            load_stack("self", 4)
            for u in range(UNITS):
                if u < 2 * KH:
                    e, k = divmod(u, KH)
                    sp.dma_start(qkv_raw[0][:, e, k, :], dense_w[e][k * P:(k + 1) * P, :]).then_inc(raw_in[0], 16)
                store_rows("self", u)
                if u == 0:
                    load_stack("self", 5)
                if 1 <= u < UNITS - SLOTS["self"] + 1:
                    load_stack("self", u + SLOTS["self"] - 1)
                if u == 10:
                    wait_weights(sp, "dense")
                    sp.dma_start(cq_raw[:, :, :], rows(cq_w)).then_inc(small_w_in, 16)
                    wait_filled(sp, ("actT", "in", T - 1))
                    sp.dma_start(w_row[:, :], row_on_all(ln_cross_w)).then_inc(w_row_in, 16)
            sp.wait_ge(small_w_ready, 1)
            sp.dma_start(cd_raw[:, :, :], rows(cdense_w)).then_inc(small_w_in, 16)
            for b in range(B):
                for m in range(KC):
                    d = cq_scr[:, m * P:(m + 1) * P, b * L:(b + 1) * L]
                    store_staged(("cqT", b, m), (d[0], d[1]), lambda a: a)
                stored(("cqT", b, KC - 1))
                if b == 0:
                    for u in range(SLOTS["cross"]):
                        sp.wait_ge(stack_set, zeroed_at[u])
                        load_stack("cross", u)

            def load_ff(n):
                e, f = ff_cuts[n]
                s = cut_at[(e, f)][0]
                f0, fw = sum(FS[:f]), FS[f]
                a = KH * 2 * fw
                if n >= 2:
                    wait_weights(sp, ff_cuts[n - 2])
                gu = ff_raw[s][:, 0:a].rearrange("p (k g n) -> p k g n", k=KH, g=2)
                sp.dma_start(gu[:, :, 0, :], rows(gate_w[e])[:, :, f0:f0 + fw]).then_inc(raw_in[s], 16)
                sp.dma_start(gu[:, :, 1, :], rows(up_w[e])[:, :, f0:f0 + fw]).then_inc(raw_in[s], 16)
                full = fw // P
                dn = ff_raw[s][:, a:a + full * H].rearrange("p (k n) -> p k n", k=full)
                sp.dma_start(dn, rows(down_w[e][f0:f0 + full * P, :])).then_inc(raw_in[s], 16)
                if fw % P:
                    w = fw % P
                    sp.dma_start(ff_raw[s][0:w, a + full * H:a + (full + 1) * H],
                                 down_w[e][f0 + full * P:f0 + fw, :]).then_inc(raw_in[s], 16)

            for u in range(UNITS):
                store_rows("cross", u)
                if 1 <= u < UNITS - SLOTS["cross"] + 1:
                    load_stack("cross", u + SLOTS["cross"] - 1)
                if u == 2:
                    sp.wait_ge(small_w_ready, 2)
                    wait_filled(sp, ("cqT", B - 1, KC - 1))
                    load_ff(0)
                    wait_filled(sp, ("actT", "cross", T - 1))
                    sp.dma_start(w_row[:, :], row_on_all(ln_attn_w)).then_inc(w_row_in, 16)
            wait_filled(sp, ("cross", "PV", UNITS - 1))
            for n in range(1, len(ff_cuts)):
                load_ff(n)
            wait_weights(sp, ff_cuts[-2])
            sp.dma_start(wg_raw[:, :, :], rows(W_gate)).then_inc(lmem_in, 16)
            sp.dma_start(wm_raw[:, :, :], rows(W_mem)).then_inc(lmem_in, 16)
            wait_filled(sp, ("actT", "mlp", T - 1))
            sp.dma_start(w_row[:, :], row_on_all(norm_w)).then_inc(w_row_in, 16)
            sp.dma_start(bias_row[:, :], row_on_all(b_gate)).then_inc(w_row_in, 16)
            wait_used(sp, *[("down", *item) for item in FF_ITEMS[-2:]])
            for b in range(B):
                if b:
                    sp.wait_ge(mc_ready, b)
                    wait_filled(sp, ("mcT", b - 1, TB - 1))
                sp.dma_start(mc_raw[:, :, :], ctx_d[b * M:(b + 1) * M, :].rearrange("(m p) c -> p m c", p=P)).then_inc(mc_in, 16)
            for t in range(T):
                sp.wait_ge(row_done, t + 1)
                sp.dma_start(out_d[t * P:(t + 1) * P, :], xs[:, t % 2, :]).then_inc(result_out[t % 2], 16)
            for i in range(2):
                sp.wait_ge(result_out[i], 16 * T // 2)


_INS = ["x", "ctx_1024", "pos_1xS", "mask_BxS_ik0", "L0_xattn_ln_in_w", "L0_xattn_ln_post_attn_w",
        "L0_xattn_ln_post_cross_w", "L0_xattn_v_qkv", "L0_xattn_l_qkv", "L0_xattn_v_dense", "L0_xattn_l_dense",
        "L0_xattn_cq_w", "L0_xattn_ckv_w", "L0_xattn_cdense_w", "L0_xattn_v_gate", "L0_xattn_v_up",
        "L0_xattn_v_down", "L0_xattn_l_gate", "L0_xattn_l_up", "L0_xattn_l_down", "L1_xattn_W_mem",
        "L1_xattn_W_gate", "L1_xattn_b_gate", "L1_xattn_norm_w"]
_OUTS = [((B, L, H), "float32")]


def kernel(**inputs):
    import numpy as _np
    import concourse.bacc as _bacc
    from concourse import mybir as _mybir
    from concourse.bass_utils import run_bass_kernel_spmd as _run

    nc = _bacc.Bacc("TRN2", target_bir_lowering=False, num_devices=1)
    arrays, args = {}, []
    for name in _INS:
        a = _np.ascontiguousarray(inputs[name])
        arrays[f"in_{name}_dram"] = a
        args.append(nc.dram_tensor(f"in_{name}_dram", a.shape, _mybir.dt.from_np(a.dtype), kind="ExternalInput").ap())
    for i, (shape, dtype) in enumerate(_OUTS):
        dt = _mybir.dt.from_np(_np.dtype(dtype))
        args.append(nc.dram_tensor(f"out_{i}_dram", shape, dt, kind="ExternalOutput").ap())
    xattn_kernel(nc, *args)
    r = _run(nc, [arrays], core_ids=[0])
    got = tuple(r.results[0][f"out_{i}_dram"] for i in range(len(_OUTS)))
    return got[0]
```
